# Optimizing a Trainium2 kernel written in Bass

```python
import numpy as np
import jax
import jax.numpy as jnp

def _softmax(x, axis=-1):
    return jax.nn.softmax(x, axis=axis)

def _gelu(x):
    return jax.nn.gelu(x, approximate=True)

def _silu(x):
    return jax.nn.silu(x)

def _sigmoid(x):
    return jax.nn.sigmoid(x)

def _layernorm(x, axis=-1, eps=1e-05):
    m = jnp.mean(x, axis=axis, keepdims=True)
    v = jnp.var(x, axis=axis, keepdims=True)
    return (x - m) / jnp.sqrt(v + eps)

def _scatter_add(tgt, idx, src, axis=0):
    return tgt.at[idx].add(src)

def _segment_sum(src, seg, n):
    return jax.ops.segment_sum(src, seg, n)
kernel_name = 'mk_decoder_preln_d2_seqx_r8_e84331'

def setup_inputs(seed: int=0):
    np.random.seed(seed)
    _w = jnp.asarray

    def _rec_inputs():
        import jax
        import jax.numpy as jnp
        _rk = jax.random.key(seed)
        x = -0.0003929 + 0.9999 * jax.random.normal(jax.random.fold_in(_rk, 1), (4, 512, 128), jnp.float32)
        _lenS = 512 - jax.random.randint(jax.random.fold_in(_rk, 7), (4,), 0, max(1, 512 // 4) + 1, jnp.int32)
        _lenS2 = 77 - jax.random.randint(jax.random.fold_in(_rk, 8), (4,), 0, max(1, 77 // 4) + 1, jnp.int32)
        _ctx_1024P = jax.random.normal(jax.random.fold_in(_rk, 11), (4, 16, 128), jnp.float32)
        _ctx_1024c = jax.random.dirichlet(jax.random.fold_in(_rk, 511), 0.3 * jnp.ones((16,), jnp.float32), (4, 77))
        _ctx_1024t = jnp.einsum('bsk,bkd->bsd', _ctx_1024c, _ctx_1024P)
        _ctx_1024t = _ctx_1024t * jax.lax.rsqrt(jnp.mean(jnp.square(_ctx_1024t)) + 1e-12) * 0.953939
        ctx_1024 = -1.39393e-06 + 0.999914 * (_ctx_1024t + 0.3 * jax.random.normal(jax.random.fold_in(_rk, 611), (4, 77, 128), jnp.float32))
        _validS = jnp.arange(512)[None, :] < _lenS[:, None]
        _validS2 = jnp.arange(77)[None, :] < _lenS2[:, None]
        _causal = jnp.tril(jnp.ones((512, 512), dtype=bool))
        mask_BxS2_bf1 = jnp.ones((4, 77), dtype=bool)
        return (x, ctx_1024, mask_BxS2_bf1)
    x, ctx_1024, mask_BxS2_bf1 = _rec_inputs()

    def _L0_attn_setup():
        import jax, jax.numpy as jnp
        import numpy as np
        B, S, F = (2, 256, 128)
        H, DK = (16, 64)
        D_MODEL = 128
        key = jax.random.key(seed)
        kx, kq, kk, kv, ko = jax.random.split(key, 5)
        x = jax.random.normal(kx, (B, S, F), dtype=jnp.float32)
        wq = jax.random.normal(kq, (H, F, DK), dtype=jnp.float32) * 0.02
        wk = jax.random.normal(kk, (H, F, DK), dtype=jnp.float32) * 0.02
        wv = jax.random.normal(kv, (H, F, DK), dtype=jnp.float32) * 0.02
        wo = jax.random.normal(ko, (H * DK, D_MODEL), dtype=jnp.float32) * 0.02
        return {'x': x, 'wq': wq, 'wk': wk, 'wv': wv, 'wo': wo}
    _L0_attn_all = _L0_attn_setup()
    _L0_attn_in = {k: v for k, v in _L0_attn_all.items() if k in ('wq', 'wk', 'wv', 'wo')}
    del _L0_attn_all

    def _L0_xattn_setup():
        import jax, jax.numpy as jnp
        import numpy as np
        GAMMA = 10.0
        BASE = 10000.0
        SCALE = 64 ** (-0.5)
        NUM_HEADS = 16

        def _larope(t, seq_len):
            B, H, L, D = t.shape
            inv_freq = 1.0 / BASE ** (jnp.arange(0, D, 2, dtype=jnp.float32) / D)
            pos = GAMMA * (jnp.arange(L, dtype=jnp.float32) / float(seq_len))
            ang = pos[:, None] * inv_freq
            cos = jnp.cos(ang)
            sin = jnp.sin(ang)
            te, to = (t[..., 0::2], t[..., 1::2])
            re = te * cos - to * sin
            ro = te * sin + to * cos
            return jnp.stack([re, ro], axis=-1).reshape(t.shape)
        key = jax.random.key(seed)
        ks = jax.random.split(key, 8)
        B, Lq, Lk, D = (8, 256, 64, 128)
        s = D ** (-0.5)
        return {'x': jax.random.normal(ks[0], (B, Lq, D), jnp.float32), 'context': jax.random.normal(ks[1], (B, Lk, D), jnp.float32), 'context_mask': jnp.ones((B, Lk), dtype=bool), 'Wq': jax.random.normal(ks[2], (D, D), jnp.float32) * s, 'bq': jnp.zeros((D,), jnp.float32), 'Wkv': jax.random.normal(ks[3], (D, 2 * D), jnp.float32) * s, 'bkv': jnp.zeros((2 * D,), jnp.float32), 'Wo': jax.random.normal(ks[4], (D, D), jnp.float32) * s, 'bo': jnp.zeros((D,), jnp.float32)}
    _L0_xattn_all = _L0_xattn_setup()
    _L0_xattn_in = {k: v for k, v in _L0_xattn_all.items() if k in ('Wq', 'bq', 'Wkv', 'bkv', 'Wo', 'bo')}
    del _L0_xattn_all

    def _L0_ffn_setup():
        import math
        import jax, jax.numpy as jnp
        import numpy as np
        B, T, D, H, E, K, S = (4, 512, 128, 256, 16, 2, 2)
        ROUTE_SCALE = 1.0

        def _swiglu(x, w1, w3, w2):
            return jax.nn.silu(x @ w1) * (x @ w3) @ w2
        key = jax.random.key(seed)
        ks = jax.random.split(key, 9)
        s = 0.02
        return {'x': jax.random.normal(ks[0], (B, T, D), jnp.float32), 'gate_w': jax.random.normal(ks[1], (D, E), jnp.float32) * s, 'gate_b': jnp.zeros((E,), jnp.float32), 'ew1': jax.random.normal(ks[2], (E, D, H), jnp.float32) * s, 'ew3': jax.random.normal(ks[3], (E, D, H), jnp.float32) * s, 'ew2': jax.random.normal(ks[4], (E, H, D), jnp.float32) * s, 'sw1': jax.random.normal(ks[5], (S, D, H), jnp.float32) * s, 'sw3': jax.random.normal(ks[6], (S, D, H), jnp.float32) * s, 'sw2': jax.random.normal(ks[7], (S, H, D), jnp.float32) * s}
    _L0_ffn_all = _L0_ffn_setup()
    _L0_ffn_in = {k: v for k, v in _L0_ffn_all.items() if k in ('gate_w', 'gate_b', 'ew1', 'ew3', 'ew2', 'sw1', 'sw3', 'sw2')}
    del _L0_ffn_all

    def _L1_attn_setup():
        import jax, jax.numpy as jnp
        import numpy as np
        HIDDEN = 128
        NUM_HEADS = 16
        HEAD = HIDDEN // NUM_HEADS
        LEFT = 64
        RIGHT = 8
        NUM_POS = LEFT + RIGHT + 1
        key = jax.random.key(seed)
        ks = jax.random.split(key, 10)
        s = 1.0 / np.sqrt(HIDDEN)
        return {'hidden_states': jax.random.normal(ks[0], (4, 256, HIDDEN), jnp.float32), 'Wq': jax.random.normal(ks[1], (HIDDEN, HIDDEN), jnp.float32) * s, 'bq': jax.random.normal(ks[2], (HIDDEN,), jnp.float32) * 0.01, 'Wk': jax.random.normal(ks[3], (HIDDEN, HIDDEN), jnp.float32) * s, 'bk': jax.random.normal(ks[4], (HIDDEN,), jnp.float32) * 0.01, 'Wv': jax.random.normal(ks[5], (HIDDEN, HIDDEN), jnp.float32) * s, 'bv': jax.random.normal(ks[6], (HIDDEN,), jnp.float32) * 0.01, 'Wo': jax.random.normal(ks[7], (HIDDEN, HIDDEN), jnp.float32) * s, 'bo': jax.random.normal(ks[8], (HIDDEN,), jnp.float32) * 0.01, 'dist_emb': jax.random.normal(ks[9], (NUM_POS, HEAD), jnp.float32)}
    _L1_attn_all = _L1_attn_setup()
    _L1_attn_in = {k: v for k, v in _L1_attn_all.items() if k in ('Wq', 'bq', 'Wk', 'bk', 'Wv', 'bv', 'Wo', 'bo', 'dist_emb')}
    del _L1_attn_all

    def _L1_xattn_setup():
        import jax, jax.numpy as jnp
        import numpy as np
        EMBED = 128
        B, I, J = (8, 256, 256)
        SCALE = EMBED ** (-0.5)
        key = jax.random.key(seed)
        ks = jax.random.split(key, 5)
        s = EMBED ** (-0.5)
        return {'q_in': jax.random.normal(ks[0], (B, I, EMBED), dtype=jnp.float32), 'k_v': jax.random.normal(ks[1], (B, J, EMBED), dtype=jnp.float32), 'Wq': jax.random.normal(ks[2], (EMBED, EMBED), dtype=jnp.float32) * s, 'bq': jnp.zeros((EMBED,), dtype=jnp.float32), 'Wk': jax.random.normal(ks[3], (EMBED, EMBED), dtype=jnp.float32) * s, 'bk': jnp.zeros((EMBED,), dtype=jnp.float32), 'Wv': jax.random.normal(ks[4], (EMBED, EMBED), dtype=jnp.float32) * s, 'bv': jnp.zeros((EMBED,), dtype=jnp.float32)}
    _L1_xattn_all = _L1_xattn_setup()
    _L1_xattn_in = {k: v for k, v in _L1_xattn_all.items() if k in ('Wq', 'bq', 'Wk', 'bk', 'Wv', 'bv')}
    del _L1_xattn_all

    def _L1_ffn_setup():
        import jax, jax.numpy as jnp
        import numpy as np
        TOP_K = 2
        key = jax.random.key(seed)
        ks = jax.random.split(key, 5)
        B, T, D, E, F = (2, 256, 128, 8, 256)
        scale_d = 1.0 / np.sqrt(D)
        scale_f = 1.0 / np.sqrt(F)
        return {'x': jax.random.normal(ks[0], (B, T, D), jnp.float32), 'kernel_router_DE': jax.random.normal(ks[1], (D, E), jnp.float32) * scale_d, 'kernel_gating_EDF': jax.random.normal(ks[2], (E, D, F), jnp.float32) * scale_d, 'kernel_up_EDF': jax.random.normal(ks[3], (E, D, F), jnp.float32) * scale_d, 'kernel_down_EFD': jax.random.normal(ks[4], (E, F, D), jnp.float32) * scale_f}
    _L1_ffn_all = _L1_ffn_setup()
    _L1_ffn_in = {k: v for k, v in _L1_ffn_all.items() if k in ('kernel_router_DE', 'kernel_gating_EDF', 'kernel_up_EDF', 'kernel_down_EFD')}
    del _L1_ffn_all
    return {'x': x, 'ctx_1024': ctx_1024, 'mask_BxS2_bf1': mask_BxS2_bf1, 'L0_attn_wq': _L0_attn_in['wq'], 'L0_attn_wk': _L0_attn_in['wk'], 'L0_attn_wv': _L0_attn_in['wv'], 'L0_attn_wo': _L0_attn_in['wo'], 'L0_xattn_Wq': _L0_xattn_in['Wq'], 'L0_xattn_bq': _L0_xattn_in['bq'], 'L0_xattn_Wkv': _L0_xattn_in['Wkv'], 'L0_xattn_bkv': _L0_xattn_in['bkv'], 'L0_xattn_Wo': _L0_xattn_in['Wo'], 'L0_xattn_bo': _L0_xattn_in['bo'], 'L0_ffn_gate_w': _L0_ffn_in['gate_w'], 'L0_ffn_gate_b': _L0_ffn_in['gate_b'], 'L0_ffn_ew1': _L0_ffn_in['ew1'], 'L0_ffn_ew3': _L0_ffn_in['ew3'], 'L0_ffn_ew2': _L0_ffn_in['ew2'], 'L0_ffn_sw1': _L0_ffn_in['sw1'], 'L0_ffn_sw3': _L0_ffn_in['sw3'], 'L0_ffn_sw2': _L0_ffn_in['sw2'], 'L1_attn_Wq': _L1_attn_in['Wq'], 'L1_attn_bq': _L1_attn_in['bq'], 'L1_attn_Wk': _L1_attn_in['Wk'], 'L1_attn_bk': _L1_attn_in['bk'], 'L1_attn_Wv': _L1_attn_in['Wv'], 'L1_attn_bv': _L1_attn_in['bv'], 'L1_attn_Wo': _L1_attn_in['Wo'], 'L1_attn_bo': _L1_attn_in['bo'], 'L1_attn_dist_emb': _L1_attn_in['dist_emb'], 'L1_xattn_Wq': _L1_xattn_in['Wq'], 'L1_xattn_bq': _L1_xattn_in['bq'], 'L1_xattn_Wk': _L1_xattn_in['Wk'], 'L1_xattn_bk': _L1_xattn_in['bk'], 'L1_xattn_Wv': _L1_xattn_in['Wv'], 'L1_xattn_bv': _L1_xattn_in['bv'], 'L1_ffn_kernel_router_DE': _L1_ffn_in['kernel_router_DE'], 'L1_ffn_kernel_gating_EDF': _L1_ffn_in['kernel_gating_EDF'], 'L1_ffn_kernel_up_EDF': _L1_ffn_in['kernel_up_EDF'], 'L1_ffn_kernel_down_EFD': _L1_ffn_in['kernel_down_EFD']}

def reference(x, ctx_1024, mask_BxS2_bf1, L0_attn_wq, L0_attn_wk, L0_attn_wv, L0_attn_wo, L0_xattn_Wq, L0_xattn_bq, L0_xattn_Wkv, L0_xattn_bkv, L0_xattn_Wo, L0_xattn_bo, L0_ffn_gate_w, L0_ffn_gate_b, L0_ffn_ew1, L0_ffn_ew3, L0_ffn_ew2, L0_ffn_sw1, L0_ffn_sw3, L0_ffn_sw2, L1_attn_Wq, L1_attn_bq, L1_attn_Wk, L1_attn_bk, L1_attn_Wv, L1_attn_bv, L1_attn_Wo, L1_attn_bo, L1_attn_dist_emb, L1_xattn_Wq, L1_xattn_bq, L1_xattn_Wk, L1_xattn_bk, L1_xattn_Wv, L1_xattn_bv, L1_ffn_kernel_router_DE, L1_ffn_kernel_gating_EDF, L1_ffn_kernel_up_EDF, L1_ffn_kernel_down_EFD):
    import jax
    import jax.numpy as jnp

    def _L0_attn_ref(x, wq, wk, wv, wo):
        import jax, jax.numpy as jnp
        import numpy as np
        B, S, F = (2, 256, 128)
        H, DK = (16, 64)
        D_MODEL = 128
        q = jnp.einsum('bsf,hfd->bhsd', x, wq)
        k = jnp.einsum('bsf,hfd->bhsd', x, wk)
        v = jnp.einsum('bsf,hfd->bhsd', x, wv)
        scale = 1.0 / jnp.sqrt(jnp.asarray(DK, dtype=x.dtype))
        scores = jnp.einsum('bhsd,bhtd->bhst', q, k) * scale
        attn = jax.nn.softmax(scores, axis=-1)
        out = jnp.einsum('bhst,bhtd->bhsd', attn, v)
        feats = out.transpose(0, 2, 1, 3).reshape(x.shape[0], x.shape[1], H * DK)
        return feats @ wo

    def _L0_xattn_ref(x, context, context_mask, Wq, bq, Wkv, bkv, Wo, bo):
        import jax, jax.numpy as jnp
        import numpy as np
        GAMMA = 10.0
        BASE = 10000.0
        SCALE = 64 ** (-0.5)
        NUM_HEADS = 16

        def _larope(t, seq_len):
            B, H, L, D = t.shape
            inv_freq = 1.0 / BASE ** (jnp.arange(0, D, 2, dtype=jnp.float32) / D)
            pos = GAMMA * (jnp.arange(L, dtype=jnp.float32) / float(seq_len))
            ang = pos[:, None] * inv_freq
            cos = jnp.cos(ang)
            sin = jnp.sin(ang)
            te, to = (t[..., 0::2], t[..., 1::2])
            re = te * cos - to * sin
            ro = te * sin + to * cos
            return jnp.stack([re, ro], axis=-1).reshape(t.shape)
        B, Lq, D = x.shape
        Lk = context.shape[1]
        H = NUM_HEADS
        hd = D // H
        q = x @ Wq + bq
        kv = context @ Wkv + bkv
        k, v = jnp.split(kv, 2, axis=-1)
        q = q.reshape(B, Lq, H, hd).transpose(0, 2, 1, 3)
        k = k.reshape(B, Lk, H, hd).transpose(0, 2, 1, 3)
        v = v.reshape(B, Lk, H, hd).transpose(0, 2, 1, 3)
        q = _larope(q, Lq)
        k = _larope(k, Lk)
        scores = jnp.einsum('bhqd,bhkd->bhqk', q, k) * SCALE
        scores = jnp.where(context_mask[:, None, None, :], scores, -jnp.inf)
        attn = jax.nn.softmax(scores, axis=-1)
        out = jnp.einsum('bhqk,bhkd->bhqd', attn, v)
        out = out.transpose(0, 2, 1, 3).reshape(B, Lq, H * hd)
        return out @ Wo + bo

    def _L0_ffn_ref(x, gate_w, gate_b, ew1, ew3, ew2, sw1, sw3, sw2):
        import math
        import jax, jax.numpy as jnp
        import numpy as np
        B, T, D, H, E, K, S = (4, 512, 128, 256, 16, 2, 2)
        ROUTE_SCALE = 1.0

        def _swiglu(x, w1, w3, w2):
            return jax.nn.silu(x @ w1) * (x @ w3) @ w2
        Bx, Tx, Dx = x.shape
        flat = x.reshape(-1, Dx)
        N = flat.shape[0]
        n_experts = gate_w.shape[1]
        logits = flat @ gate_w
        scores = jax.nn.softmax(logits.astype(jnp.float32), -1) + gate_b
        _, topi = jax.lax.top_k(scores, K)
        weights = jnp.take_along_axis(logits, topi, axis=-1) * ROUTE_SCALE
        weights = weights.astype(flat.dtype)
        capacity = math.ceil(N * K / n_experts * 1.25)

        def per_expert(gid, w1, w3, w2):
            match = topi == gid
            assigned = match.any(-1)
            w_tok = jnp.sum(jnp.where(match, weights, 0.0), -1)
            wm = jnp.where(assigned, w_tok, -jnp.inf)
            vals, idx = jax.lax.top_k(wm, capacity)
            valid = assigned[idx]
            xs = flat[idx]
            y = _swiglu(xs, w1, w3, w2) * jnp.where(valid, vals, 0.0)[:, None]
            return (idx, y)
        idxs, ys = jax.vmap(per_expert)(jnp.arange(n_experts), ew1, ew3, ew2)
        out = jnp.zeros_like(flat).at[idxs.reshape(-1)].add(ys.reshape(-1, Dx))
        shared = jax.vmap(lambda w1, w3, w2: _swiglu(flat, w1, w3, w2))(sw1, sw3, sw2)
        out = out + shared.mean(0)
        return out.reshape(Bx, Tx, Dx)

    def _L1_attn_ref(hidden_states, Wq, bq, Wk, bk, Wv, bv, Wo, bo, dist_emb):
        import jax, jax.numpy as jnp
        import numpy as np
        HIDDEN = 128
        NUM_HEADS = 16
        HEAD = HIDDEN // NUM_HEADS
        LEFT = 64
        RIGHT = 8
        NUM_POS = LEFT + RIGHT + 1
        B, L, H = hidden_states.shape
        scale = 1.0 / np.sqrt(HEAD)

        def proj(W, b):
            return (hidden_states @ W.T + b).reshape(B, L, NUM_HEADS, HEAD).transpose(0, 2, 1, 3)
        q = proj(Wq, bq)
        k = proj(Wk, bk)
        v = proj(Wv, bv)
        attn = jnp.einsum('bhld,bhrd->bhlr', q, k) * scale
        dist = jnp.arange(L)[None, :] - jnp.arange(L)[:, None]
        dist = jnp.clip(dist, -LEFT, RIGHT) + LEFT
        pos_emb = dist_emb[dist]
        rel = jnp.einsum('bhld,lrd->bhlr', q, pos_emb) * scale
        attn = jax.nn.softmax(attn + rel, axis=-1)
        out = jnp.einsum('bhlr,bhrd->bhld', attn, v)
        out = out.transpose(0, 2, 1, 3).reshape(B, L, H)
        return out @ Wo.T + bo

    def _L1_xattn_ref(q_in, k_v, Wq, bq, Wk, bk, Wv, bv):
        import jax, jax.numpy as jnp
        import numpy as np
        EMBED = 128
        B, I, J = (8, 256, 256)
        SCALE = EMBED ** (-0.5)
        q = q_in @ Wq + bq
        k = k_v @ Wk + bk
        v = k_v @ Wv + bv
        sim = jnp.einsum('bid,bjd->bij', q, k) * SCALE
        attn = jax.nn.softmax(sim, axis=-1)
        out = jnp.einsum('bij,bjd->bid', attn, v)
        return out

    def _L1_ffn_ref(x, kernel_router_DE, kernel_gating_EDF, kernel_up_EDF, kernel_down_EFD):
        import jax, jax.numpy as jnp
        import numpy as np
        TOP_K = 2
        E = kernel_router_DE.shape[-1]
        x = x.astype(jnp.float32)
        router_logits_BTE = jnp.einsum('BTD,DE->BTE', x, kernel_router_DE)
        probs_BTE = jax.nn.softmax(router_logits_BTE.astype(jnp.float32), axis=-1)
        weights_BTX, indices_BTX = jax.lax.top_k(probs_BTE, TOP_K)
        norm_weights_BTX = jax.nn.softmax(weights_BTX, axis=-1)
        one_hot_BTXE = jax.nn.one_hot(indices_BTX, num_classes=E, dtype=jnp.float32)
        full_weights_BTE = jnp.sum(one_hot_BTXE * norm_weights_BTX[..., None], axis=2)
        gating_BTEF = jnp.einsum('BTD,EDF->BTEF', x, kernel_gating_EDF)
        fuse_BTEF = jax.nn.silu(gating_BTEF) * jnp.einsum('BTD,EDF->BTEF', x, kernel_up_EDF)
        down_BTED = jnp.einsum('BTEF,EFD->BTED', fuse_BTEF, kernel_down_EFD)
        out_BTD = jnp.einsum('BTED,BTE->BTD', down_BTED, full_weights_BTE)
        return out_BTD.astype(jnp.float32)
    x = x + _L0_attn_ref(_layernorm(x, axis=-1), L0_attn_wq, L0_attn_wk, L0_attn_wv, L0_attn_wo)
    x = x + _L0_xattn_ref(_layernorm(x, axis=-1), ctx_1024, mask_BxS2_bf1, L0_xattn_Wq, L0_xattn_bq, L0_xattn_Wkv, L0_xattn_bkv, L0_xattn_Wo, L0_xattn_bo)
    x = x + _L0_ffn_ref(_layernorm(x, axis=-1), L0_ffn_gate_w, L0_ffn_gate_b, L0_ffn_ew1, L0_ffn_ew3, L0_ffn_ew2, L0_ffn_sw1, L0_ffn_sw3, L0_ffn_sw2)
    x = x + _L1_attn_ref(_layernorm(x, axis=-1), L1_attn_Wq, L1_attn_bq, L1_attn_Wk, L1_attn_bk, L1_attn_Wv, L1_attn_bv, L1_attn_Wo, L1_attn_bo, L1_attn_dist_emb)
    x = x + _L1_xattn_ref(_layernorm(x, axis=-1), ctx_1024, L1_xattn_Wq, L1_xattn_bq, L1_xattn_Wk, L1_xattn_bk, L1_xattn_Wv, L1_xattn_bv)
    x = x + _L1_ffn_ref(_layernorm(x, axis=-1), L1_ffn_kernel_router_DE, L1_ffn_kernel_gating_EDF, L1_ffn_kernel_up_EDF, L1_ffn_kernel_down_EFD)
    return x

_drawn_inputs = setup_inputs


def setup_inputs(seed=0):
    import zlib

    import numpy as np

    out = dict(_drawn_inputs(seed))
    spreads = {'L0_xattn_bq': (0.0, 0.385),
     'L0_xattn_bkv': (0.0, 0.1),
     'L0_xattn_bo': (0.0, 0.1),
     'L0_ffn_gate_b': (0.0, 0.689),
     'L1_xattn_bq': (0.0, 0.754),
     'L1_xattn_bk': (0.0, 2.0),
     'L1_xattn_bv': (0.0, 0.319)}
    factors = {'L0_attn_wq': 8.0,
     'L0_attn_wk': 8.0,
     'L0_attn_wv': 2.867,
     'L0_attn_wo': 2.784,
     'L0_ffn_gate_w': 6.286,
     'L0_ffn_ew1': 6.701,
     'L0_ffn_ew3': 6.631,
     'L0_ffn_ew2': 6.192,
     'L0_ffn_sw1': 3.411,
     'L0_ffn_sw3': 3.525,
     'L0_ffn_sw2': 3.44,
     'L1_attn_bq': 62.528,
     'L1_attn_bk': 64.0,
     'L1_attn_bo': 16.92,
     'L1_attn_bv': 8.0,
     'L1_attn_dist_emb': 2.794}
    for name, (base, spread) in spreads.items():
        noise = np.random.default_rng([zlib.crc32(name.encode()), seed]).standard_normal(out[name].shape)
        drawn = base * np.exp(spread * noise) if base else spread * noise
        out[name] = jnp.asarray(drawn.astype(out[name].dtype))
    for name, factor in factors.items():
        out[name] = (out[name] * factor).astype(out[name].dtype)
    return out
```

```python
from contextlib import ExitStack

import numpy as np

import concourse.bass as bass
from concourse import mybir
from concourse.bass import ds

F32 = mybir.dt.float32
BF16 = mybir.dt.bfloat16
U8 = mybir.dt.uint8
ALU = mybir.AluOpType
ACT = mybir.ActivationFunctionType
AX = mybir.AxisListType
RMAX = bass.bass_isa.ReduceOp.max

P = 128
B, SEQ, D = 4, 512, 128
TOK = B * SEQ
NT = TOK // P
QT = SEQ // P
LK = 77
H = 16
DK = 64
HP = H // 2
HD = D // H
E0, E1 = 16, 8
NSH = 2
FF = 256
CAP = -(-TOK * 2 // E0 * 5 // 4)
LEFT, RIGHT = 64, 8
NPOS = LEFT + RIGHT + 1
LG = 16
HG = 8
EPS = 1e-5
BISECT = 30
OFF = SEQ - LG

C_ID = 0
C_MH = C_ID + P
C_DL = C_MH + H
C_IO = C_DL + LG
C_TRI = C_IO + E0
C_CQ = C_TRI + P
C_SQ = C_CQ + SEQ
C_CK = C_SQ + SEQ
C_SK = C_CK + LK
C_N = C_SK + LK


def shape_constants():
    c = np.zeros((P, C_N), np.float32)
    p = np.arange(P)
    c[:, C_ID:C_ID + P] = np.eye(P)
    c[p, C_MH + p // HD] = 1.0
    c[p, C_DL + p // HD] = 1.0
    c[:, C_IO:C_IO + E0] = np.arange(E0)
    c[:, C_TRI:C_TRI + P] = np.triu(np.ones((P, P)), 1)
    inv = (1.0 / 10000.0 ** (np.arange(0, HD, 2, dtype=np.float32) / HD)).astype(np.float32)
    sign = np.where(p % 2 == 0, -1.0, 1.0)[:, None]
    for n, at_c, at_s, scale in ((SEQ, C_CQ, C_SQ, 64 ** -0.5), (LK, C_CK, C_SK, 1.0)):
        pos = (np.float32(10.0) * (np.arange(n, dtype=np.float32) / np.float32(n))).astype(np.float32)
        ang = (pos[None, :] * inv[(p % HD) // 2][:, None]).astype(np.float32)
        c[:, at_c:at_c + n] = np.cos(ang) * scale
        c[:, at_s:at_s + n] = np.sin(ang) * sign * scale
    return c


def bcast(ap, axis, n):
    a = ap.unsqueeze(axis)
    shape = list(a.shape)
    shape[axis] = n
    return a.broadcast_to(shape)


def decoder_kernel(nc, a, out):
    ctx = ExitStack()
    with ctx:
        def sb(name, shape, dt=F32):
            return ctx.enter_context(nc.sbuf_tensor(name, shape, dt))

        def sem(name):
            return ctx.enter_context(nc.semaphore(name))

        bank = [ctx.enter_context(nc.psum_tensor(f"bank{i}", [P, 512], F32)) for i in range(8)]
        q_by_row = nc.dram_tensor("q_by_row", (TOK, D), F32, kind="Internal").ap()

        X = sb("X", [P, NT, D])
        hT = sb("hT", [P, TOK])
        cst = sb("cst", [P, C_N])
        ident = cst[:, C_ID:C_ID + P]
        headmask = cst[:, C_MH:C_MH + H]
        rowmask = cst[:, C_DL:C_DL + LG]
        iota = cst[:, C_IO:C_IO + E0]
        tri = cst[:, C_TRI:C_TRI + P]
        ones = sb("ones", [P, P])
        ones_bf = sb("ones_bf", [1, P], BF16)

        xc = sb("xc", [P, QT, D])
        xsq = sb("xsq", [P, QT, D])
        ln_h = sb("ln_h", [P, NT, D])
        ln_mean = sb("ln_mean", [P, QT])
        ln_var = sb("ln_var", [P, QT])
        ln_std = sb("ln_std", [P, QT])
        ln_rstd = sb("ln_rstd", [P, QT])
        ln_new = sb("ln_new", [P, QT])

        wqkv0 = sb("wqkv0", [P, 4 * H * DK])
        wqkv = wqkv0[:, 0:3 * H * DK].rearrange("p (i n) -> p i n", i=3)
        wo0 = wqkv0[:, 3 * H * DK:].rearrange("p (c n) -> p c n", n=D)
        x0w = sb("x0w", [P, 6, D])
        x0b = sb("x0b", [P, 4])
        x0rows = sb("x0rows", [1, 2, D])
        x1w = sb("x1w", [P, 3, D])
        x1b = sb("x1b", [P, 2])
        x1rows = sb("x1rows", [1, D])
        a1w = sb("a1w", [P, 5, D])
        a1b = sb("a1b", [P, 2])
        a1bs = sb("a1bs", [P, 1])
        a1rows = sb("a1rows", [1, 3, D])
        emb = sb("emb", [HD, NPOS])
        gw0 = sb("gw0", [P, E0])
        gb0 = sb("gb0", [P, E0])
        gw1 = sb("gw1", [P, E1])
        w13 = sb("w13", [P, E0 + NSH, 2, FF])
        w2 = sb("w2", [P, E0 + NSH, 2, D])
        ctxT = sb("ctxT", [P, B * LK])
        mask8 = sb("mask8", [1, B * LK], U8)
        maskrow = sb("maskrow", [1, B * LK], BF16)

        wst = sb("wst", [P, 3, P])
        hst = sb("hst", [P, SEQ])
        qT = sb("qT", [P, SEQ])
        kT = sb("kT", [P, SEQ])
        vtok = sb("vtok", [P, QT, P])
        arena = sb("arena", [P, 4, QT, SEQ])
        prob = [arena[:, i, :, :] for i in range(2)]
        probT = [arena[:, 2 + i, :, :] for i in range(2)]
        negmax = sb("negmax", [P, 2 * QT])
        den = sb("den", [P, 2 * QT])
        rden = sb("rden", [P, 2, QT])
        feats = sb("feats", [P, QT, P])
        featsT = sb("featsT", [P, SEQ])

        big_q = sb("big_q", [P, TOK])
        big_k = sb("big_k", [P, B, H, LK])
        big_k_flat = big_k[:, :, :, :].rearrange("p b h k -> p (b h k)")
        a1_k = big_k_flat[:, 0:TOK]
        a1_q2 = big_k_flat[:, TOK:2 * TOK].rearrange("p (g h) -> p g h", h=H)
        vx0 = sb("vx0", [LK, B, H, HD + 1])
        k1T = sb("k1T", [P, B * LK])
        vx1 = sb("vx1", [LK, B, D])
        krope = sb("krope", [P, B, LK])
        krope2 = sb("krope2", [P, B, LK])
        qrope2 = sb("qrope2", [P, SEQ])
        qst = sb("qst", [P, P])
        mx0 = sb("mx0", [P, H])
        rd0 = sb("rd0", [P, H])
        f0 = sb("f0", [P, D])
        f0T = sb("f0T", [P, D])
        prob0 = prob[0][:, :, :].rearrange("p a b -> p (a b)")[:, 0:H * LK]
        shifted0 = prob[1][:, :, :].rearrange("p a b -> p (a b)")[:, 0:H * LK]
        prob0T = probT[0][:, :, :]

        w13st = arena[:, 3, 0:2, :].rearrange("p e (w f) -> p e w f", w=2)
        silu = arena[:, 3, 2:4, :]
        hid = arena[:, 1, :, :].rearrange("p (u h) t -> p u h t", u=2)
        g_tiles = arena[:, 2, :, :].rearrange("p a (b t e) -> p (a b) t e", b=2, e=E0)
        G = sb("G", [P, NT, E0 + NSH])
        g_lg = g_tiles[:, 0, :, :]
        g_sc = g_tiles[:, 1, :, :]
        g_t1 = g_tiles[:, 2, :, :]
        g_t2 = g_tiles[:, 3, :, :]
        g_oh1 = g_tiles[:, 4, :, :]
        g_oh2 = g_tiles[:, 5, :, :]
        g_wm = g_tiles[:, 6, :, :]
        g_m1 = sb("g_m1", [P, NT])
        g_m2 = sb("g_m2", [P, NT])
        g_mx = sb("g_mx", [P, NT])
        g_abs = sb("g_abs", [P, 1])
        g_all = sb("g_all", [P, 1])
        g_step = sb("g_step", [P, 1])
        g_lo = sb("g_lo", [P, E0])
        g_try = sb("g_try", [P, E0])
        g_cnt = sb("g_cnt", [P, E0])
        g_inc = sb("g_inc", [P, E0])

        spare = w13[:, E1:, :, :].rearrange("p e w f -> p (e w f)")
        embpad = spare[0:HD, 0:2 * SEQ - 1]
        relT = spare[:, 2 * SEQ:2 * SEQ + SEQ + OFF]
        vst = spare[:, 4 * SEQ:4 * SEQ + QT * H * 32].rearrange("p (k h d) -> p k h d", h=H, d=32)
        blocks = wqkv0[:, 0:4 * P * HG].rearrange("p (n g l h) -> p n g l h", n=4, l=LG, h=HG)
        qblk = [blocks[:, i, :, :, :] for i in range(2)]
        rblk = [blocks[:, 2 + i, :, :, :] for i in range(2)]
        v1 = ln_h
        osb = sb("osb", [P, 2, P])
        rd1 = sb("rd1", [P, HG])
        feats1 = sb("feats1", [P, D])
        feats1T = sb("feats1T", [P, D])
        qtok = prob[0][:, :, :].rearrange("p a (c d) -> p (a c) d", d=D)
        ptile = [hst[:, :], qT[:, :], kT[:, :], vtok[:, :, :].rearrange("p a b -> p (a b)")]
        probTh = [arena[:, 2 - 2 * i:4 - 2 * i, :, :].rearrange("p a b (c l) -> p (a b c) l", l=P)
                  .rearrange("p (k h) l -> p k h l", k=QT) for i in range(2)]

        ld_x, ld_cst, ld_a0, ld_x0, ld_f0, ld_a1, ld_x1, ld_f1 = (
            sem(n) for n in ("ld_x", "ld_cst", "ld_a0", "ld_x0", "ld_f0", "ld_a1", "ld_x1", "ld_f1"))
        stored = sem("stored")
        setup = sem("setup")
        ln_step, ln_var_ok, ln_std_ok, ln_ready, ln_tp, ln_out = (
            sem(n) for n in ("ln_step", "ln_var_ok", "ln_std_ok", "ln_ready", "ln_tp", "ln_out"))
        pre_mm, pre_act, pre_dve, pre_pool = (sem(n) for n in ("pre_mm", "pre_act", "pre_dve", "pre_pool"))
        a0_staged, a0_q, a0_k, a0_v, a0_s, a0_t, a0_pv, a0_ft, a0_o = (
            sem("a0_" + n) for n in ("staged", "q", "k", "v", "s", "t", "pv", "ft", "o"))
        a0_qc, a0_kc, a0_vc, a0_exp, a0_max, a0_tc, a0_rd, a0_norm, a0_ftc, a0_x = (
            sem("a0_" + n) for n in ("qc", "kc", "vc", "exp", "max", "tc", "rd", "norm", "ftc", "x"))
        x0_q, x0_qr, x0_staged, x0_s, x0_t, x0_pv, x0_ft, x0_o = (
            sem("x0_" + n) for n in ("q", "qr", "staged", "s", "t", "pv", "ft", "o"))
        x0_max, x0_sub, x0_exp, x0_tcd, x0_tca, x0_rd, x0_norm, x0_ftc, x0_x = (
            sem("x0_" + n) for n in ("max", "sub", "exp", "tcd", "tca", "rd", "norm", "ftc", "x"))
        g_mm, g_chain, g_exp, g_pool, b_chain, b_cnt = (
            sem(n) for n in ("g_mm", "g_chain", "g_exp", "g_pool", "b_chain", "b_cnt"))
        ffs = [{n: sem(f"f{i}_{n}") for n in ("staged", "h", "silu", "hid", "y", "acc")} for i in range(2)]
        a1_pre_mm, a1_pre_act, a1_pre_dve, a1_qout, a1_qin, a1_rel = (
            sem("a1_" + n) for n in ("pre_mm", "pre_act", "pre_dve", "qout", "qin", "rel"))
        a1_qb, a1_vs, a1_s, a1_t, a1_pv, a1_ot, a1_ft, a1_o = (
            sem("a1_" + n) for n in ("qb", "vs", "s", "t", "pv", "ot", "ft", "o"))
        a1_max, a1_exp, a1_tc, a1_oc, a1_rd, a1_norm, a1_ftc, a1_x = (
            sem("a1_" + n) for n in ("max", "exp", "tc", "oc", "rd", "norm", "ftc", "x"))
        x1_q, x1_qc, x1_staged, x1_s, x1_max, x1_sub, x1_exp, x1_den, x1_t, x1_tc, x1_pv, x1_x = (
            sem("x1_" + n) for n in
            ("q", "qc", "staged", "s", "max", "sub", "exp", "den", "t", "tc", "pv", "x"))

        A0, X0, F0, A1, X1, F1 = range(6)
        SCALE1 = float(1.0 / np.sqrt(HD))
        SCALEX1 = float(D) ** -0.5
        LT = P // LG

        block = ctx.enter_context(nc.Block())

        @block.sync
        def _(sp):
            sp.dma_start(X[:, :, :], a["x"].rearrange("(t p) d -> p t d", p=P)).then_inc(ld_x, 16)
            sp.dma_start(cst[:, :], a["cst"]).then_inc(ld_cst, 16)
            for i, n in enumerate(("wq", "wk", "wv")):
                sp.dma_start(wqkv[:, i, :], a[n]).then_inc(ld_a0, 16)
            sp.dma_start(wo0[:, :, :], a["wo"].rearrange("(c p) n -> p c n", p=P)).then_inc(ld_a0, 16)
            sp.dma_start(ctxT[:, :], a["ctxT"]).then_inc(ld_x0, 16)
            sp.dma_start(mask8[:, :], a["mask"]).then_inc(ld_x0, 16)
            sp.dma_start(x0w[:, :, :], a["x0w"]).then_inc(ld_x0, 16)
            sp.dma_start(x0b[:, :], a["x0b"]).then_inc(ld_x0, 16)
            sp.dma_start(x0rows[:, :, :], a["x0rows"]).then_inc(ld_x0, 16)
            sp.dma_start(x1w[:, :, :], a["x1w"]).then_inc(ld_x0, 16)
            sp.dma_start(x1b[:, :], a["x1b"]).then_inc(ld_x0, 16)
            sp.dma_start(x1rows[:, :], a["x1rows"]).then_inc(ld_x0, 16)
            sp.dma_start(gw0[:, :], a["gw0"]).then_inc(ld_f0, 16)
            sp.dma_start(gb0[:, :], a["gb0"].partition_broadcast(P)).then_inc(ld_f0, 16)
            sp.dma_start(w13[:, 0:E0, 0, :], a["ew1"].rearrange("e d f -> d e f")).then_inc(ld_f0, 16)
            sp.dma_start(w13[:, 0:E0, 1, :], a["ew3"].rearrange("e d f -> d e f")).then_inc(ld_f0, 16)
            sp.dma_start(w13[:, E0:, 0, :], a["sw1"].rearrange("e d f -> d e f")).then_inc(ld_f0, 16)
            sp.dma_start(w13[:, E0:, 1, :], a["sw3"].rearrange("e d f -> d e f")).then_inc(ld_f0, 16)
            for hf in range(2):
                sp.dma_start(w2[:, 0:E0, hf, :], a["ew2"][:, hf * P:(hf + 1) * P, :].rearrange("e p d -> p e d")).then_inc(ld_f0, 16)
                sp.dma_start(w2[:, E0:, hf, :], a["sw2"][:, hf * P:(hf + 1) * P, :].rearrange("e p d -> p e d")).then_inc(ld_f0, 16)
            sp.dma_start(a1w[:, :, :], a["a1w"]).then_inc(ld_a1, 16)
            sp.dma_start(a1b[:, :], a["a1b"]).then_inc(ld_a1, 16)
            sp.dma_start(a1rows[:, :, :], a["a1rows"]).then_inc(ld_a1, 16)
            sp.dma_start(emb[:, :], a["emb"]).then_inc(ld_a1, 16)
            sp.dma_start(gw1[:, :], a["gw1"]).then_inc(ld_a1, 16)
            sp.wait_ge(a1_pre_dve, 3)
            for l in range(LG):
                sp.dma_start(relT[l * HD:(l + 1) * HD, :],
                             embpad[:, LG - 1 - l:LG - 1 - l + SEQ + OFF]).then_inc(a1_rel, 16)
            sp.wait_ge(ffs[0]["y"], (E0 + NSH) * B)
            sp.dma_start(w13[:, 0:E1, 0, :], a["f1g"].rearrange("e d f -> d e f")).then_inc(ld_f1, 16)
            sp.dma_start(w13[:, 0:E1, 1, :], a["f1u"].rearrange("e d f -> d e f")).then_inc(ld_f1, 16)
            for hf in range(2):
                sp.dma_start(w2[:, 0:E1, hf, :], a["f1d"][:, hf * P:(hf + 1) * P, :].rearrange("e p d -> p e d")).then_inc(ld_f1, 16)
            sp.wait_ge(a1_pre_act, 8)
            sp.dma_start(q_by_row.rearrange("(t p) n -> p t n", p=P), qtok).then_inc(a1_qout, 16)
            sp.wait_ge(a1_qout, 16)
            sp.dma_start(a1_q2, q_by_row.rearrange("(g l) (d h) -> (l d) g h", l=LG, h=H)).then_inc(a1_qin, 16)
            sp.wait_ge(ffs[1]["acc"], E1 * B)
            sp.dma_start(out.rearrange("(t p) d -> p t d", p=P), X[:, :, :]).then_inc(stored, 16)
            sp.wait_ge(stored, 16)

        @block.gpsimd
        def _(pool):
            pool.memset(ones[:, :], 1.0).then_inc(setup, 1)
            pool.memset(ones_bf[:, :], 1.0).then_inc(setup, 1)
            pool.memset(vx0[:, :, :, HD:HD + 1], 1.0).then_inc(setup, 1)
            pool.memset(G[:, :, E0:], 1.0 / NSH).then_inc(setup, 1)
            pool.wait_ge(ld_cst, 16)
            pool.wait_ge(pre_dve, 4)
            for b in range(B):
                pool.tensor_tensor(big_k[:, b, :, :], bcast(krope[:, b, :], 1, H), bcast(headmask, 2, LK),
                                   ALU.mult).then_inc(pre_pool, 1)
            pool.wait_ge(ld_a0, 64)
            pool.wait_ge(ln_out, 4)

            def stage_a0(g):
                for i in range(3):
                    pool.tensor_copy(wst[:, i, :], wqkv[:, i, ds((g % HP) * P, P)]).then_inc(a0_staged, 1)
                pool.tensor_copy(hst[:, :], hT[:, ds((g // HP) * SEQ, SEQ)]).then_inc(a0_staged, 1)

            stage_a0(0)
            with pool.Fori(1, B * HP) as g:
                pool.wait_ge(a0_v, g)
                stage_a0(g)
            pool.wait_ge(x0_qr, 4)
            pool.tensor_copy(qst[:, :], big_q[:, 0:P]).then_inc(x0_staged, 1)
            with pool.Fori(1, NT) as t:
                pool.wait_ge(x0_s, t * 3)
                pool.tensor_copy(qst[:, :], big_q[:, ds(t * P, P)]).then_inc(x0_staged, 1)

            def feed_forward(f, n, loaded, count):
                s = ffs[f]
                pool.wait_ge(loaded, count)
                for e in range(2):
                    pool.tensor_copy(w13st[:, e, :, :], w13[:, e, :, :]).then_inc(s["staged"], 1)
                with pool.Fori(1, n // 2) as i:
                    for e in range(2):
                        pool.wait_ge(s["h"], i * 16 - 8 + e * 8)
                        pool.tensor_copy(w13st[:, e, :, :], w13[:, ds(i * 2 + e, 1), :, :].rearrange("p a b c -> p (a b) c")).then_inc(s["staged"], 1)

            pool.wait_ge(g_pool, 1)
            pool.partition_all_reduce(g_all[:, :], g_abs[:, :], P, RMAX).then_inc(g_pool, 1)
            feed_forward(0, E0 + NSH, ld_f0, 160)

            pool.wait_ge(a1_pre_act, 4)
            pool.wait_ge(a1_qin, 16)
            pool.wait_ge(a1_pre_dve, 12)
            pool.memset(vst, 0.0).then_inc(setup, 1)
            pool.wait_ge(setup, 5)
            pool.memset(vst[:, :, :, HD:HD + 1], 1.0).then_inc(setup, 1)

            def stage_a1(it, first):
                for hg in range(2):
                    if not first:
                        pool.wait_ge(a1_s, it * 16 - 8 + hg * 8)
                    pool.tensor_tensor(
                        rblk[hg][:, :, :, :],
                        bcast(a1_q2[:, ds(it * LT, LT), hg * HG:(hg + 1) * HG], 2, LG),
                        bcast(bcast(rowmask, 2, HG), 1, LT), ALU.mult).then_inc(a1_qb, 1)
                    pool.tensor_tensor(
                        qblk[hg][:, :, :, :],
                        bcast(big_q[:, ds(it * P, P)].rearrange("p (g l) -> p g l", l=LG), 3, HG),
                        bcast(bcast(headmask[:, hg * HG:(hg + 1) * HG], 1, LG), 1, LT), ALU.mult).then_inc(a1_qb, 1)
                if not first:
                    pool.wait_ge(a1_pv, it * 2)
                pool.tensor_copy(vst[:, :, :, 0:HD],
                                 v1[:, ds((it // QT) * QT, QT), :].rearrange("p a (h d) -> p a h d", d=HD)).then_inc(a1_vs, 1)

            stage_a1(0, True)
            with pool.Fori(1, NT) as it:
                stage_a1(it, False)

            pool.wait_ge(x1_qc, 4)
            pool.tensor_copy(hst[:, :], big_q[:, 0:SEQ]).then_inc(x1_staged, 1)
            with pool.Fori(1, B) as b:
                pool.wait_ge(x1_s, b)
                pool.tensor_copy(hst[:, :], big_q[:, ds(b * SEQ, SEQ)]).then_inc(x1_staged, 1)
            feed_forward(1, E1, ld_f1, 64)

        @block.scalar
        def _(act):
            def norm_layer(layer):
                for b in range(B):
                    act.wait_ge(ln_var_ok, layer * B + b + 1)
                    act.activation(ln_std[:, :], ln_var[:, :], ACT.Sqrt).then_inc(ln_std_ok, 1)
                    act.wait_ge(ln_tp, layer * B + b + 1)
                    act.activation(hT[:, b * SEQ:(b + 1) * SEQ], bank[4 + b][:, :], ACT.Copy).then_inc(ln_out, 1)

            norm_layer(A0)
            act.wait_ge(ld_x0, 128)
            act.wait_ge(pre_mm, 3)
            act.activation(k1T[:, :], bank[2][:, 0:B * LK], ACT.Identity, bias=x1b[:, 1:2]).then_inc(pre_act, 1)
            act.wait_ge(setup, 4)
            act.wait_ge(pre_mm, 4)
            act.activation(vx0[:, :, :, 0:HD], bank[3][0:LK, :].rearrange("p (b h d) -> p b h d", b=B, d=HD),
                           ACT.Copy).then_inc(pre_act, 1)
            act.wait_ge(pre_mm, 5)
            act.activation(vx1[:, :, :], bank[4][0:LK, :].rearrange("p (b d) -> p b d", b=B), ACT.Copy).then_inc(pre_act, 1)

            def a0_turn(g):
                act.wait_ge(a0_q, g + 1)
                act.activation(qT[:, :], bank[6][:, :], ACT.Copy, scale=float(DK) ** -0.5).then_inc(a0_qc, 1)
                act.wait_ge(a0_k, g + 1)
                act.activation(kT[:, :], bank[7][:, :], ACT.Copy).then_inc(a0_kc, 1)
                act.wait_ge(a0_v, g + 1)
                act.activation(vtok[:, :, :], bank[6][:, :].rearrange("p (a b) -> p a b", a=QT), ACT.Copy).then_inc(a0_vc, 1)
                for h in range(2):
                    for j in range(QT):
                        act.wait_ge(a0_max, g * 8 + h * 4 + j + 1)
                        act.activation(prob[h][:, j, :], bank[j][:, :], ACT.Exp,
                                       bias=negmax[:, h * QT + j:h * QT + j + 1],
                                       accum_out=den[:, h * QT + j:h * QT + j + 1]).then_inc(a0_exp, 1)

            a0_turn(0)
            with act.Fori(1, B * HP) as g:
                a0_turn(g)

            norm_layer(X0)

            def x0_copies(t):
                for c in (1, 3):
                    act.wait_ge(x0_t, t * 4 + c + 1)
                    act.activation(prob0T[0:LK, c, :], bank[4 + c % 2][0:LK, :], ACT.Copy).then_inc(x0_tca, 1)

            def x0_exps(t, first):
                act.wait_ge(x0_sub, t * 3 + 3)
                if not first:
                    act.wait_ge(x0_t, t * 4)
                act.activation(prob0, shifted0, ACT.Exp).then_inc(x0_exp, 1)

            x0_exps(0, True)
            with act.Fori(1, NT) as t:
                x0_copies(t - 1)
                x0_exps(t, False)
            x0_copies(NT - 1)

            def feed_forward(f, n):
                s = ffs[f]
                with act.Fori(0, n // 2) as i:
                    for u in range(16):
                        act.wait_ge(s["h"], i * 16 + u + 1)
                        if u >= 2:
                            act.wait_ge(s["hid"], i * 16 + u - 1)
                        act.activation(silu[:, u % 2, :], bank[2 * (u % 2)][:, :], ACT.Silu).then_inc(s["silu"], 1)

            norm_layer(F0)
            act.wait_ge(g_exp, 1)
            act.activation(g_t2[:, :, :], g_t1[:, :, :], ACT.Exp).then_inc(g_exp, 1)
            feed_forward(0, E0 + NSH)

            norm_layer(A1)
            act.wait_ge(a1_pre_dve, 4)
            for b in range(B):
                act.wait_ge(a1_pre_mm, b + 1)
                act.activation(big_q[:, b * SEQ:(b + 1) * SEQ], bank[b][:, :], ACT.Identity,
                               bias=a1bs[:, :], scale=SCALE1).then_inc(a1_pre_act, 1)
            for b in range(B):
                act.wait_ge(a1_pre_mm, 8 + b + 1)
                act.activation(qtok[:, b * QT:(b + 1) * QT, :], bank[b][:, :].rearrange("p (t d) -> p t d", d=D),
                               ACT.Copy, scale=SCALE1).then_inc(a1_pre_act, 1)

            def a1_turn(it):
                for n in range(16):
                    act.wait_ge(a1_max, it * 16 + n + 1)
                    act.activation(ptile[n % 4], bank[n % 4][:, :], ACT.Exp, bias=negmax[:, n % 8:n % 8 + 1]).then_inc(a1_exp, 1)

            with act.Fori(0, NT) as it:
                a1_turn(it)

            norm_layer(X1)
            for b in range(B):
                act.wait_ge(x1_q, b + 1)
                act.activation(big_q[:, b * SEQ:(b + 1) * SEQ], bank[b][:, :], ACT.Identity, bias=x1b[:, 0:1]).then_inc(x1_qc, 1)
            with act.Fori(0, B) as b:
                act.wait_ge(x1_sub, b + 1)
                act.activation(prob0[:, 0:QT * LK], shifted0[:, 0:QT * LK], ACT.Exp, scale=SCALEX1).then_inc(x1_exp, 1)
                act.wait_ge(x1_t, b + 1)
                act.activation(prob0T[0:LK, 0, :], bank[4][0:LK, :], ACT.Copy).then_inc(x1_tc, 1)

            norm_layer(F1)
            act.wait_ge(g_exp, 3)
            act.activation(g_t2[:, :, 0:E1], g_t1[:, :, 0:E1], ACT.Exp).then_inc(g_exp, 1)
            act.wait_ge(g_exp, 5)
            act.activation(g_m1[:, :], g_m2[:, :], ACT.Exp).then_inc(g_exp, 1)
            feed_forward(1, E1)

        @block.tensor
        def _(pe):
            def norm_layer(layer):
                for b in range(B):
                    pe.wait_ge(ln_ready, layer * B + b + 1)
                    for t in range(QT):
                        mm = pe.transpose(bank[4 + b][:, t * P:(t + 1) * P], ln_h[:, b * QT + t, :], ident)
                    mm.then_inc(ln_tp, 1)

            pe.wait_ge(ld_cst, 16)
            pe.wait_ge(setup, 4)
            norm_layer(A0)
            pe.wait_ge(ld_x0, 128)
            pe.wait_ge(ln_out, 4)
            for i, w in enumerate((x0w[:, 2, :], x0w[:, 3, :], x1w[:, 1, :])):
                pe.matmul(bank[i][:, 0:B * LK], w, ctxT[:, :], start=True, stop=True).then_inc(pre_mm, 1)
            for i, (w, row) in enumerate(((x0w[:, 4, :], x0rows[:, 0, :]), (x1w[:, 2, :], x1rows[:, :]))):
                for b in range(B):
                    o = bank[3 + i][0:LK, b * D:(b + 1) * D]
                    pe.matmul(o, ctxT[:, b * LK:(b + 1) * LK], w, start=True, stop=False)
                    mm = pe.matmul(o, ones[0:1, 0:LK], row, start=False, stop=True)
                mm.then_inc(pre_mm, 1)
            pe.wait_ge(pre_act, 3)
            pe.wait_ge(pre_dve, 4)

            def a0_turn_t(g, h, kt):
                n = g * 8 + h * 4 + kt
                pe.wait_ge(a0_exp, g * 8 + h * 4 + 4)
                if not (isinstance(n, int) and n < 2):
                    pe.wait_ge(a0_tc, n - 1)
                for q in range(QT):
                    mm = pe.transpose(bank[4 + kt % 2][:, q * P:(q + 1) * P], prob[h][:, q, kt * P:(kt + 1) * P], ident)
                mm.then_inc(a0_t, 1)

            def a0_turn_pv(g, h, o):
                pe.wait_ge(a0_tc, g * 8 + h * 4 + 4)
                pe.wait_ge(a0_vc, g + 1)
                for q in range(QT):
                    for kt in range(QT):
                        mm = pe.matmul(o[:, q * DK:(q + 1) * DK], probT[h][:, kt, q * P:(q + 1) * P],
                                       vtok[:, kt, h * DK:(h + 1) * DK], start=(kt == 0), stop=(kt == QT - 1))
                mm.then_inc(a0_pv, 1)

            def a0_turn_s(g, h, j, first):
                if h == 0:
                    pe.wait_ge(a0_qc, g + 1)
                    pe.wait_ge(a0_kc, g + 1)
                if not (first and h == 0):
                    pe.wait_ge(a0_exp, g * 8 + h * 4 + j - 3)
                r = h * DK
                pe.matmul(bank[j][:, :], qT[r:r + DK, j * P:(j + 1) * P], kT[r:r + DK, :],
                          start=True, stop=True).then_inc(a0_s, 1)

            def a0_turn_ft(g):
                pe.wait_ge(a0_norm, g * 2 + 2)
                for q in range(QT):
                    mm = pe.transpose(bank[6][:, q * P:(q + 1) * P], feats[:, q, :], ident)
                mm.then_inc(a0_ft, 1)

            def a0_turn_o(g):
                pe.wait_ge(a0_ftc, g + 1)
                for q in range(QT):
                    mm = pe.matmul(bank[7][:, q * P:(q + 1) * P], featsT[:, q * P:(q + 1) * P],
                                   wo0[:, ds(g % HP, 1), :].rearrange("p a n -> p (a n)"), start=True, stop=True)
                mm.then_inc(a0_o, 1)

            def a0_turn(g, first):
                pe.wait_ge(a0_staged, g * 4 + 4)
                if not first:
                    a0_turn_t(g - 1, 1, 2)
                    pe.wait_ge(a0_norm, g * 2 - 1)
                pe.matmul(bank[6][:, :], wst[:, 0, :], hst[:, :], start=True, stop=True).then_inc(a0_q, 1)
                if not first:
                    a0_turn_t(g - 1, 1, 3)
                    pe.wait_ge(a0_max, g * 8 - 3)
                pe.matmul(bank[7][:, :], wst[:, 1, :], hst[:, :], start=True, stop=True).then_inc(a0_k, 1)
                if not first:
                    pe.wait_ge(a0_kc, g + 1)
                    a0_turn_pv(g - 1, 1, bank[7])
                pe.wait_ge(a0_qc, g + 1)
                for kt in range(QT):
                    mm = pe.matmul(bank[6][:, kt * P:(kt + 1) * P], hst[:, kt * P:(kt + 1) * P], wst[:, 2, :],
                                   start=True, stop=True)
                mm.then_inc(a0_v, 1)
                for j in range(QT):
                    a0_turn_s(g, 0, j, first)
                pe.wait_ge(a0_vc, g + 1)
                if not first:
                    a0_turn_ft(g - 1)
                a0_turn_t(g, 0, 0)
                a0_turn_t(g, 0, 1)
                if not first:
                    a0_turn_o(g - 1)
                a0_turn_s(g, 1, 0, first)
                a0_turn_t(g, 0, 2)
                a0_turn_s(g, 1, 1, first)
                a0_turn_t(g, 0, 3)
                a0_turn_s(g, 1, 2, first)
                a0_turn_s(g, 1, 3, first)
                if not first:
                    pe.wait_ge(a0_ftc, g)
                a0_turn_pv(g, 0, bank[6])
                a0_turn_t(g, 1, 0)
                a0_turn_t(g, 1, 1)

            pe.wait_ge(ld_a0, 64)
            a0_turn(0, True)
            with pe.Fori(1, B * HP) as g:
                a0_turn(g, False)
            last = B * HP - 1
            a0_turn_t(last, 1, 2)
            a0_turn_t(last, 1, 3)
            pe.wait_ge(a0_x, last)
            a0_turn_pv(last, 1, bank[7])
            a0_turn_ft(last)
            a0_turn_o(last)

            norm_layer(X0)
            for b in range(B):
                pe.wait_ge(ln_out, X0 * B + b + 1)
                if b >= 2:
                    pe.wait_ge(x0_qr, b - 1)
                for i in range(2):
                    mm = pe.matmul(bank[2 * (b % 2) + i][:, :], x0w[:, i, :], hT[:, b * SEQ:(b + 1) * SEQ], start=True, stop=True)
                mm.then_inc(x0_q, 1)
            pe.wait_ge(x0_qr, 4)
            pe.wait_ge(pre_pool, 4)
            HS = (0, 6, 12, 16)

            def x0_scores(t, first):
                pe.wait_ge(x0_staged, t + 1)
                for i in range(3):
                    n = HS[i + 1] - HS[i]
                    if not first:
                        pe.wait_ge(x0_sub, t * 3 - 2 + i)
                    o = bank[i][:, 0:n * LK]
                    pe.matmul(o, qst[:, :], big_k[:, ds(t // QT, 1), HS[i]:HS[i + 1], :].rearrange("p b h k -> p (b h k)"),
                              start=True, stop=False)
                    pe.matmul(o.rearrange("p (h k) -> p h k", k=LK), ones_bf[:, :],
                              bcast(maskrow[:, ds((t // QT) * LK, LK)], 1, n), start=False, stop=True).then_inc(x0_s, 1)

            def x0_rest(t, first):
                pe.wait_ge(x0_exp, t + 1)
                for c in range(4):
                    if c >= 2:
                        if c % 2 == 0:
                            pe.wait_ge(x0_tcd, t * 2 + c // 2)
                        else:
                            pe.wait_ge(x0_tca, t * 2 + c // 2)
                    for j in range(4):
                        mm = pe.transpose(bank[4 + c % 2][0:LK, j * P:(j + 1) * P],
                                          prob0[:, (c * 4 + j) * LK:(c * 4 + j + 1) * LK], ident)
                    mm.then_inc(x0_t, 1)
                pe.wait_ge(x0_tcd, t * 2 + 2)
                pe.wait_ge(x0_tca, t * 2 + 2)
                for h in range(H):
                    mm = pe.matmul(bank[6][:, h * (HD + 1):(h + 1) * (HD + 1)], prob0T[0:LK, h // 4, (h % 4) * P:(h % 4 + 1) * P],
                                   vx0[:, ds(t // QT, 1), h, :].rearrange("p b d -> p (b d)"), start=True, stop=True)
                mm.then_inc(x0_pv, 1)
                pe.wait_ge(x0_norm, t + 1)
                pe.transpose(bank[7][:, 0:P], f0[:, :], ident).then_inc(x0_ft, 1)
                pe.wait_ge(x0_ftc, t + 1)
                pe.matmul(bank[3][:, 0:D], f0T[:, :], x0w[:, 5, :], start=True, stop=False)
                pe.matmul(bank[3][:, 0:D], ones[0:1, :], x0rows[:, 1, :], start=False, stop=True).then_inc(x0_o, 1)

            x0_scores(0, True)
            with pe.Fori(1, NT) as t:
                x0_scores(t, False)
                x0_rest(t - 1, False)
            x0_rest(NT - 1, False)

            def router(layer, w, n):
                for b in range(B):
                    pe.wait_ge(ln_out, layer * B + b + 1)
                for t in range(NT):
                    mm = pe.matmul(bank[0][:, t * n:(t + 1) * n], hT[:, t * P:(t + 1) * P], w, start=True, stop=True)
                mm.then_inc(g_mm, 1)

            def feed_forward(f, n):
                s = ffs[f]

                def products(i, k):
                    c = k % 4
                    pe.wait_ge(s["hid"], i * 16 + 2 * k + 2)
                    if k >= 2:
                        pe.wait_ge(s["acc"], i * 8 + k - 1)
                    for t in range(QT):
                        for hf in range(2):
                            mm = pe.matmul(bank[4 + k % 2][:, t * P:(t + 1) * P], hid[:, k % 2, hf, t * P:(t + 1) * P],
                                           w2[:, ds(i * 2 + k // 4, 1), hf, :].rearrange("p a n -> p (a n)"),
                                           start=(hf == 0), stop=(hf == 1))
                    mm.then_inc(s["y"], 1)

                with pe.Fori(0, n // 2) as i:
                    for k in range(8):
                        e, c = k // 4, k % 4
                        if c == 0:
                            pe.wait_ge(s["staged"], i * 2 + e + 1)
                        for hf in range(2):
                            u = 2 * k + hf
                            if u >= 2:
                                pe.wait_ge(s["hid"], i * 16 + u - 1)
                            for w in range(2):
                                mm = pe.matmul(bank[2 * (u % 2) + w][:, :], w13st[:, e, w, hf * P:(hf + 1) * P],
                                               hT[:, c * SEQ:(c + 1) * SEQ], start=True, stop=True)
                            mm.then_inc(s["h"], 1)
                        if k >= 1:
                            products(i, k - 1)
                    products(i, 7)

            norm_layer(F0)
            pe.wait_ge(ld_f0, 160)
            router(F0, gw0[:, :], E0)
            with pe.Fori(0, BISECT) as i:
                pe.wait_ge(b_chain, i * 5 + 3)
                pe.matmul(bank[1][:, 0:E0], ones[:, :], g_cnt[:, :], start=True, stop=True).then_inc(b_cnt, 1)
            pe.wait_ge(g_chain, 100)
            pe.matmul(bank[1][:, 0:E0], ones[:, :], g_cnt[:, :], start=True, stop=True)
            pe.matmul(bank[2][:, 0:NT * E0], tri, g_t1[:, :, :].rearrange("p t e -> p (t e)"), start=True, stop=True)
            pe.matmul(bank[3][:, 0:NT * E0], ones[:, :], g_t1[:, :, :].rearrange("p t e -> p (t e)"), start=True, stop=True).then_inc(g_mm, 1)
            pe.wait_ge(g_chain, 200)
            feed_forward(0, E0 + NSH)

            norm_layer(A1)
            pe.wait_ge(ld_a1, 80)
            for i, w in enumerate((0, 2)):
                for b in range(B):
                    pe.wait_ge(ln_out, A1 * B + (b if i == 0 else B - 1) + 1)
                    pe.matmul(bank[4 * i + b][:, :], a1w[:, w, :], hT[:, b * SEQ:(b + 1) * SEQ], start=True, stop=True).then_inc(a1_pre_mm, 1)
            for i, (w, row) in enumerate(((1, 0), (3, 1))):
                for b in range(B):
                    if i == 0:
                        pe.wait_ge(a1_pre_act, b + 1)
                    else:
                        pe.wait_ge(a1_pre_dve, 4 + b + 1)
                    for t in range(QT):
                        o = bank[4 * i + b][:, t * D:(t + 1) * D]
                        tt = b * QT + t
                        pe.matmul(o, hT[:, tt * P:(tt + 1) * P], a1w[:, w, :], start=True, stop=False)
                        mm = pe.matmul(o, ones[0:1, :], a1rows[:, row, :], start=False, stop=True)
                    mm.then_inc(a1_pre_mm, 1)
            pe.wait_ge(a1_pre_act, 8)
            pe.wait_ge(a1_pre_dve, 12)
            pe.wait_ge(a1_rel, 16 * LG)

            def a1_scores(it, n, first):
                hg, lg = n // 8, n % 8
                if lg == 0:
                    pe.wait_ge(a1_qb, it * 4 + hg * 2 + 2)
                if not (first and n < 4):
                    pe.wait_ge(a1_exp, it * 16 + n - 3)
                pe.matmul(bank[n % 4][:, :], qblk[hg][:, lg, :, :].rearrange("p l h -> p (l h)"),
                          a1_k[:, ds((it // QT) * SEQ, SEQ)], start=True, stop=False)
                pe.matmul(bank[n % 4][:, :], rblk[hg][:, lg, :, :].rearrange("p l h -> p (l h)"),
                          relT[:, ds((it % QT) * -P + (OFF - lg * LG), SEQ)], start=False, stop=True).then_inc(a1_s, 1)

            def a1_turn_t(it, n):
                pe.wait_ge(a1_exp, it * 16 + n + 1)
                if not (isinstance(it, int) and it == 0 and n < 2):
                    pe.wait_ge(a1_tc, it * 16 + n - 1)
                for kt in range(QT):
                    mm = pe.transpose(bank[4 + n % 2][:, kt * P:(kt + 1) * P], ptile[n % 4][:, kt * P:(kt + 1) * P], ident)
                mm.then_inc(a1_t, 1)

            def a1_values(it, hg):
                pe.wait_ge(a1_tc, it * 16 + hg * 8 + 8)
                pe.wait_ge(a1_vs, it + 1)
                if not (isinstance(it, int) and it == 0 and hg == 0):
                    pe.wait_ge(a1_oc, it * 2 + hg)
                for grp in range(2):
                    for kt in range(QT):
                        for j in range(4):
                            mm = pe.matmul(bank[6][32 * j:32 * j + 32, grp * P:(grp + 1) * P],
                                           vst[:, kt, hg * HG + grp * 4 + j, :], probTh[hg][:, kt, grp * 4 + j, :],
                                           start=(kt == 0), stop=(kt == QT - 1))
                mm.then_inc(a1_pv, 1)

            def a1_back(it, hg):
                pe.wait_ge(a1_oc, it * 2 + hg + 1)
                if hg == 1:
                    pe.wait_ge(a1_norm, it * 2 + 1)
                elif not (isinstance(it, int) and it == 0):
                    pe.wait_ge(a1_x, it)
                for grp in range(2):
                    mm = pe.transpose(bank[7][:, grp * P:(grp + 1) * P], osb[:, grp, :], ident)
                mm.then_inc(a1_ot, 1)

            def a1_feats(it):
                pe.wait_ge(a1_norm, it * 2 + 2)
                pe.transpose(bank[7][:, 2 * P:3 * P], feats1[:, :], ident).then_inc(a1_ft, 1)

            def a1_project(it):
                pe.wait_ge(a1_ftc, it + 1)
                pe.matmul(bank[7][:, 3 * P:], feats1T[:, :], a1w[:, 4, :], start=True, stop=False)
                pe.matmul(bank[7][:, 3 * P:], ones[0:1, :], a1rows[:, 2, :], start=False, stop=True).then_inc(a1_o, 1)

            def a1_turn(it, first):
                for n in range(16):
                    a1_scores(it, n, first)
                    if n >= 2:
                        a1_turn_t(it, n - 2)
                    elif not first:
                        a1_turn_t(it - 1, 14 + n)
                    if not first:
                        if n == 3:
                            a1_values(it - 1, 1)
                        if n == 4:
                            a1_back(it - 1, 1)
                        if n == 6:
                            a1_feats(it - 1)
                        if n == 8:
                            a1_project(it - 1)
                    if n == 11:
                        a1_values(it, 0)
                    if n == 13:
                        a1_back(it, 0)

            a1_turn(0, True)
            with pe.Fori(1, NT) as it:
                a1_turn(it, False)
            it = NT - 1
            a1_turn_t(it, 14)
            a1_turn_t(it, 15)
            a1_values(it, 1)
            a1_back(it, 1)
            a1_feats(it)
            a1_project(it)

            norm_layer(X1)
            for b in range(B):
                pe.wait_ge(ln_out, X1 * B + b + 1)
                pe.matmul(bank[b][:, :], x1w[:, 0, :], hT[:, b * SEQ:(b + 1) * SEQ], start=True, stop=True).then_inc(x1_q, 1)
            pe.wait_ge(x1_qc, 4)
            def x1_turn(b, first):
                pe.wait_ge(x1_staged, b + 1)
                if not first:
                    pe.wait_ge(x1_x, b * QT)
                for t in range(QT):
                    mm = pe.matmul(bank[0][:, t * LK:(t + 1) * LK], hst[:, t * P:(t + 1) * P], k1T[:, ds(b * LK, LK)], start=True, stop=True)
                mm.then_inc(x1_s, 1)
                pe.wait_ge(x1_exp, b + 1)
                for t in range(QT):
                    mm = pe.transpose(bank[4][0:LK, t * P:(t + 1) * P], prob0[:, t * LK:(t + 1) * LK], ident)
                mm.then_inc(x1_t, 1)
                pe.wait_ge(x1_tc, b + 1)
                for t in range(QT):
                    mm = pe.matmul(bank[5][:, t * D:(t + 1) * D], prob0T[0:LK, 0, t * P:(t + 1) * P],
                                   vx1[:, ds(b, 1), :].rearrange("p b d -> p (b d)"), start=True, stop=True)
                mm.then_inc(x1_pv, 1)

            x1_turn(0, True)
            with pe.Fori(1, B) as b:
                x1_turn(b, False)

            norm_layer(F1)
            router(F1, gw1[:, :], E1)
            pe.wait_ge(g_chain, 300)
            feed_forward(1, E1)

        @block.vector
        def _(dve):
            steps = [0]

            def ln(ins):
                steps[0] += 1
                ins.then_inc(ln_step, 1)
                dve.wait_ge(ln_step, steps[0])

            def norm_layer(layer):
                for b in range(B):
                    xb = X[:, b * QT:(b + 1) * QT, :]
                    ln(dve.tensor_reduce(ln_mean[:, :], xb, AX.X, ALU.add))
                    ln(dve.tensor_scalar(ln_mean[:, :], ln_mean[:, :], 1.0 / D, None, ALU.mult))
                    ln(dve.tensor_tensor(xc[:, :, :], xb, bcast(ln_mean[:, :], 2, D), ALU.subtract))
                    ln(dve.tensor_tensor(xsq[:, :, :], xc[:, :, :], xc[:, :, :], ALU.mult))
                    ln(dve.tensor_reduce(ln_var[:, :], xsq[:, :, :], AX.X, ALU.add))
                    dve.tensor_scalar(ln_var[:, :], ln_var[:, :], 1.0 / D, EPS, ALU.mult, ALU.add).then_inc(ln_var_ok, 1)
                    dve.wait_ge(ln_std_ok, layer * B + b + 1)
                    ln(dve.reciprocal(ln_rstd[:, :], ln_std[:, :]))
                    ln(dve.tensor_tensor(ln_new[:, :], ln_rstd[:, :], ln_rstd[:, :], ALU.mult))
                    ln(dve.tensor_tensor(ln_new[:, :], ln_new[:, :], ln_var[:, :], ALU.mult))
                    ln(dve.tensor_scalar(ln_new[:, :], ln_new[:, :], -0.5, 1.5, ALU.mult, ALU.add))
                    ln(dve.tensor_tensor(ln_rstd[:, :], ln_rstd[:, :], ln_new[:, :], ALU.mult))
                    dve.tensor_tensor(ln_h[:, b * QT:(b + 1) * QT, :], xc[:, :, :], bcast(ln_rstd[:, :], 2, D), ALU.mult).then_inc(ln_ready, 1)

            dve.wait_ge(ld_x, 16)
            norm_layer(A0)
            dve.wait_ge(ld_x0, 128)
            dve.tensor_scalar(maskrow[:, :], mask8[:, :], -1.0, 1e38, ALU.add, ALU.mult).then_inc(pre_dve, 1)
            dve.wait_ge(ld_cst, 16)
            kc = bcast(cst[:, C_CK:C_CK + LK], 1, B)
            ks = bcast(cst[:, C_SK:C_SK + LK], 1, B)
            for i, (o, tab) in enumerate(((krope, kc), (krope2, ks))):
                dve.wait_ge(pre_mm, i + 1)
                dve.scalar_tensor_tensor(o[:, :, :], bank[i][:, 0:B * LK].rearrange("p (b k) -> p b k", b=B),
                                         x0b[:, 2 + i:3 + i], tab, ALU.add, ALU.mult).then_inc(pre_dve, 1)
            dve.wait_ge(pre_dve, 3)
            dve.tensor_tensor(krope[:, :, :], krope[:, :, :], krope2[:, :, :], ALU.add).then_inc(pre_dve, 1)

            def a0_copy(g, h, kt):
                dve.wait_ge(a0_t, g * 8 + h * 4 + kt + 1)
                dve.tensor_copy(probT[h][:, kt, :], bank[4 + kt % 2][:, :]).then_inc(a0_tc, 1)

            def a0_normalise(g, h, o):
                dve.wait_ge(a0_exp, g * 8 + h * 4 + 4)
                dve.reciprocal(rden[:, h, :], den[:, h * QT:(h + 1) * QT]).then_inc(a0_rd, 1)
                dve.wait_ge(a0_rd, g * 2 + h + 1)
                dve.wait_ge(a0_pv, g * 2 + h + 1)
                dve.tensor_tensor(feats[:, :, h * DK:(h + 1) * DK], o[:, 0:QT * DK].rearrange("p (a b) -> p a b", b=DK),
                                  bcast(rden[:, h, :], 2, DK), ALU.mult).then_inc(a0_norm, 1)

            def a0_maximum(g, h, j):
                dve.wait_ge(a0_s, g * 8 + h * 4 + j + 1)
                dve.tensor_reduce(negmax[:, h * QT + j:h * QT + j + 1], bank[j][:, :], AX.X, ALU.max, negate=True).then_inc(a0_max, 1)

            def a0_feats(g):
                dve.wait_ge(a0_ft, g + 1)
                dve.tensor_copy(featsT[:, :], bank[6][:, :]).then_inc(a0_ftc, 1)

            def a0_add(g):
                dve.wait_ge(a0_o, g + 1)
                xb = X[:, ds((g // HP) * QT, QT), :]
                dve.tensor_tensor(xb, xb, bank[7][:, :].rearrange("p (a b) -> p a b", b=P), ALU.add).then_inc(a0_x, 1)

            def a0_turn(g, first):
                if not first:
                    a0_copy(g - 1, 1, 2)
                    a0_copy(g - 1, 1, 3)
                    a0_normalise(g - 1, 1, bank[7])
                for j in range(QT):
                    a0_maximum(g, 0, j)
                if not first:
                    a0_feats(g - 1)
                a0_copy(g, 0, 0)
                a0_copy(g, 0, 1)
                if not first:
                    a0_add(g - 1)
                a0_maximum(g, 1, 0)
                a0_copy(g, 0, 2)
                a0_maximum(g, 1, 1)
                a0_copy(g, 0, 3)
                a0_maximum(g, 1, 2)
                a0_maximum(g, 1, 3)
                a0_normalise(g, 0, bank[6])
                a0_copy(g, 1, 0)
                a0_copy(g, 1, 1)

            a0_turn(0, True)
            with dve.Fori(1, B * HP) as g:
                a0_turn(g, False)
            last = B * HP - 1
            a0_copy(last, 1, 2)
            a0_copy(last, 1, 3)
            a0_normalise(last, 1, bank[7])
            a0_feats(last)
            a0_add(last)
            dve.wait_ge(a0_x, B * HP)

            norm_layer(X0)
            for b in range(B):
                dve.wait_ge(x0_q, b + 1)
                qb = big_q[:, b * SEQ:(b + 1) * SEQ]
                dve.scalar_tensor_tensor(qb, bank[2 * (b % 2)][:, :], x0b[:, 0:1], cst[:, C_CQ:C_CQ + SEQ], ALU.add, ALU.mult)
                if b:
                    dve.wait_ge(x0_qr, b)
                ln(dve.scalar_tensor_tensor(qrope2[:, :], bank[2 * (b % 2) + 1][:, :], x0b[:, 1:2], cst[:, C_SQ:C_SQ + SEQ], ALU.add, ALU.mult))
                dve.tensor_tensor(qb, qb, qrope2[:, :], ALU.add).then_inc(x0_qr, 1)
            HS = (0, 6, 12, 16)

            def x0_shift(t, first):
                for i in range(3):
                    n = HS[i + 1] - HS[i]
                    s = bank[i][:, 0:n * LK].rearrange("p (h k) -> p h k", k=LK)
                    dve.wait_ge(x0_s, t * 3 + i + 1)
                    dve.tensor_reduce(mx0[:, HS[i]:HS[i + 1]], s, AX.X, ALU.max).then_inc(x0_max, 1)
                    dve.wait_ge(x0_max, t * 3 + i + 1)
                    if not first and i == 0:
                        dve.wait_ge(x0_exp, t)
                    dve.tensor_tensor(shifted0[:, HS[i] * LK:HS[i + 1] * LK].rearrange("p (h k) -> p h k", k=LK), s,
                                      bcast(mx0[:, HS[i]:HS[i + 1]], 2, LK), ALU.subtract).then_inc(x0_sub, 1)

            def x0_rest(t):
                for c in (0, 2):
                    dve.wait_ge(x0_t, t * 4 + c + 1)
                    dve.tensor_copy(prob0T[0:LK, c, :], bank[4][0:LK, :]).then_inc(x0_tcd, 1)
                dve.wait_ge(x0_pv, t + 1)
                o = bank[6][:, 0:H * (HD + 1)].rearrange("p (h d) -> p h d", h=H)
                dve.reciprocal(rd0[:, :].unsqueeze(2), o[:, :, HD:HD + 1]).then_inc(x0_rd, 1)
                dve.wait_ge(x0_rd, t + 1)
                dve.tensor_tensor(f0[:, :].rearrange("p (h d) -> p h d", h=H), o[:, :, 0:HD], bcast(rd0[:, :], 2, HD),
                                  ALU.mult).then_inc(x0_norm, 1)
                dve.wait_ge(x0_ft, t + 1)
                dve.tensor_copy(f0T[:, :], bank[7][:, 0:P]).then_inc(x0_ftc, 1)
                dve.wait_ge(x0_o, t + 1)
                xt = X[:, ds(t, 1), :].rearrange("p a d -> p (a d)")
                dve.tensor_tensor(xt, xt, bank[3][:, 0:D], ALU.add).then_inc(x0_x, 1)

            x0_shift(0, True)
            with dve.Fori(1, NT) as t:
                x0_shift(t, False)
                x0_rest(t - 1)
            x0_rest(NT - 1)
            dve.wait_ge(x0_x, NT)

            chain = [0]

            def link(ins):
                chain[0] += 1
                ins.then_inc(g_chain, 1)
                dve.wait_ge(g_chain, chain[0])

            def upto(n):
                ins_left = n - chain[0]
                chain[0] = n
                return ins_left

            def softmax_scores(n, mm, exp_turn):
                lg, t1, t2, sc = (x[:, :, 0:n] for x in (g_lg, g_t1, g_t2, g_sc))
                dve.wait_ge(g_mm, mm)
                link(dve.tensor_copy(lg, bank[0][:, 0:NT * n].rearrange("p (t e) -> p t e", e=n)))
                link(dve.tensor_reduce(g_mx[:, :], lg, AX.X, ALU.max))
                dve.tensor_tensor(t1, lg, bcast(g_mx[:, :], 2, n), ALU.subtract).then_inc(g_exp, 1)
                dve.wait_ge(g_exp, exp_turn)
                link(dve.tensor_reduce(g_mx[:, :], t2, AX.X, ALU.add))
                link(dve.reciprocal(g_mx[:, :], g_mx[:, :]))
                link(dve.tensor_tensor(sc, t2, bcast(g_mx[:, :], 2, n), ALU.mult))

            def first_largest(n, score, best, onehot):
                t1 = g_t1[:, :, 0:n]
                io = bcast(iota[:, 0:n], 1, NT)
                link(dve.tensor_reduce(best[:, :], score, AX.X, ALU.max))
                link(dve.tensor_tensor(t1, score, bcast(best[:, :], 2, n), ALU.is_equal))
                link(dve.tensor_scalar(t1, t1, -64.0, 64.0, ALU.mult, ALU.add))
                link(dve.tensor_tensor(t1, t1, io, ALU.add))
                link(dve.tensor_reduce(g_mx[:, :], t1, AX.X, ALU.min))
                link(dve.tensor_tensor(onehot, io, bcast(g_mx[:, :], 2, n), ALU.is_equal))

            def top_two(n):
                sc, t2, oh1, oh2 = (x[:, :, 0:n] for x in (g_sc, g_t2, g_oh1, g_oh2))
                first_largest(n, sc, g_m1, oh1)
                link(dve.scalar_tensor_tensor(t2, oh1, -1e30, sc, ALU.mult, ALU.add))
                first_largest(n, t2, g_m2, oh2)

            def count_at_least(edge, into, inc):
                inc(dve.tensor_tensor(into, g_wm[:, :, :], bcast(edge, 1, NT), ALU.is_ge))
                return dve.tensor_reduce(g_cnt[:, :], into.rearrange("p t e -> p e t"), AX.X, ALU.add)

            def feed_forward(f, n):
                s = ffs[f]

                def add(i, k):
                    dve.wait_ge(s["y"], i * 8 + k + 1)
                    for t in range(QT):
                        tt = (k % 4) * QT + t
                        ins = dve.scalar_tensor_tensor(
                            X[:, tt, :], bank[4 + k % 2][:, t * P:(t + 1) * P],
                            G[:, tt, ds(i * 2 + k // 4, 1)], X[:, tt, :], ALU.mult, ALU.add)
                    ins.then_inc(s["acc"], 1)

                with dve.Fori(0, n // 2) as i:
                    for k in range(8):
                        for hf in range(2):
                            u = 2 * k + hf
                            dve.wait_ge(s["silu"], i * 16 + u + 1)
                            dve.tensor_tensor(hid[:, k % 2, hf, :], bank[2 * (u % 2) + 1][:, :], silu[:, u % 2, :],
                                              ALU.mult).then_inc(s["hid"], 1)
                        if k >= 1:
                            add(i, k - 1)
                    add(i, 7)
                dve.wait_ge(s["acc"], n * 4)

            norm_layer(F0)
            dve.wait_ge(ld_f0, 160)
            softmax_scores(E0, 1, 2)
            link(dve.tensor_tensor(g_sc[:, :, :], g_sc[:, :, :], bcast(gb0[:, :], 1, NT), ALU.add))
            top_two(E0)
            link(dve.tensor_tensor(g_oh1[:, :, :], g_oh1[:, :, :], g_oh2[:, :, :], ALU.add))
            link(dve.tensor_tensor(g_t1[:, :, :], g_lg[:, :, :], g_oh1[:, :, :], ALU.mult))
            link(dve.tensor_scalar(g_t2[:, :, :], g_oh1[:, :, :], -1.0, 1e30, ALU.add, ALU.mult))
            link(dve.tensor_tensor(g_wm[:, :, :], g_t1[:, :, :], g_t2[:, :, :], ALU.add))
            dve.tensor_reduce(g_abs[:, :], g_lg[:, :, :], AX.XY, ALU.max, apply_absolute_value=True).then_inc(g_pool, 1)
            dve.wait_ge(g_pool, 2)
            link(dve.tensor_scalar(g_step[:, :], g_all[:, :], 1e-20, None, ALU.max))
            link(dve.memset(g_lo[:, :], 0.0))
            link(dve.tensor_scalar(g_lo[:, :], g_lo[:, :], g_step[:, 0:1], None, ALU.subtract))
            with dve.Fori(0, BISECT) as i:
                def blink(k):
                    def inc(ins):
                        ins.then_inc(b_chain, 1)
                        dve.wait_ge(b_chain, i * 5 + k)
                    return inc
                blink(1)(dve.tensor_scalar(g_try[:, :], g_lo[:, :], g_step[:, 0:1], None, ALU.add))
                blink(3)(count_at_least(g_try[:, :], g_t1[:, :, :], blink(2)))
                dve.wait_ge(b_cnt, i + 1)
                blink(4)(dve.tensor_scalar(g_inc[:, :], bank[1][:, 0:E0], CAP - 0.5, g_step[:, 0:1], ALU.is_ge, ALU.mult))
                dve.tensor_scalar(g_step[:, :], g_step[:, :], 0.5, None, ALU.mult)
                blink(5)(dve.tensor_tensor(g_lo[:, :], g_lo[:, :], g_inc[:, :], ALU.add))
            link(dve.tensor_scalar(g_step[:, :], g_step[:, :], 2.0, None, ALU.mult))
            link(dve.tensor_scalar(g_try[:, :], g_lo[:, :], g_step[:, 0:1], None, ALU.add))
            link(dve.tensor_tensor(g_t1[:, :, :], g_wm[:, :, :], bcast(g_lo[:, :], 1, NT), ALU.is_ge))
            link(count_at_least(g_try[:, :], g_t2[:, :, :], link))
            left = upto(100)
            dve.tensor_tensor(g_t1[:, :, :], g_t1[:, :, :], g_t2[:, :, :], ALU.subtract).then_inc(g_chain, left)
            dve.wait_ge(g_mm, 2)
            link(dve.tensor_scalar(g_inc[:, :], bank[1][:, 0:E0], -1.0, float(CAP), ALU.mult, ALU.add))
            tot = bank[3][:, 0:NT * E0].rearrange("p (t e) -> p t e", e=E0)
            link(dve.memset(g_sc[:, 0, :], 0.0))
            for t in range(1, NT):
                link(dve.tensor_tensor(g_sc[:, t, :], g_sc[:, t - 1, :], tot[:, t - 1, :], ALU.add))
            link(dve.tensor_tensor(g_sc[:, :, :], g_sc[:, :, :], bank[2][:, 0:NT * E0].rearrange("p (t e) -> p t e", e=E0), ALU.add))
            link(dve.tensor_tensor(g_sc[:, :, :], g_sc[:, :, :], bcast(g_inc[:, :], 1, NT), ALU.is_lt))
            link(dve.tensor_tensor(g_sc[:, :, :], g_sc[:, :, :], g_t1[:, :, :], ALU.mult))
            link(dve.tensor_tensor(g_sc[:, :, :], g_sc[:, :, :], g_t2[:, :, :], ALU.add))
            left = upto(200)
            dve.wait_ge(setup, 4)
            dve.tensor_tensor(G[:, :, 0:E0], g_sc[:, :, :], g_lg[:, :, :], ALU.mult).then_inc(g_chain, left)
            dve.wait_ge(g_chain, 200)
            feed_forward(0, E0 + NSH)

            norm_layer(A1)
            dve.wait_ge(ld_a1, 80)
            edge = SEQ - 1 - LEFT
            dve.tensor_copy(embpad[:, 0:edge], emb[:, 0:1].broadcast_to([HD, edge])).then_inc(a1_pre_dve, 1)
            dve.tensor_copy(embpad[:, edge:edge + NPOS], emb[:, :]).then_inc(a1_pre_dve, 1)
            dve.tensor_copy(embpad[:, edge + NPOS:], emb[:, NPOS - 1:NPOS].broadcast_to([HD, 2 * SEQ - 1 - edge - NPOS])).then_inc(a1_pre_dve, 1)
            dve.tensor_scalar(a1bs[:, :], a1b[:, 0:1], SCALE1, None, ALU.mult).then_inc(a1_pre_dve, 1)
            for b in range(B):
                dve.wait_ge(a1_pre_mm, B + b + 1)
                dve.tensor_scalar(a1_k[:, b * SEQ:(b + 1) * SEQ], bank[4 + b][:, :], a1b[:, 1:2], None, ALU.add).then_inc(a1_pre_dve, 1)
            dve.wait_ge(ln_tp, (A1 + 1) * B)
            for b in range(B):
                dve.wait_ge(a1_pre_mm, 3 * B + b + 1)
                dve.tensor_copy(v1[:, b * QT:(b + 1) * QT, :], bank[4 + b][:, :].rearrange("p (t d) -> p t d", d=D)).then_inc(a1_pre_dve, 1)

            def a1_maximum(it, n):
                dve.wait_ge(a1_s, it * 16 + n + 1)
                dve.tensor_reduce(negmax[:, n % 8:n % 8 + 1], bank[n % 4][:, :], AX.X, ALU.max, negate=True).then_inc(a1_max, 1)

            def a1_copy(it, n):
                dve.wait_ge(a1_t, it * 16 + n + 1)
                hg, lg = n // 8, n % 8
                dve.tensor_copy(probTh[hg][:, :, :, lg * LG:(lg + 1) * LG].rearrange("p k h l -> p k l h"),
                                bank[4 + n % 2][:, :].rearrange("p (k l h) -> p k l h", k=QT, l=LG)).then_inc(a1_tc, 1)

            def a1_out(it, hg):
                dve.wait_ge(a1_pv, it * 2 + hg + 1)
                dve.tensor_copy(osb[:, :, :], bank[6][:, 0:2 * P].rearrange("p (g l) -> p g l", g=2)).then_inc(a1_oc, 1)

            def a1_normalise(it, hg):
                dve.wait_ge(a1_ot, it * 2 + hg + 1)
                o = bank[7][:, 0:2 * P].rearrange("p (h d) -> p h d", d=32)
                dve.reciprocal(rd1[:, :].unsqueeze(2), o[:, :, HD:HD + 1]).then_inc(a1_rd, 1)
                dve.wait_ge(a1_rd, it * 2 + hg + 1)
                dve.tensor_tensor(feats1[:, hg * HG * HD:(hg + 1) * HG * HD].rearrange("p (h d) -> p h d", d=HD), o[:, :, 0:HD],
                                  bcast(rd1[:, :], 2, HD), ALU.mult).then_inc(a1_norm, 1)

            def a1_feats(it):
                dve.wait_ge(a1_ft, it + 1)
                dve.tensor_copy(feats1T[:, :], bank[7][:, 2 * P:3 * P]).then_inc(a1_ftc, 1)

            def a1_add(it):
                dve.wait_ge(a1_o, it + 1)
                xt = X[:, ds(it, 1), :].rearrange("p a d -> p (a d)")
                dve.tensor_tensor(xt, xt, bank[7][:, 3 * P:], ALU.add).then_inc(a1_x, 1)

            def a1_turn(it, first):
                for n in range(16):
                    a1_maximum(it, n)
                    if n >= 2:
                        a1_copy(it, n - 2)
                    elif not first:
                        a1_copy(it - 1, 14 + n)
                    if not first:
                        if n == 3:
                            a1_out(it - 1, 1)
                        if n == 4:
                            a1_normalise(it - 1, 1)
                        if n == 6:
                            a1_feats(it - 1)
                        if n == 8:
                            a1_add(it - 1)
                    if n == 11:
                        a1_out(it, 0)
                    if n == 13:
                        a1_normalise(it, 0)

            a1_turn(0, True)
            with dve.Fori(1, NT) as it:
                a1_turn(it, False)
            it = NT - 1
            a1_copy(it, 14)
            a1_copy(it, 15)
            a1_out(it, 1)
            a1_normalise(it, 1)
            a1_feats(it)
            a1_add(it)
            dve.wait_ge(a1_x, NT)

            norm_layer(X1)
            with dve.Fori(0, B) as b:
                s = bank[0][:, 0:QT * LK].rearrange("p (t k) -> p t k", k=LK)
                p3 = prob0[:, 0:QT * LK].rearrange("p (t k) -> p t k", k=LK)
                dve.wait_ge(x1_s, b + 1)
                dve.tensor_reduce(negmax[:, 0:QT], s, AX.X, ALU.max).then_inc(x1_max, 1)
                dve.wait_ge(x1_max, b + 1)
                dve.tensor_tensor(shifted0[:, 0:QT * LK].rearrange("p (t k) -> p t k", k=LK), s,
                                  bcast(negmax[:, 0:QT], 2, LK), ALU.subtract).then_inc(x1_sub, 1)
                dve.wait_ge(x1_exp, b + 1)
                dve.tensor_reduce(den[:, 0:QT], p3, AX.X, ALU.add).then_inc(x1_den, 1)
                dve.wait_ge(x1_den, b * 2 + 1)
                dve.reciprocal(den[:, 0:QT], den[:, 0:QT]).then_inc(x1_den, 1)
                dve.wait_ge(x1_den, b * 2 + 2)
                dve.wait_ge(x1_pv, b + 1)
                for t in range(QT):
                    xt = X[:, ds(b * QT + t, 1), :].rearrange("p a d -> p (a d)")
                    dve.scalar_tensor_tensor(xt, bank[5][:, t * D:(t + 1) * D], den[:, t:t + 1], xt, ALU.mult, ALU.add).then_inc(x1_x, 1)
            dve.wait_ge(x1_x, NT)

            norm_layer(F1)
            softmax_scores(E1, 3, 4)
            top_two(E1)
            dve.tensor_tensor(g_m2[:, :], g_m2[:, :], g_m1[:, :], ALU.subtract).then_inc(g_exp, 1)
            dve.wait_ge(g_exp, 6)
            link(dve.tensor_scalar(g_m1[:, :], g_m1[:, :], 1.0, None, ALU.add))
            link(dve.reciprocal(g_m1[:, :], g_m1[:, :]))
            link(dve.tensor_scalar(g_m2[:, :], g_m1[:, :], -1.0, 1.0, ALU.mult, ALU.add))
            link(dve.tensor_tensor(g_t1[:, :, 0:E1], g_oh1[:, :, 0:E1], bcast(g_m1[:, :], 2, E1), ALU.mult))
            link(dve.tensor_tensor(g_t2[:, :, 0:E1], g_oh2[:, :, 0:E1], bcast(g_m2[:, :], 2, E1), ALU.mult))
            left = upto(300)
            dve.tensor_tensor(G[:, :, 0:E1], g_t1[:, :, 0:E1], g_t2[:, :, 0:E1], ALU.add).then_inc(g_chain, left)
            dve.wait_ge(g_chain, 300)
            feed_forward(1, E1)


def kernel(**inputs):
    import concourse.bacc as _bacc
    from concourse.bass_utils import run_bass_kernel_spmd as _run

    i = {k: np.asarray(v) for k, v in inputs.items()}

    def swap(w):
        return w.reshape(w.shape[:-1] + (D // 2, 2))[..., ::-1].reshape(w.shape)

    def dh(w):
        return w.reshape(w.shape[:-1] + (H, HD)).swapaxes(-1, -2).reshape(w.shape)

    def heads(w):
        return w.transpose(1, 0, 2).reshape(D, H * DK)

    kv, bkv = i["L0_xattn_Wkv"], i["L0_xattn_bkv"]
    wk, wv, bk, bv = kv[:, :D], kv[:, D:], bkv[:D], bkv[D:]
    wq0, bq0 = i["L0_xattn_Wq"], i["L0_xattn_bq"]
    arrays = {
        "x": i["x"].reshape(TOK, D),
        "cst": shape_constants(),
        "wq": heads(i["L0_attn_wq"]), "wk": heads(i["L0_attn_wk"]), "wv": heads(i["L0_attn_wv"]), "wo": i["L0_attn_wo"],
        "ctxT": i["ctx_1024"].reshape(B * LK, D).T,
        "mask": i["mask_BxS2_bf1"].reshape(1, B * LK).view(np.uint8),
        "x0w": np.stack([wq0, swap(wq0), wk, swap(wk), wv, i["L0_xattn_Wo"]], 1),
        "x0b": np.stack([bq0, swap(bq0), bk, swap(bk)], 1),
        "x0rows": np.stack([bv, i["L0_xattn_bo"]], 0)[None],
        "x1w": np.stack([i["L1_xattn_Wq"], i["L1_xattn_Wk"], i["L1_xattn_Wv"]], 1),
        "x1b": np.stack([i["L1_xattn_bq"], i["L1_xattn_bk"]], 1),
        "x1rows": i["L1_xattn_bv"][None],
        "gw0": i["L0_ffn_gate_w"], "gb0": i["L0_ffn_gate_b"],
        "ew1": i["L0_ffn_ew1"], "ew3": i["L0_ffn_ew3"], "ew2": i["L0_ffn_ew2"],
        "sw1": i["L0_ffn_sw1"], "sw3": i["L0_ffn_sw3"], "sw2": i["L0_ffn_sw2"],
        "a1w": np.stack([i["L1_attn_Wq"].T, dh(i["L1_attn_Wq"].T), i["L1_attn_Wk"].T, i["L1_attn_Wv"].T, i["L1_attn_Wo"].T], 1),
        "a1b": np.stack([i["L1_attn_bq"], i["L1_attn_bk"]], 1),
        "a1rows": np.stack([dh(i["L1_attn_bq"]), i["L1_attn_bv"], i["L1_attn_bo"]], 0)[None],
        "emb": i["L1_attn_dist_emb"].T,
        "gw1": i["L1_ffn_kernel_router_DE"],
        "f1g": i["L1_ffn_kernel_gating_EDF"], "f1u": i["L1_ffn_kernel_up_EDF"], "f1d": i["L1_ffn_kernel_down_EFD"],
    }
    nc = _bacc.Bacc("TRN2", target_bir_lowering=False, num_devices=1)
    feed, aps = {}, {}
    for name, v in arrays.items():
        v = np.ascontiguousarray(v)
        feed[f"in_{name}"] = v
        aps[name] = nc.dram_tensor(f"in_{name}", v.shape, mybir.dt.from_np(v.dtype), kind="ExternalInput").ap()
    out = nc.dram_tensor("out", (TOK, D), F32, kind="ExternalOutput").ap()
    decoder_kernel(nc, aps, out)
    r = _run(nc, [feed], core_ids=[0])
    return r.results[0]["out"].reshape(B, SEQ, D)
```

```python
from contextlib import ExitStack

import numpy as np

import concourse.bass as bass
from concourse import mybir
from concourse.bass import ds

F32 = mybir.dt.float32
BF16 = mybir.dt.bfloat16
U8 = mybir.dt.uint8
U32 = mybir.dt.uint32
ALU = mybir.AluOpType
ACT = mybir.ActivationFunctionType
AX = mybir.AxisListType
RMAX = bass.bass_isa.ReduceOp.max

P = 128
B, SEQ, D = 4, 512, 128
TOK = B * SEQ
NT = TOK // P
QT = SEQ // P
LK = 77
H = 16
DK = 64
HP = H // 2
HD = D // H
E0, E1 = 16, 8
NSH = 2
FF = 256
CAP = -(-TOK * 2 // E0 * 5 // 4)
LEFT, RIGHT = 64, 8
NPOS = LEFT + RIGHT + 1
LG = 16
HG = 8
EPS = 1e-5
BISECT = 30
BSTEPS = 5
ET = -(-CAP // P)
PITCH = ET * P
ROWS = E0 * PITCH
OFF = SEQ - LG
WIN = P + LEFT + 2 * RIGHT
WLAST = SEQ - WIN

C_ID = 0
C_MH = C_ID + P
C_DL = C_MH + H
C_IO = C_DL + LG
C_TRI = C_IO + E0
C_CQ = C_TRI + P
C_SQ = C_CQ + SEQ
C_CK = C_SQ + SEQ
C_SK = C_CK + LK
C_BLK = C_SK + LK
C_N = C_BLK + P


def shape_constants():
    c = np.zeros((P, C_N), np.float32)
    p = np.arange(P)
    c[:, C_ID:C_ID + P] = np.eye(P)
    c[p, C_MH + p // HD] = 1.0
    c[p, C_DL + p // HD] = 1.0
    c[:, C_IO:C_IO + E0] = np.arange(E0)
    c[:, C_TRI:C_TRI + P] = np.triu(np.ones((P, P)), 1)
    c[:, C_BLK:C_BLK + P] = (p[:, None] % E0) == (p[None, :] % E0)
    inv = (1.0 / 10000.0 ** (np.arange(0, HD, 2, dtype=np.float32) / HD)).astype(np.float32)
    sign = np.where(p % 2 == 0, -1.0, 1.0)[:, None]
    for n, at_c, at_s, scale in ((SEQ, C_CQ, C_SQ, 64 ** -0.5), (LK, C_CK, C_SK, 1.0)):
        pos = (np.float32(10.0) * (np.arange(n, dtype=np.float32) / np.float32(n))).astype(np.float32)
        ang = (pos[None, :] * inv[(p % HD) // 2][:, None]).astype(np.float32)
        c[:, at_c:at_c + n] = np.cos(ang) * scale
        c[:, at_s:at_s + n] = np.sin(ang) * sign * scale
    return c


def bcast(ap, axis, n):
    a = ap.unsqueeze(axis)
    shape = list(a.shape)
    shape[axis] = n
    return a.broadcast_to(shape)


def window(t):
    return (t * 3 // 2) * LEFT + (t // (QT - 1)) * (WLAST - (3 * (QT - 1) // 2) * LEFT)


assert all(window(t) <= max(0, P * t - LEFT + 1) and min(SEQ, P * t + P + RIGHT - 1) <= window(t) + WIN <= SEQ for t in range(QT))


def decoder_kernel(nc, a, out):
    ctx = ExitStack()
    with ctx:
        def sb(name, shape, dt=F32):
            return ctx.enter_context(nc.sbuf_tensor(name, shape, dt))

        def sem(name):
            return ctx.enter_context(nc.semaphore(name))

        bank = [ctx.enter_context(nc.psum_tensor(f"bank{i}", [P, 512], F32)) for i in range(8)]
        xs_rows = nc.dram_tensor("xs_rows", (ROWS, D), F32, kind="Internal").ap()
        ys_rows = nc.dram_tensor("ys_rows", (ROWS, D), F32, kind="Internal").ap()
        q_by_row = nc.dram_tensor("q_by_row", (TOK, D), F32, kind="Internal").ap()

        X = sb("X", [P, NT, D])
        hT = sb("hT", [P, TOK])
        cst = sb("cst", [P, C_N])
        ident = cst[:, C_ID:C_ID + P]
        headmask = cst[:, C_MH:C_MH + H]
        rowmask = cst[:, C_DL:C_DL + LG]
        iota = cst[:, C_IO:C_IO + E0]
        tri = cst[:, C_TRI:C_TRI + P]
        same_expert = cst[:, C_BLK:C_BLK + P]
        ones = sb("ones", [P, P])
        ones_bf = sb("ones_bf", [1, P], BF16)

        ln_buf = sb("ln_buf", [P, 2, QT, D])
        xc = ln_buf[:, 0, :, :]
        xsq = ln_buf[:, 1, :, :]
        ln_h = sb("ln_h", [P, NT, D])
        ln_mean = sb("ln_mean", [P, QT])
        ln_var = sb("ln_var", [P, QT])
        ln_std = sb("ln_std", [P, QT])
        ln_rstd = sb("ln_rstd", [P, QT])
        ln_new = sb("ln_new", [P, QT])

        wqkv0 = sb("wqkv0", [P, 4 * H * DK])
        wqkv = wqkv0[:, 0:3 * H * DK].rearrange("p (i n) -> p i n", i=3)
        wo0 = wqkv0[:, 3 * H * DK:].rearrange("p (c n) -> p c n", n=D)
        x0w = sb("x0w", [P, 6, D])
        x0b = sb("x0b", [P, 4])
        x0rows = sb("x0rows", [1, 2, D])
        x1w = sb("x1w", [P, 3, D])
        x1b = sb("x1b", [P, 2])
        x1rows = sb("x1rows", [1, D])
        a1w = sb("a1w", [P, 5, D])
        a1b = sb("a1b", [P, 2])
        a1bs = sb("a1bs", [P, 1])
        a1rows = sb("a1rows", [1, 3, D])
        emb = sb("emb", [HD, NPOS])
        emb_ends = sb("emb_ends", [P, 2])
        gw0 = sb("gw0", [P, E0])
        gb0 = sb("gb0", [P, E0])
        gw1 = sb("gw1", [P, E1])
        w13 = sb("w13", [P, E0 + NSH, 2, FF])
        w2 = sb("w2", [P, E0 + NSH, 2, D])
        ctxT = sb("ctxT", [P, B * LK])
        mask8 = sb("mask8", [1, B * LK], U8)
        maskrow = sb("maskrow", [1, B * LK], BF16)

        wst = sb("wst", [P, 3, P])
        hst = sb("hst", [P, SEQ])
        qT = sb("qT", [P, SEQ])
        kT = sb("kT", [P, SEQ])
        vtok = sb("vtok", [P, QT, P])
        arena = sb("arena", [P, 4, QT, SEQ])
        prob = [arena[:, i, :, :] for i in range(2)]
        probT = [arena[:, 2 + i, :, :] for i in range(2)]
        negmax = sb("negmax", [P, 2 * QT])
        den = sb("den", [P, 2 * QT])
        rden = sb("rden", [P, 2 * QT])
        featsT = sb("featsT", [P, SEQ])
        a0_p = [arena[:, 0, i, :] for i in range(QT)]
        a0_pT = [arena[:, 1 + h, :, :] for h in range(2)]
        a0_qT = [qT[:, :], arena[:, 3, 0, :]]
        a0_kT = [kT[:, :], arena[:, 3, 1, :]]
        a0_vtok = [vtok[:, :, :], arena[:, 3, 2, :].rearrange("p (a b) -> p a b", a=QT)]

        big_q = sb("big_q", [P, TOK])
        big_k = sb("big_k", [P, B, H, LK])
        big_k_flat = big_k[:, :, :, :].rearrange("p b h k -> p (b h k)")
        gathered = [t.rearrange("p (t d) -> p t d", d=D) for t in (big_q[:, :], big_k_flat[:, 0:TOK])]
        a1_k = big_k_flat[:, 0:TOK]
        a1_q2 = big_k_flat[:, TOK:2 * TOK].rearrange("p (g h) -> p g h", h=H)
        vx0 = sb("vx0", [LK, B, H, HD + 1])
        k1T = sb("k1T", [P, B * LK])
        vx1 = sb("vx1", [LK, B, D])
        krope = sb("krope", [P, B, LK])
        krope2 = sb("krope2", [P, B, LK])
        qrope2 = sb("qrope2", [P, SEQ])
        qst = sb("qst", [P, P])
        mx0 = sb("mx0", [P, H])
        rd0 = sb("rd0", [P, H])
        f0 = sb("f0", [P, D])
        f0T = sb("f0T", [P, D])
        prob0 = prob[0][:, :, :].rearrange("p a b -> p (a b)")[:, 0:H * LK]
        shifted0 = prob[1][:, :, :].rearrange("p a b -> p (a b)")[:, 0:H * LK]
        prob0T = probT[0][:, :, :]

        w13st = arena[:, 3, 0:2, :].rearrange("p e (w f) -> p e w f", w=2)
        silu = arena[:, 3, 2:4, :]
        hid = arena[:, 1, :, :].rearrange("p (u h) t -> p u h t", u=2)
        g_tiles = arena[:, 2, :, :].rearrange("p a (b t e) -> p (a b) t e", b=2, e=E0)
        G = sb("G", [P, NT, E1])
        g_w = sb("g_w", [P, 2, NT])
        g_row = sb("g_row", [P, 2, NT], U32)
        g_wmT = sb("g_wmT", [P, 2 * P])
        g_ge = sb("g_ge", [P, 2 * P])
        g_edges = sb("g_edges", [P, 2, P])
        arena0 = arena[:, 0, :, :].rearrange("p a b -> p (a b)")
        xs = arena0[:, 0:4 * PITCH].rearrange("p (i t d) -> p i t d", i=2, d=D)
        ys = wqkv0[:, 0:4 * PITCH].rearrange("p (i t d) -> p i t d", i=2, d=D)
        hs = wqkv0[:, 4 * PITCH:8 * PITCH].rearrange("p (e h n) -> p e h n", e=2, h=2)
        xsT = wqkv0[:, 8 * PITCH:8 * PITCH + 2 * CAP].rearrange("p (e n) -> p e n", e=2)
        g_lg = g_tiles[:, 0, :, :]
        g_sc = g_tiles[:, 1, :, :]
        g_t1 = g_tiles[:, 2, :, :]
        g_t2 = g_tiles[:, 3, :, :]
        g_oh1 = g_tiles[:, 4, :, :]
        g_oh2 = g_tiles[:, 5, :, :]
        g_wm = g_tiles[:, 6, :, :]
        g_rt = g_tiles[:, 7, :, :]
        g_m1 = sb("g_m1", [P, NT])
        g_m2 = sb("g_m2", [P, NT])
        g_mx = sb("g_mx", [P, NT])
        g_abs = sb("g_abs", [P, 1])
        g_all = sb("g_all", [P, 1])
        g_step = sb("g_step", [P, 1])
        g_lo = sb("g_lo", [P, 1])
        g_try = sb("g_try", [P, 1])
        g_ge_cnt = sb("g_ge_cnt", [P, 1])
        g_inc = sb("g_inc", [P, 1])
        g_elo = sb("g_elo", [P, E0])
        g_ehi = sb("g_ehi", [P, E0])
        g_cnt = sb("g_cnt", [P, E0])
        g_left = sb("g_left", [P, E0])

        spare = w13[:, E1:, :, :].rearrange("p e w f -> p (e w f)")
        embpad = spare[0:HD, 0:2 * SEQ - 1]
        relT = spare[:, 2 * SEQ:2 * SEQ + SEQ + OFF]
        vst = spare[:, 4 * SEQ:4 * SEQ + QT * H * 32].rearrange("p (k h d) -> p k h d", h=H, d=32)
        ends = spare[:, 4 * SEQ + QT * H * 32:4 * SEQ + QT * H * 32 + WLAST + SEQ]
        a1_keys = ln_buf[:, :, :, :].rearrange("p i t d -> p i (t d)")
        blocks = wqkv0[:, 0:4 * P * HG].rearrange("p (n g l h) -> p n g l h", n=4, l=LG, h=HG)
        qblk = [blocks[:, i, :, :, :] for i in range(2)]
        rblk = [blocks[:, 2 + i, :, :, :] for i in range(2)]
        v1 = ln_h
        osb = sb("osb", [P, 2, P])
        rd1 = sb("rd1", [P, HG])
        feats1 = sb("feats1", [P, D])
        feats1T = sb("feats1T", [P, D])
        qtok = prob[0][:, :, :].rearrange("p a (c d) -> p (a c) d", d=D)
        ptile = [hst[:, :], qT[:, :], kT[:, :], vtok[:, :, :].rearrange("p a b -> p (a b)")]
        probTh = [arena[:, 2 - 2 * i:4 - 2 * i, :, :].rearrange("p a b (c l) -> p (a b c) l", l=P)
                  .rearrange("p (k h) l -> p k h l", k=QT) for i in range(2)]

        ld_x, ld_cst, ld_a0, ld_x0, ld_f0, ld_a1, ld_x1, ld_f1 = (
            sem(n) for n in ("ld_x", "ld_cst", "ld_a0", "ld_x0", "ld_f0", "ld_a1", "ld_x1", "ld_f1"))
        stored = sem("stored")
        setup = sem("setup")
        ln_step, ln_var_ok, ln_std_ok, ln_ready, ln_tp, ln_out = (
            sem(n) for n in ("ln_step", "ln_var_ok", "ln_std_ok", "ln_ready", "ln_tp", "ln_out"))
        pre_mm, pre_act, pre_dve, pre_pool = (sem(n) for n in ("pre_mm", "pre_act", "pre_dve", "pre_pool"))
        a0_staged, a0_q, a0_k, a0_v, a0_s, a0_t, a0_pv, a0_o = (
            sem("a0_" + n) for n in ("staged", "q", "k", "v", "s", "t", "pv", "o"))
        a0_qc, a0_kc, a0_vc, a0_exp, a0_max, a0_rd, a0_tc, a0_norm, a0_ftc, a0_x = (
            sem("a0_" + n) for n in ("qc", "kc", "vc", "exp", "max", "rd", "tc", "norm", "ftc", "x"))
        x0_q, x0_qr, x0_staged, x0_s, x0_t, x0_pv, x0_ft, x0_o = (
            sem("x0_" + n) for n in ("q", "qr", "staged", "s", "t", "pv", "ft", "o"))
        x0_max, x0_sub, x0_exp, x0_tcd, x0_tca, x0_rd, x0_norm, x0_ftc, x0_x = (
            sem("x0_" + n) for n in ("max", "sub", "exp", "tcd", "tca", "rd", "norm", "ftc", "x"))
        g_mm, g_chain, g_exp, g_pool, b_chain, b_count, b_total = (
            sem(n) for n in ("g_mm", "g_chain", "g_exp", "g_pool", "b_chain", "b_count", "b_total"))
        zeroed, scattered, gath_zero = (sem(n) for n in ("zeroed", "scattered", "gath_zero"))
        got = [sem(f"got{b}") for b in range(B)]
        xs_in = [sem(f"xs_in{i}") for i in range(2)]
        ys_out = [sem(f"ys_out{i}") for i in range(2)]
        r_staged, r_t, r_tc, r_h, r_silu, r_hid, r_y, r_yc, r_pad = (
            sem("r_" + n) for n in ("staged", "t", "tc", "h", "silu", "hid", "y", "yc", "pad"))
        sh_h, sh_silu, sh_hid, sh_y, sh_acc, f0_x = (
            sem(n) for n in ("sh_h", "sh_silu", "sh_hid", "sh_y", "sh_acc", "f0_x"))
        ff = {n: sem(f"f1_{n}") for n in ("staged", "h", "silu", "hid", "y", "acc")}
        a1_pre_mm, a1_pre_act, a1_pre_dve, a1_qout, a1_qin, a1_rel = (
            sem("a1_" + n) for n in ("pre_mm", "pre_act", "pre_dve", "qout", "qin", "rel"))
        a1_qb, a1_vs, a1_s, a1_t, a1_pv, a1_ot, a1_ft, a1_o = (
            sem("a1_" + n) for n in ("qb", "vs", "s", "t", "pv", "ot", "ft", "o"))
        a1_max, a1_exp, a1_tcd, a1_tca, a1_oc, a1_rd, a1_norm, a1_ftc, a1_x = (
            sem("a1_" + n) for n in ("max", "exp", "tcd", "tca", "oc", "rd", "norm", "ftc", "x"))
        x1_q, x1_qc, x1_staged, x1_s, x1_max, x1_sub, x1_exp, x1_den, x1_t, x1_tc, x1_pv, x1_x = (
            sem("x1_" + n) for n in
            ("q", "qc", "staged", "s", "max", "sub", "exp", "den", "t", "tc", "pv", "x"))

        A0, X0, F0, A1, X1, F1 = range(6)
        SCALE1 = float(1.0 / np.sqrt(HD))
        SCALEX1 = float(D) ** -0.5
        LT = P // LG
        PAIRS = B * HP
        UN = 2 * QT

        block = ctx.enter_context(nc.Block())

        @block.sync
        def _(sp):
            sp.dma_start(X[:, :, :], a["x"].rearrange("(t p) d -> p t d", p=P)).then_inc(ld_x, 16)
            sp.dma_start(cst[:, :], a["cst"]).then_inc(ld_cst, 16)
            for i, n in enumerate(("wq", "wk", "wv")):
                sp.dma_start(wqkv[:, i, :], a[n]).then_inc(ld_a0, 16)
            sp.dma_start(wo0[:, :, :], a["wo"].rearrange("(c p) n -> p c n", p=P)).then_inc(ld_a0, 16)
            sp.dma_start(ctxT[:, :], a["ctxT"]).then_inc(ld_x0, 16)
            sp.dma_start(mask8[:, :], a["mask"]).then_inc(ld_x0, 16)
            sp.dma_start(x0w[:, :, :], a["x0w"]).then_inc(ld_x0, 16)
            sp.dma_start(x0b[:, :], a["x0b"]).then_inc(ld_x0, 16)
            sp.dma_start(x0rows[:, :, :], a["x0rows"]).then_inc(ld_x0, 16)
            sp.dma_start(x1w[:, :, :], a["x1w"]).then_inc(ld_x0, 16)
            sp.dma_start(x1b[:, :], a["x1b"]).then_inc(ld_x0, 16)
            sp.dma_start(x1rows[:, :], a["x1rows"]).then_inc(ld_x0, 16)
            sp.dma_start(gw0[:, :], a["gw0"]).then_inc(ld_f0, 16)
            sp.dma_start(gb0[:, :], a["gb0"].partition_broadcast(P)).then_inc(ld_f0, 16)
            sp.dma_start(w13[:, 0:E0, 0, :], a["ew1"].rearrange("e d f -> d e f")).then_inc(ld_f0, 16)
            sp.dma_start(w13[:, 0:E0, 1, :], a["ew3"].rearrange("e d f -> d e f")).then_inc(ld_f0, 16)
            sp.dma_start(w13[:, E0:, 0, :], a["sw1"].rearrange("e d f -> d e f")).then_inc(ld_f0, 16)
            sp.dma_start(w13[:, E0:, 1, :], a["sw3"].rearrange("e d f -> d e f")).then_inc(ld_f0, 16)
            for hf in range(2):
                sp.dma_start(w2[:, 0:E0, hf, :], a["ew2"][:, hf * P:(hf + 1) * P, :].rearrange("e p d -> p e d")).then_inc(ld_f0, 16)
                sp.dma_start(w2[:, E0:, hf, :], a["sw2"][:, hf * P:(hf + 1) * P, :].rearrange("e p d -> p e d")).then_inc(ld_f0, 16)
            sp.dma_start(a1w[:, :, :], a["a1w"]).then_inc(ld_a1, 16)
            sp.dma_start(a1b[:, :], a["a1b"]).then_inc(ld_a1, 16)
            sp.dma_start(a1rows[:, :, :], a["a1rows"]).then_inc(ld_a1, 16)
            sp.dma_start(emb[:, :], a["emb"]).then_inc(ld_a1, 16)
            sp.dma_start(emb_ends[:, :], a["emb_ends"]).then_inc(ld_a1, 16)
            sp.dma_start(gw1[:, :], a["gw1"]).then_inc(ld_a1, 16)
            sp.wait_ge(setup, 4)
            for i in range(ROWS * D // (P * TOK)):
                sp.dma_start(xs_rows.rearrange("(i p r) d -> i p (r d)", p=P, r=TOK // D)[i], big_q[:, :]).then_inc(zeroed, 16)
            xs_pairs = xs_rows.rearrange("(j i t p) d -> j i p t d", i=2, t=2 * ET, p=P)
            ys_pairs = ys_rows.rearrange("(j i t p) d -> j i p t d", i=2, t=2 * ET, p=P)

            def load_xs(j, i):
                sp.dma_start(xs[:, i, :, :], xs_pairs[ds(j, 1), i].rearrange("j p t d -> p (j t) d")).then_inc(xs_in[i], 16)

            def store_ys(j, i):
                sp.wait_ge(r_yc, j * 4 + i * 2 + 2)
                sp.dma_start(ys_pairs[ds(j, 1), i].rearrange("j p t d -> p (j t) d"), ys[:, i, :, :]).then_inc(ys_out[i], 16)

            sp.wait_ge(scattered, 16 * 2 * NT)
            for i in range(2):
                load_xs(0, i)
            with sp.Fori(0, E0 // 4 - 1) as j:
                for i in range(2):
                    sp.wait_ge(r_t, j * 4 + i * 2 + 2)
                    load_xs(j + 1, i)
                    store_ys(j, i)
            for i in range(2):
                store_ys(E0 // 4 - 1, i)
            sp.wait_ge(a1_pre_dve, 3)
            for l in range(LG):
                sp.dma_start(relT[l * HD:(l + 1) * HD, :],
                             embpad[:, LG - 1 - l:LG - 1 - l + SEQ + OFF]).then_inc(a1_rel, 16)
            sp.wait_ge(r_y, E0)
            sp.dma_start(w13[:, 0:E1, 0, :], a["f1g"].rearrange("e d f -> d e f")).then_inc(ld_f1, 16)
            sp.dma_start(w13[:, 0:E1, 1, :], a["f1u"].rearrange("e d f -> d e f")).then_inc(ld_f1, 16)
            for hf in range(2):
                sp.dma_start(w2[:, 0:E1, hf, :], a["f1d"][:, hf * P:(hf + 1) * P, :].rearrange("e p d -> p e d")).then_inc(ld_f1, 16)
            sp.wait_ge(a1_pre_act, 8)
            sp.dma_start(q_by_row.rearrange("(t p) n -> p t n", p=P), qtok).then_inc(a1_qout, 16)
            sp.wait_ge(a1_qout, 16)
            sp.dma_start(a1_q2, q_by_row.rearrange("(g l) (d h) -> (l d) g h", l=LG, h=H)).then_inc(a1_qin, 16)
            sp.wait_ge(ff["acc"], E1 * B)
            sp.dma_start(out.rearrange("(t p) d -> p t d", p=P), X[:, :, :]).then_inc(stored, 16)
            sp.wait_ge(stored, 16)

        @block.gpsimd
        def _(pool):
            pool.memset(ones[:, :], 1.0).then_inc(setup, 1)
            pool.memset(ones_bf[:, :], 1.0).then_inc(setup, 1)
            pool.memset(vx0[:, :, :, HD:HD + 1], 1.0).then_inc(setup, 1)
            pool.memset(big_q[:, :], 0.0).then_inc(setup, 1)
            pool.wait_ge(ld_cst, 16)
            pool.wait_ge(pre_dve, 4)
            for b in range(B):
                pool.tensor_tensor(big_k[:, b, :, :], bcast(krope[:, b, :], 1, H), bcast(headmask, 2, LK),
                                   ALU.mult).then_inc(pre_pool, 1)
            pool.wait_ge(ld_a0, 64)
            pool.wait_ge(ln_out, 4)

            def a0_stage(g):
                pool.tensor_copy(wst[:, :, :], wqkv[:, :, ds((g % HP) * P, P)]).then_inc(a0_staged, 1)
                pool.tensor_copy(hst[:, :], hT[:, ds((g // HP) * SEQ, SEQ)]).then_inc(a0_staged, 1)

            def a0_turn(g, last):
                if not last:
                    pool.wait_ge(a0_v, g + 1)
                    a0_stage(g + 1)
                for u in range(UN):
                    pool.wait_ge(a0_rd, g * UN + u + 1)
                    pool.tensor_tensor(a0_p[u % 4], a0_p[u % 4], rden[:, u:u + 1].broadcast_to([P, SEQ]), ALU.mult).then_inc(a0_norm, 1)

            a0_stage(0)
            with pool.Fori(0, PAIRS - 1) as g:
                a0_turn(g, False)
            a0_turn(PAIRS - 1, True)
            pool.wait_ge(x0_qr, 4)
            pool.tensor_copy(qst[:, :], big_q[:, 0:P]).then_inc(x0_staged, 1)
            with pool.Fori(1, NT) as t:
                pool.wait_ge(x0_s, t * 3)
                pool.tensor_copy(qst[:, :], big_q[:, ds(t * P, P)]).then_inc(x0_staged, 1)

            pool.wait_ge(g_pool, 1)
            pool.partition_all_reduce(g_all[:, :], g_abs[:, :], P, RMAX).then_inc(g_pool, 1)
            pool.wait_ge(x0_x, NT)
            for c in range(2):
                pool.memset(gathered[c], 0.0).then_inc(gath_zero, 1)
            pool.memset(hs[:, :, :, CAP:], 0.0).then_inc(r_pad, 1)
            pool.wait_ge(ld_f0, 160)
            for e in range(2):
                pool.tensor_copy(w13st[:, e, :, :], w13[:, e, :, :]).then_inc(r_staged, 1)
            pool.wait_ge(g_chain, 200)
            pool.wait_ge(zeroed, 16 * (ROWS // TOK))
            for t in range(NT):
                for c in range(2):
                    pool.indirect_dma_start(xs_rows, bass.IndirectOffsetOnAxis(ap=g_row[:, c, t:t + 1], axis=0), ln_h[:, t, :], None,
                                            bounds_check=ROWS - 1, oob_is_err=False).then_inc(scattered, 16)
            with pool.Fori(1, E0 // 2) as i:
                for e in range(2):
                    pool.wait_ge(r_h, i * 4 - 2 + e * 2)
                    pool.tensor_copy(w13st[:, e, :, :], w13[:, ds(i * 2 + e, 1), :, :].rearrange("p a b c -> p (a b) c")).then_inc(r_staged, 1)
            for i in range(2):
                pool.wait_ge(ys_out[i], 16 * E0 // 4)
            pool.wait_ge(gath_zero, 2)
            for t in range(NT):
                for c in range(2):
                    pool.indirect_dma_start(gathered[c][:, t, :], None, ys_rows, bass.IndirectOffsetOnAxis(ap=g_row[:, c, t:t + 1], axis=0),
                                            bounds_check=ROWS - 1, oob_is_err=False).then_inc(got[t // QT], 16)

            pool.wait_ge(a1_pre_act, 4)
            pool.wait_ge(a1_qin, 16)
            pool.wait_ge(a1_pre_dve, 15)
            pool.memset(vst, 0.0).then_inc(setup, 1)
            pool.wait_ge(setup, 5)
            pool.memset(vst[:, :, :, HD:HD + 1], 1.0).then_inc(setup, 1)

            def stage_a1(it, first):
                for hg in range(2):
                    if not first:
                        pool.wait_ge(a1_s, it * 16 - 8 + hg * 8)
                    if hg == 0:
                        pool.tensor_tensor(a1_keys[:, ds(it % 2, 1), :].rearrange("p i n -> p (i n)"),
                                           a1_k[:, ds((it // QT) * SEQ, SEQ)],
                                           ends[:, ds(window(it % QT) * -1 + WLAST, SEQ)], ALU.add).then_inc(a1_qb, 1)
                    pool.tensor_tensor(
                        rblk[hg][:, :, :, :],
                        bcast(a1_q2[:, ds(it * LT, LT), hg * HG:(hg + 1) * HG], 2, LG),
                        bcast(bcast(rowmask, 2, HG), 1, LT), ALU.mult).then_inc(a1_qb, 1)
                    pool.tensor_tensor(
                        qblk[hg][:, :, :, :],
                        bcast(big_q[:, ds(it * P, P)].rearrange("p (g l) -> p g l", l=LG), 3, HG),
                        bcast(bcast(headmask[:, hg * HG:(hg + 1) * HG], 1, LG), 1, LT), ALU.mult).then_inc(a1_qb, 1)
                if not first:
                    pool.wait_ge(a1_pv, it * 2)
                pool.tensor_copy(vst[:, :, :, 0:HD],
                                 v1[:, ds((it // QT) * QT, QT), :].rearrange("p a (h d) -> p a h d", d=HD)).then_inc(a1_vs, 1)

            stage_a1(0, True)
            with pool.Fori(1, NT) as it:
                stage_a1(it, False)

            pool.wait_ge(x1_qc, 4)
            pool.tensor_copy(hst[:, :], big_q[:, 0:SEQ]).then_inc(x1_staged, 1)
            with pool.Fori(1, B) as b:
                pool.wait_ge(x1_s, b)
                pool.tensor_copy(hst[:, :], big_q[:, ds(b * SEQ, SEQ)]).then_inc(x1_staged, 1)
            pool.wait_ge(ld_f1, 64)
            for e in range(2):
                pool.tensor_copy(w13st[:, e, :, :], w13[:, e, :, :]).then_inc(ff["staged"], 1)
            with pool.Fori(1, E1 // 2) as i:
                for e in range(2):
                    pool.wait_ge(ff["h"], i * 16 - 8 + e * 8)
                    pool.tensor_copy(w13st[:, e, :, :], w13[:, ds(i * 2 + e, 1), :, :].rearrange("p a b c -> p (a b) c")).then_inc(ff["staged"], 1)

        @block.scalar
        def _(act):
            def norm_layer(layer):
                for b in range(B):
                    act.wait_ge(ln_var_ok, layer * B + b + 1)
                    act.activation(ln_std[:, :], ln_var[:, :], ACT.Sqrt).then_inc(ln_std_ok, 1)
                    act.wait_ge(ln_tp, layer * B + b + 1)
                    act.activation(hT[:, b * SEQ:(b + 1) * SEQ], bank[4 + b][:, :], ACT.Copy).then_inc(ln_out, 1)

            norm_layer(A0)
            act.wait_ge(ld_x0, 128)
            act.wait_ge(pre_mm, 3)
            act.activation(k1T[:, :], bank[2][:, 0:B * LK], ACT.Identity, bias=x1b[:, 1:2]).then_inc(pre_act, 1)
            act.wait_ge(setup, 4)
            act.wait_ge(pre_mm, 4)
            act.activation(vx0[:, :, :, 0:HD], bank[3][0:LK, :].rearrange("p (b h d) -> p b h d", b=B, d=HD),
                           ACT.Copy).then_inc(pre_act, 1)
            act.wait_ge(pre_mm, 5)
            act.activation(vx1[:, :, :], bank[4][0:LK, :].rearrange("p (b d) -> p b d", b=B), ACT.Copy).then_inc(pre_act, 1)

            def a0_copy_q(g, par):
                act.wait_ge(a0_q, g + 1)
                act.activation(a0_qT[par], bank[6][:, :], ACT.Copy, scale=float(DK) ** -0.5).then_inc(a0_qc, 1)

            def a0_copy_k(g, par):
                act.wait_ge(a0_k, g + 1)
                act.activation(a0_kT[par], bank[6][:, :], ACT.Copy).then_inc(a0_kc, 1)

            def a0_copy_v(g, par):
                act.wait_ge(a0_v, g + 1)
                act.activation(a0_vtok[par], bank[6][:, :].rearrange("p (a b) -> p a b", a=QT), ACT.Copy).then_inc(a0_vc, 1)

            def a0_copy_feats(g):
                act.wait_ge(a0_pv, g + 1)
                act.activation(featsT[:, :], bank[7][:, :], ACT.Copy).then_inc(a0_ftc, 1)

            def a0_turn(g, par, first, last):
                for u in range(UN):
                    if not first and u == 4:
                        a0_copy_feats(g - 1)
                    act.wait_ge(a0_max, g * UN + u + 1)
                    if not (first and u < 4):
                        act.wait_ge(a0_t, g * UN + u - 3)
                    act.activation(a0_p[u % 4], bank[u % 4][:, :], ACT.Exp, bias=negmax[:, u:u + 1],
                                   accum_out=den[:, u:u + 1]).then_inc(a0_exp, 1)
                    if not last:
                        if u == 4:
                            a0_copy_q(g + 1, 1 - par)
                        if u == 5:
                            a0_copy_k(g + 1, 1 - par)
                        if u == 6:
                            a0_copy_v(g + 1, 1 - par)

            a0_copy_q(0, 0)
            a0_copy_k(0, 0)
            a0_copy_v(0, 0)
            a0_turn(0, 0, True, False)
            with act.Fori(0, PAIRS // 2 - 1) as i:
                a0_turn(i * 2 + 1, 1, False, False)
                a0_turn(i * 2 + 2, 0, False, False)
            a0_turn(PAIRS - 1, 1, False, True)
            a0_copy_feats(PAIRS - 1)

            norm_layer(X0)

            def x0_copies(t):
                for c in (1, 3):
                    act.wait_ge(x0_t, t * 4 + c + 1)
                    act.activation(prob0T[0:LK, c, :], bank[4 + c % 2][0:LK, :], ACT.Copy).then_inc(x0_tca, 1)

            def x0_exps(t, first):
                act.wait_ge(x0_sub, t * 3 + 3)
                if not first:
                    act.wait_ge(x0_t, t * 4)
                act.activation(prob0, shifted0, ACT.Exp).then_inc(x0_exp, 1)

            x0_exps(0, True)
            with act.Fori(1, NT) as t:
                x0_copies(t - 1)
                x0_exps(t, False)
            x0_copies(NT - 1)

            def shared_expert(s):
                for u in range(s * 8, s * 8 + 8):
                    act.wait_ge(sh_h, u + 1)
                    if u >= 2:
                        act.wait_ge(sh_hid, u - 1)
                    act.activation(silu[:, u % 2, :], bank[2 * (u % 2)][:, :], ACT.Silu).then_inc(sh_silu, 1)

            def routed_silu(e):
                for hf in range(2):
                    act.wait_ge(r_h, e * 2 + hf + 1)
                    act.activation(silu[:, hf, 0:CAP], bank[2 * hf][:, 0:CAP], ACT.Silu).then_inc(r_silu, 1)

            def routed_y(j, k):
                act.wait_ge(r_y, j * 4 + k + 1)
                act.activation(ys[:, k // 2, (k % 2) * ET:(k % 2 + 1) * ET, :],
                               bank[6 + k % 2][:, 0:PITCH].rearrange("p (t d) -> p t d", d=D), ACT.Copy).then_inc(r_yc, 1)

            def routed_turn(j, first):
                for k in range(4):
                    routed_silu(j * 4 + k)
                    if k:
                        routed_y(j, k - 1)
                    if k in (0, 2) and not first:
                        act.wait_ge(ys_out[k // 2], j * 16)
                routed_y(j, 3)

            norm_layer(F0)
            act.wait_ge(g_exp, 1)
            act.activation(g_t2[:, :, :], g_t1[:, :, :], ACT.Exp).then_inc(g_exp, 1)
            shared_expert(0)
            routed_turn(0, True)
            with act.Fori(1, E0 // 4) as j:
                routed_turn(j, False)
            shared_expert(1)

            norm_layer(A1)
            act.wait_ge(a1_pre_dve, 7)
            for b in range(B):
                act.wait_ge(a1_pre_mm, b + 1)
                act.activation(big_q[:, b * SEQ:(b + 1) * SEQ], bank[b][:, :], ACT.Identity,
                               bias=a1bs[:, :], scale=SCALE1).then_inc(a1_pre_act, 1)
            for b in range(B):
                act.wait_ge(a1_pre_mm, 8 + b + 1)
                act.activation(qtok[:, b * QT:(b + 1) * QT, :], bank[b][:, :].rearrange("p (t d) -> p t d", d=D),
                               ACT.Copy, scale=SCALE1).then_inc(a1_pre_act, 1)

            def a1_copy(it, n):
                act.wait_ge(a1_t, it * 16 + n + 1)
                hg, lg = n // 8, n % 8
                act.activation(probTh[hg][:, :, :, lg * LG:(lg + 1) * LG].rearrange("p k h l -> p k l h"),
                               bank[5][:, :].rearrange("p (k l h) -> p k l h", k=QT, l=LG), ACT.Copy).then_inc(a1_tca, 1)

            def a1_turn(it, first):
                for n in range(16):
                    act.wait_ge(a1_max, it * 16 + n + 1)
                    act.activation(ptile[n % 4], bank[n % 4][:, :], ACT.Exp, bias=negmax[:, n % 8:n % 8 + 1]).then_inc(a1_exp, 1)
                    if n >= 3 and n % 2 == 1:
                        a1_copy(it, n - 2)
                    elif n == 1 and not first:
                        a1_copy(it - 1, 15)

            a1_turn(0, True)
            with act.Fori(1, NT) as it:
                a1_turn(it, False)
            a1_copy(NT - 1, 15)

            norm_layer(X1)
            for b in range(B):
                act.wait_ge(x1_q, b + 1)
                act.activation(big_q[:, b * SEQ:(b + 1) * SEQ], bank[b][:, :], ACT.Identity, bias=x1b[:, 0:1]).then_inc(x1_qc, 1)
            with act.Fori(0, B) as b:
                act.wait_ge(x1_sub, b + 1)
                act.activation(prob0[:, 0:QT * LK], shifted0[:, 0:QT * LK], ACT.Exp, scale=SCALEX1).then_inc(x1_exp, 1)
                act.wait_ge(x1_t, b + 1)
                act.activation(prob0T[0:LK, 0, :], bank[4][0:LK, :], ACT.Copy).then_inc(x1_tc, 1)

            norm_layer(F1)
            act.wait_ge(g_exp, 3)
            act.activation(g_t2[:, :, 0:E1], g_t1[:, :, 0:E1], ACT.Exp).then_inc(g_exp, 1)
            act.wait_ge(g_exp, 5)
            act.activation(g_m1[:, :], g_m2[:, :], ACT.Exp).then_inc(g_exp, 1)
            with act.Fori(0, E1 // 2) as i:
                for u in range(16):
                    act.wait_ge(ff["h"], i * 16 + u + 1)
                    if u >= 2:
                        act.wait_ge(ff["hid"], i * 16 + u - 1)
                    act.activation(silu[:, u % 2, :], bank[2 * (u % 2)][:, :], ACT.Silu).then_inc(ff["silu"], 1)

        @block.tensor
        def _(pe):
            def norm_layer(layer):
                for b in range(B):
                    pe.wait_ge(ln_ready, layer * B + b + 1)
                    for t in range(QT):
                        mm = pe.transpose(bank[4 + b][:, t * P:(t + 1) * P], ln_h[:, b * QT + t, :], ident)
                    mm.then_inc(ln_tp, 1)

            pe.wait_ge(ld_cst, 16)
            pe.wait_ge(setup, 4)
            norm_layer(A0)
            pe.wait_ge(ld_x0, 128)
            pe.wait_ge(ln_out, 4)
            for i, w in enumerate((x0w[:, 2, :], x0w[:, 3, :], x1w[:, 1, :])):
                pe.matmul(bank[i][:, 0:B * LK], w, ctxT[:, :], start=True, stop=True).then_inc(pre_mm, 1)
            for i, (w, row) in enumerate(((x0w[:, 4, :], x0rows[:, 0, :]), (x1w[:, 2, :], x1rows[:, :]))):
                for b in range(B):
                    o = bank[3 + i][0:LK, b * D:(b + 1) * D]
                    pe.matmul(o, ctxT[:, b * LK:(b + 1) * LK], w, start=True, stop=False)
                    mm = pe.matmul(o, ones[0:1, 0:LK], row, start=False, stop=True)
                mm.then_inc(pre_mm, 1)
            pe.wait_ge(pre_act, 3)
            pe.wait_ge(pre_dve, 4)

            def a0_project_q(g):
                pe.wait_ge(a0_staged, g * 2 + 2)
                if not (isinstance(g, int) and g == 0):
                    pe.wait_ge(a0_vc, g)
                pe.matmul(bank[6][:, :], wst[:, 0, :], hst[:, :], start=True, stop=True).then_inc(a0_q, 1)

            def a0_project_k(g):
                pe.wait_ge(a0_qc, g + 1)
                pe.matmul(bank[6][:, :], wst[:, 1, :], hst[:, :], start=True, stop=True).then_inc(a0_k, 1)

            def a0_project_v(g):
                pe.wait_ge(a0_kc, g + 1)
                for kt in range(QT):
                    mm = pe.matmul(bank[6][:, kt * P:(kt + 1) * P], hst[:, kt * P:(kt + 1) * P], wst[:, 2, :],
                                   start=True, stop=True)
                mm.then_inc(a0_v, 1)

            def a0_scores(g, u, par, first):
                if u == 0:
                    pe.wait_ge(a0_qc, g + 1)
                    pe.wait_ge(a0_kc, g + 1)
                if not (first and u < 4):
                    pe.wait_ge(a0_exp, g * UN + u - 3)
                r = (u // QT) * DK
                j = u % QT
                pe.matmul(bank[j][:, :], a0_qT[par][r:r + DK, j * P:(j + 1) * P], a0_kT[par][r:r + DK, :],
                          start=True, stop=True).then_inc(a0_s, 1)

            def a0_turn_t(g, u, first):
                pe.wait_ge(a0_norm, g * UN + u + 1)
                if not (first and u < 2):
                    pe.wait_ge(a0_tc, g * UN + u - 1)
                for kt in range(QT):
                    mm = pe.transpose(bank[4 + u % 2][:, kt * P:(kt + 1) * P], a0_p[u % 4][:, kt * P:(kt + 1) * P], ident)
                mm.then_inc(a0_t, 1)

            def a0_values(g, par, first):
                pe.wait_ge(a0_tc, g * UN + UN)
                pe.wait_ge(a0_vc, g + 1)
                if not first:
                    pe.wait_ge(a0_x, g)
                for kt in range(QT):
                    for h in range(2):
                        mm = pe.matmul(bank[7][h * DK:(h + 1) * DK, :], a0_vtok[par][:, kt, h * DK:(h + 1) * DK],
                                       a0_pT[h][:, kt, :], start=(kt == 0), stop=(kt == QT - 1))
                mm.then_inc(a0_pv, 1)

            def a0_output(g):
                pe.wait_ge(a0_ftc, g + 1)
                for q in range(QT):
                    mm = pe.matmul(bank[7][:, q * P:(q + 1) * P], featsT[:, q * P:(q + 1) * P],
                                   wo0[:, ds(g % HP, 1), :].rearrange("p a n -> p (a n)"), start=True, stop=True)
                mm.then_inc(a0_o, 1)

            def a0_turn(g, par, first, last, second=False):
                for u in range(UN):
                    a0_scores(g, u, par, first)
                    if not first and u < 3:
                        a0_turn_t(g - 1, u + 5, False)
                    if not first and u == 3:
                        a0_values(g - 1, 1 - par, second)
                    if u >= 3:
                        a0_turn_t(g, u - 3, first)
                    if not first and u == 5:
                        a0_output(g - 1)
                    if not last:
                        if u == 4:
                            a0_project_q(g + 1)
                        if u == 5:
                            a0_project_k(g + 1)
                        if u == 6:
                            a0_project_v(g + 1)

            a0_project_q(0)
            a0_project_k(0)
            a0_project_v(0)
            a0_turn(0, 0, True, False)
            a0_turn(1, 1, False, False, second=True)
            with pe.Fori(1, PAIRS // 2 - 1) as i:
                a0_turn(i * 2, 0, False, False)
                a0_turn(i * 2 + 1, 1, False, False)
            a0_turn(PAIRS - 2, 0, False, False)
            a0_turn(PAIRS - 1, 1, False, True)
            for u in range(5, UN):
                a0_turn_t(PAIRS - 1, u, False)
            a0_values(PAIRS - 1, 1, False)
            a0_output(PAIRS - 1)

            norm_layer(X0)
            for b in range(B):
                pe.wait_ge(ln_out, X0 * B + b + 1)
                if b >= 2:
                    pe.wait_ge(x0_qr, b - 1)
                for i in range(2):
                    mm = pe.matmul(bank[2 * (b % 2) + i][:, :], x0w[:, i, :], hT[:, b * SEQ:(b + 1) * SEQ], start=True, stop=True)
                mm.then_inc(x0_q, 1)
            pe.wait_ge(x0_qr, 4)
            pe.wait_ge(pre_pool, 4)
            HS = (0, 6, 12, 16)

            def x0_scores(t, first):
                pe.wait_ge(x0_staged, t + 1)
                for i in range(3):
                    n = HS[i + 1] - HS[i]
                    if not first:
                        pe.wait_ge(x0_sub, t * 3 - 2 + i)
                    o = bank[i][:, 0:n * LK]
                    pe.matmul(o, qst[:, :], big_k[:, ds(t // QT, 1), HS[i]:HS[i + 1], :].rearrange("p b h k -> p (b h k)"),
                              start=True, stop=False)
                    pe.matmul(o.rearrange("p (h k) -> p h k", k=LK), ones_bf[:, :],
                              bcast(maskrow[:, ds((t // QT) * LK, LK)], 1, n), start=False, stop=True).then_inc(x0_s, 1)

            def x0_rest(t, first):
                pe.wait_ge(x0_exp, t + 1)
                for c in range(4):
                    if c >= 2:
                        if c % 2 == 0:
                            pe.wait_ge(x0_tcd, t * 2 + c // 2)
                        else:
                            pe.wait_ge(x0_tca, t * 2 + c // 2)
                    for j in range(4):
                        mm = pe.transpose(bank[4 + c % 2][0:LK, j * P:(j + 1) * P],
                                          prob0[:, (c * 4 + j) * LK:(c * 4 + j + 1) * LK], ident)
                    mm.then_inc(x0_t, 1)
                pe.wait_ge(x0_tcd, t * 2 + 2)
                pe.wait_ge(x0_tca, t * 2 + 2)
                for h in range(H):
                    mm = pe.matmul(bank[6][:, h * (HD + 1):(h + 1) * (HD + 1)], prob0T[0:LK, h // 4, (h % 4) * P:(h % 4 + 1) * P],
                                   vx0[:, ds(t // QT, 1), h, :].rearrange("p b d -> p (b d)"), start=True, stop=True)
                mm.then_inc(x0_pv, 1)
                pe.wait_ge(x0_norm, t + 1)
                pe.transpose(bank[7][:, 0:P], f0[:, :], ident).then_inc(x0_ft, 1)
                pe.wait_ge(x0_ftc, t + 1)
                pe.matmul(bank[3][:, 0:D], f0T[:, :], x0w[:, 5, :], start=True, stop=False)
                pe.matmul(bank[3][:, 0:D], ones[0:1, :], x0rows[:, 1, :], start=False, stop=True).then_inc(x0_o, 1)

            x0_scores(0, True)
            with pe.Fori(1, NT) as t:
                x0_scores(t, False)
                x0_rest(t - 1, False)
            x0_rest(NT - 1, False)

            def router(layer, w, n):
                for b in range(B):
                    pe.wait_ge(ln_out, layer * B + b + 1)
                for t in range(NT):
                    mm = pe.matmul(bank[0][:, t * n:(t + 1) * n], hT[:, t * P:(t + 1) * P], w, start=True, stop=True)
                mm.then_inc(g_mm, 1)

            def shared_expert(s):
                def products(k):
                    pe.wait_ge(sh_hid, 2 * k + 2)
                    if k >= 2:
                        pe.wait_ge(sh_acc, k - 1)
                    for t in range(QT):
                        for hf in range(2):
                            mm = pe.matmul(bank[4 + k % 2][:, t * P:(t + 1) * P], hid[:, k % 2, hf, t * P:(t + 1) * P],
                                           w2[:, E0 + s, hf, :], start=(hf == 0), stop=(hf == 1))
                    mm.then_inc(sh_y, 1)

                for k in range(s * B, s * B + B):
                    c = k % B
                    for hf in range(2):
                        u = 2 * k + hf
                        if u >= 2:
                            pe.wait_ge(sh_hid, u - 1)
                        for w in range(2):
                            mm = pe.matmul(bank[2 * (u % 2) + w][:, :], w13[:, E0 + s, w, hf * P:(hf + 1) * P],
                                           hT[:, c * SEQ:(c + 1) * SEQ], start=True, stop=True)
                        mm.then_inc(sh_h, 1)
                    if c:
                        products(k - 1)
                products(s * B + B - 1)

            def routed_t(e, k, first):
                pe.wait_ge(xs_in[k // 2], (e // 4) * 16 + 16)
                if not (first and k < 2):
                    pe.wait_ge(r_tc, e - 1)
                for t in range(ET):
                    mm = pe.transpose(bank[4 + k % 2][:, t * P:(t + 1) * P], xs[:, k // 2, (k % 2) * ET + t, :], ident)
                mm.then_inc(r_t, 1)

            def routed_up(e, k, first):
                pe.wait_ge(r_tc, e + 1)
                pe.wait_ge(r_staged, e + 1)
                for hf in range(2):
                    if not (first and k == 0):
                        pe.wait_ge(r_hid, e * 2 + hf - 1)
                    for w in range(2):
                        mm = pe.matmul(bank[2 * hf + w][:, 0:CAP], w13st[:, k % 2, w, hf * P:(hf + 1) * P], xsT[:, k % 2, :],
                                       start=True, stop=True)
                    mm.then_inc(r_h, 1)

            def routed_down(e, k, first):
                pe.wait_ge(r_hid, e * 2 + 2)
                if not (first and k < 2):
                    pe.wait_ge(r_yc, e - 1)
                for t in range(ET):
                    for hf in range(2):
                        mm = pe.matmul(bank[6 + k % 2][:, t * P:(t + 1) * P], hs[:, k % 2, hf, t * P:(t + 1) * P],
                                       w2[:, e, hf, :] if isinstance(e, int) else w2[:, ds(e, 1), hf, :].rearrange("p a n -> p (a n)"),
                                       start=(hf == 0), stop=(hf == 1))
                mm.then_inc(r_y, 1)

            def routed_turn(j, first):
                for k in (0, 2):
                    e = j * 4 + k
                    routed_t(e, k, first)
                    routed_t(e + 1, k + 1, first)
                    if not (first and k == 0):
                        routed_down(e - 1, (k + 3) % 4, first)
                    routed_up(e, k, first)
                    routed_up(e + 1, k + 1, first)
                    routed_down(e, k, first)

            norm_layer(F0)
            pe.wait_ge(ld_f0, 160)
            router(F0, gw0[:, :], E0)
            pe.wait_ge(g_chain, 60)
            for i in range(2):
                mm = pe.transpose(bank[1][:, i * P:(i + 1) * P], g_wm[:, i * NT // 2:(i + 1) * NT // 2, :].rearrange("p t e -> p (t e)"), ident)
            mm.then_inc(g_mm, 1)
            with pe.Fori(0, BISECT) as i:
                pe.wait_ge(b_count, i + 1)
                pe.matmul(bank[2][:, 0:1], same_expert, g_ge_cnt[:, :], start=True, stop=True).then_inc(b_total, 1)
            pe.wait_ge(g_chain, 80)
            for i in range(2):
                mm = pe.transpose(bank[1][:, i * P:(i + 1) * P], g_edges[:, i, :], ident)
            mm.then_inc(g_mm, 1)
            pe.wait_ge(g_chain, 100)
            pe.matmul(bank[1][:, 0:E0], ones[:, :], g_cnt[:, :], start=True, stop=True)

            def places(mask):
                m = mask.rearrange("p t e -> p (t e)")
                pe.matmul(bank[2][:, 0:NT * E0], tri, m, start=True, stop=True)
                pe.matmul(bank[3][:, 0:NT * E0], ones[:, :], m, start=True, stop=True).then_inc(g_mm, 1)

            places(g_t1[:, :, :])
            pe.wait_ge(g_chain, 150)
            places(g_sc[:, :, :])
            pe.wait_ge(g_chain, 200)
            shared_expert(0)
            pe.wait_ge(sh_acc, B)
            pe.wait_ge(r_pad, 1)
            routed_turn(0, True)
            with pe.Fori(1, E0 // 4) as j:
                routed_turn(j, False)
            routed_down(E0 - 1, 3, False)
            pe.wait_ge(r_hid, 2 * E0)
            shared_expert(1)

            norm_layer(A1)
            pe.wait_ge(ld_a1, 96)
            for i, w in enumerate((0, 2)):
                for b in range(B):
                    pe.wait_ge(ln_out, A1 * B + (b if i == 0 else B - 1) + 1)
                    pe.matmul(bank[4 * i + b][:, :], a1w[:, w, :], hT[:, b * SEQ:(b + 1) * SEQ], start=True, stop=True).then_inc(a1_pre_mm, 1)
            for i, (w, row) in enumerate(((1, 0), (3, 1))):
                for b in range(B):
                    if i == 0:
                        pe.wait_ge(a1_pre_act, b + 1)
                    else:
                        pe.wait_ge(a1_pre_dve, 7 + b + 1)
                    for t in range(QT):
                        o = bank[4 * i + b][:, t * D:(t + 1) * D]
                        tt = b * QT + t
                        pe.matmul(o, hT[:, tt * P:(tt + 1) * P], a1w[:, w, :], start=True, stop=False)
                        mm = pe.matmul(o, ones[0:1, :], a1rows[:, row, :], start=False, stop=True)
                    mm.then_inc(a1_pre_mm, 1)
            pe.wait_ge(a1_pre_act, 8)
            pe.wait_ge(a1_pre_dve, 15)
            pe.wait_ge(a1_rel, 16 * LG)

            def a1_scores(it, n, first):
                hg, lg = n // 8, n % 8
                if lg == 0:
                    pe.wait_ge(a1_qb, it * 5 + hg * 2 + 3)
                if not (first and n < 4):
                    pe.wait_ge(a1_exp, it * 16 + n - 3)
                pe.matmul(bank[n % 4][:, :], qblk[hg][:, lg, :, :].rearrange("p l h -> p (l h)"),
                          a1_keys[:, ds(it % 2, 1), :].rearrange("p i n -> p (i n)"), start=True, stop=False)
                first_key = window(it % QT)
                pe.matmul(bank[n % 4][:, ds(first_key, WIN)], rblk[hg][:, lg, :, :].rearrange("p l h -> p (l h)"),
                          relT[:, ds((it % QT) * -P + first_key + (OFF - lg * LG), WIN)], start=False, stop=True).then_inc(a1_s, 1)

            def a1_turn_t(it, n):
                pe.wait_ge(a1_exp, it * 16 + n + 1)
                if not (isinstance(it, int) and it == 0 and n < 2):
                    pe.wait_ge((a1_tcd, a1_tca)[n % 2], it * 8 + n // 2)
                for kt in range(QT):
                    mm = pe.transpose(bank[4 + n % 2][:, kt * P:(kt + 1) * P], ptile[n % 4][:, kt * P:(kt + 1) * P], ident)
                mm.then_inc(a1_t, 1)

            def a1_values(it, hg):
                for copied in (a1_tcd, a1_tca):
                    pe.wait_ge(copied, it * 8 + hg * 4 + 4)
                pe.wait_ge(a1_vs, it + 1)
                if not (isinstance(it, int) and it == 0 and hg == 0):
                    pe.wait_ge(a1_oc, it * 2 + hg)
                for grp in range(2):
                    for kt in range(QT):
                        for j in range(4):
                            mm = pe.matmul(bank[6][32 * j:32 * j + 32, grp * P:(grp + 1) * P],
                                           vst[:, kt, hg * HG + grp * 4 + j, :], probTh[hg][:, kt, grp * 4 + j, :],
                                           start=(kt == 0), stop=(kt == QT - 1))
                mm.then_inc(a1_pv, 1)

            def a1_back(it, hg):
                pe.wait_ge(a1_oc, it * 2 + hg + 1)
                if hg == 1:
                    pe.wait_ge(a1_norm, it * 2 + 1)
                elif not (isinstance(it, int) and it == 0):
                    pe.wait_ge(a1_x, it)
                for grp in range(2):
                    mm = pe.transpose(bank[7][:, grp * P:(grp + 1) * P], osb[:, grp, :], ident)
                mm.then_inc(a1_ot, 1)

            def a1_feats(it):
                pe.wait_ge(a1_norm, it * 2 + 2)
                pe.transpose(bank[7][:, 2 * P:3 * P], feats1[:, :], ident).then_inc(a1_ft, 1)

            def a1_project(it):
                pe.wait_ge(a1_ftc, it + 1)
                pe.matmul(bank[7][:, 3 * P:], feats1T[:, :], a1w[:, 4, :], start=True, stop=False)
                pe.matmul(bank[7][:, 3 * P:], ones[0:1, :], a1rows[:, 2, :], start=False, stop=True).then_inc(a1_o, 1)

            def a1_turn(it, first):
                for n in range(16):
                    a1_scores(it, n, first)
                    if n >= 2:
                        a1_turn_t(it, n - 2)
                    elif not first:
                        a1_turn_t(it - 1, 14 + n)
                    if not first:
                        if n == 3:
                            a1_values(it - 1, 1)
                        if n == 4:
                            a1_back(it - 1, 1)
                        if n == 6:
                            a1_feats(it - 1)
                        if n == 8:
                            a1_project(it - 1)
                    if n == 11:
                        a1_values(it, 0)
                    if n == 13:
                        a1_back(it, 0)

            a1_turn(0, True)
            with pe.Fori(1, NT) as it:
                a1_turn(it, False)
            it = NT - 1
            a1_turn_t(it, 14)
            a1_turn_t(it, 15)
            a1_values(it, 1)
            a1_back(it, 1)
            a1_feats(it)
            a1_project(it)

            norm_layer(X1)
            for b in range(B):
                pe.wait_ge(ln_out, X1 * B + b + 1)
                pe.matmul(bank[b][:, :], x1w[:, 0, :], hT[:, b * SEQ:(b + 1) * SEQ], start=True, stop=True).then_inc(x1_q, 1)
            pe.wait_ge(x1_qc, 4)
            def x1_turn(b, first):
                pe.wait_ge(x1_staged, b + 1)
                if not first:
                    pe.wait_ge(x1_x, b * QT)
                for t in range(QT):
                    mm = pe.matmul(bank[0][:, t * LK:(t + 1) * LK], hst[:, t * P:(t + 1) * P], k1T[:, ds(b * LK, LK)], start=True, stop=True)
                mm.then_inc(x1_s, 1)
                pe.wait_ge(x1_exp, b + 1)
                for t in range(QT):
                    mm = pe.transpose(bank[4][0:LK, t * P:(t + 1) * P], prob0[:, t * LK:(t + 1) * LK], ident)
                mm.then_inc(x1_t, 1)
                pe.wait_ge(x1_tc, b + 1)
                for t in range(QT):
                    mm = pe.matmul(bank[5][:, t * D:(t + 1) * D], prob0T[0:LK, 0, t * P:(t + 1) * P],
                                   vx1[:, ds(b, 1), :].rearrange("p b d -> p (b d)"), start=True, stop=True)
                mm.then_inc(x1_pv, 1)

            x1_turn(0, True)
            with pe.Fori(1, B) as b:
                x1_turn(b, False)

            norm_layer(F1)
            router(F1, gw1[:, :], E1)
            pe.wait_ge(g_chain, 300)

            def products(i, k):
                c = k % 4
                pe.wait_ge(ff["hid"], i * 16 + 2 * k + 2)
                if k >= 2:
                    pe.wait_ge(ff["acc"], i * 8 + k - 1)
                for t in range(QT):
                    for hf in range(2):
                        mm = pe.matmul(bank[4 + k % 2][:, t * P:(t + 1) * P], hid[:, k % 2, hf, t * P:(t + 1) * P],
                                       w2[:, ds(i * 2 + k // 4, 1), hf, :].rearrange("p a n -> p (a n)"),
                                       start=(hf == 0), stop=(hf == 1))
                mm.then_inc(ff["y"], 1)

            with pe.Fori(0, E1 // 2) as i:
                for k in range(8):
                    e, c = k // 4, k % 4
                    if c == 0:
                        pe.wait_ge(ff["staged"], i * 2 + e + 1)
                    for hf in range(2):
                        u = 2 * k + hf
                        if u >= 2:
                            pe.wait_ge(ff["hid"], i * 16 + u - 1)
                        for w in range(2):
                            mm = pe.matmul(bank[2 * (u % 2) + w][:, :], w13st[:, e, w, hf * P:(hf + 1) * P],
                                           hT[:, c * SEQ:(c + 1) * SEQ], start=True, stop=True)
                        mm.then_inc(ff["h"], 1)
                    if k >= 1:
                        products(i, k - 1)
                products(i, 7)

        @block.vector
        def _(dve):
            steps = [0]

            def ln(ins):
                steps[0] += 1
                ins.then_inc(ln_step, 1)
                dve.wait_ge(ln_step, steps[0])

            def norm_layer(layer):
                for b in range(B):
                    xb = X[:, b * QT:(b + 1) * QT, :]
                    ln(dve.tensor_reduce(ln_mean[:, :], xb, AX.X, ALU.add))
                    ln(dve.tensor_scalar(ln_mean[:, :], ln_mean[:, :], 1.0 / D, None, ALU.mult))
                    ln(dve.tensor_tensor(xc[:, :, :], xb, bcast(ln_mean[:, :], 2, D), ALU.subtract))
                    ln(dve.tensor_tensor(xsq[:, :, :], xc[:, :, :], xc[:, :, :], ALU.mult))
                    ln(dve.tensor_reduce(ln_var[:, :], xsq[:, :, :], AX.X, ALU.add))
                    dve.tensor_scalar(ln_var[:, :], ln_var[:, :], 1.0 / D, EPS, ALU.mult, ALU.add).then_inc(ln_var_ok, 1)
                    dve.wait_ge(ln_std_ok, layer * B + b + 1)
                    ln(dve.reciprocal(ln_rstd[:, :], ln_std[:, :]))
                    ln(dve.tensor_tensor(ln_new[:, :], ln_rstd[:, :], ln_rstd[:, :], ALU.mult))
                    ln(dve.tensor_tensor(ln_new[:, :], ln_new[:, :], ln_var[:, :], ALU.mult))
                    ln(dve.tensor_scalar(ln_new[:, :], ln_new[:, :], -0.5, 1.5, ALU.mult, ALU.add))
                    ln(dve.tensor_tensor(ln_rstd[:, :], ln_rstd[:, :], ln_new[:, :], ALU.mult))
                    dve.tensor_tensor(ln_h[:, b * QT:(b + 1) * QT, :], xc[:, :, :], bcast(ln_rstd[:, :], 2, D), ALU.mult).then_inc(ln_ready, 1)

            dve.wait_ge(ld_x, 16)
            norm_layer(A0)
            dve.wait_ge(ld_x0, 128)
            dve.tensor_scalar(maskrow[:, :], mask8[:, :], -1.0, 1e38, ALU.add, ALU.mult).then_inc(pre_dve, 1)
            dve.wait_ge(ld_cst, 16)
            kc = bcast(cst[:, C_CK:C_CK + LK], 1, B)
            ks = bcast(cst[:, C_SK:C_SK + LK], 1, B)
            for i, (o, tab) in enumerate(((krope, kc), (krope2, ks))):
                dve.wait_ge(pre_mm, i + 1)
                dve.scalar_tensor_tensor(o[:, :, :], bank[i][:, 0:B * LK].rearrange("p (b k) -> p b k", b=B),
                                         x0b[:, 2 + i:3 + i], tab, ALU.add, ALU.mult).then_inc(pre_dve, 1)
            dve.wait_ge(pre_dve, 3)
            dve.tensor_tensor(krope[:, :, :], krope[:, :, :], krope2[:, :, :], ALU.add).then_inc(pre_dve, 1)

            def a0_copy(g, u):
                dve.wait_ge(a0_t, g * UN + u + 1)
                dve.tensor_copy(a0_pT[u // QT][:, :, (u % QT) * P:(u % QT + 1) * P],
                                bank[4 + u % 2][:, :].rearrange("p (a b) -> p a b", a=QT)).then_inc(a0_tc, 1)

            def a0_maximum(g, u):
                dve.wait_ge(a0_s, g * UN + u + 1)
                dve.tensor_reduce(negmax[:, u:u + 1], bank[u % 4][:, :], AX.X, ALU.max, negate=True).then_inc(a0_max, 1)

            def a0_add(g):
                dve.wait_ge(a0_o, g + 1)
                xb = X[:, ds((g // HP) * QT, QT), :]
                dve.tensor_tensor(xb, xb, bank[7][:, :].rearrange("p (a b) -> p a b", b=P), ALU.add).then_inc(a0_x, 1)

            def a0_reciprocal(g, u):
                dve.wait_ge(a0_exp, g * UN + u + 1)
                dve.reciprocal(rden[:, u:u + 1], den[:, u:u + 1]).then_inc(a0_rd, 1)

            def a0_turn(g, first):
                for u in range(UN):
                    a0_maximum(g, u)
                    if u:
                        a0_reciprocal(g, u - 1)
                    elif not first:
                        a0_reciprocal(g - 1, UN - 1)
                    if u >= 3:
                        a0_copy(g, u - 3)
                    elif not first:
                        a0_copy(g - 1, u + 5)
                    if u == 6 and not first:
                        a0_add(g - 1)

            a0_turn(0, True)
            with dve.Fori(1, PAIRS) as g:
                a0_turn(g, False)
            a0_reciprocal(PAIRS - 1, UN - 1)
            for u in range(5, UN):
                a0_copy(PAIRS - 1, u)
            a0_add(PAIRS - 1)
            dve.wait_ge(a0_x, PAIRS)

            norm_layer(X0)
            dve.wait_ge(zeroed, 16 * (ROWS // TOK))
            for b in range(B):
                dve.wait_ge(x0_q, b + 1)
                qb = big_q[:, b * SEQ:(b + 1) * SEQ]
                dve.scalar_tensor_tensor(qb, bank[2 * (b % 2)][:, :], x0b[:, 0:1], cst[:, C_CQ:C_CQ + SEQ], ALU.add, ALU.mult)
                if b:
                    dve.wait_ge(x0_qr, b)
                ln(dve.scalar_tensor_tensor(qrope2[:, :], bank[2 * (b % 2) + 1][:, :], x0b[:, 1:2], cst[:, C_SQ:C_SQ + SEQ], ALU.add, ALU.mult))
                dve.tensor_tensor(qb, qb, qrope2[:, :], ALU.add).then_inc(x0_qr, 1)
            HS = (0, 6, 12, 16)

            def x0_shift(t, first):
                for i in range(3):
                    n = HS[i + 1] - HS[i]
                    s = bank[i][:, 0:n * LK].rearrange("p (h k) -> p h k", k=LK)
                    dve.wait_ge(x0_s, t * 3 + i + 1)
                    dve.tensor_reduce(mx0[:, HS[i]:HS[i + 1]], s, AX.X, ALU.max).then_inc(x0_max, 1)
                    dve.wait_ge(x0_max, t * 3 + i + 1)
                    if not first and i == 0:
                        dve.wait_ge(x0_exp, t)
                    dve.tensor_tensor(shifted0[:, HS[i] * LK:HS[i + 1] * LK].rearrange("p (h k) -> p h k", k=LK), s,
                                      bcast(mx0[:, HS[i]:HS[i + 1]], 2, LK), ALU.subtract).then_inc(x0_sub, 1)

            def x0_rest(t):
                for c in (0, 2):
                    dve.wait_ge(x0_t, t * 4 + c + 1)
                    dve.tensor_copy(prob0T[0:LK, c, :], bank[4][0:LK, :]).then_inc(x0_tcd, 1)
                dve.wait_ge(x0_pv, t + 1)
                o = bank[6][:, 0:H * (HD + 1)].rearrange("p (h d) -> p h d", h=H)
                dve.reciprocal(rd0[:, :].unsqueeze(2), o[:, :, HD:HD + 1]).then_inc(x0_rd, 1)
                dve.wait_ge(x0_rd, t + 1)
                dve.tensor_tensor(f0[:, :].rearrange("p (h d) -> p h d", h=H), o[:, :, 0:HD], bcast(rd0[:, :], 2, HD),
                                  ALU.mult).then_inc(x0_norm, 1)
                dve.wait_ge(x0_ft, t + 1)
                dve.tensor_copy(f0T[:, :], bank[7][:, 0:P]).then_inc(x0_ftc, 1)
                dve.wait_ge(x0_o, t + 1)
                xt = X[:, ds(t, 1), :].rearrange("p a d -> p (a d)")
                dve.tensor_tensor(xt, xt, bank[3][:, 0:D], ALU.add).then_inc(x0_x, 1)

            x0_shift(0, True)
            with dve.Fori(1, NT) as t:
                x0_shift(t, False)
                x0_rest(t - 1)
            x0_rest(NT - 1)
            dve.wait_ge(x0_x, NT)

            chain = [0]

            def link(ins):
                chain[0] += 1
                ins.then_inc(g_chain, 1)
                dve.wait_ge(g_chain, chain[0])

            def upto(n):
                ins_left = n - chain[0]
                chain[0] = n
                return ins_left

            def softmax_scores(n, mm, exp_turn):
                lg, t1, t2, sc = (x[:, :, 0:n] for x in (g_lg, g_t1, g_t2, g_sc))
                dve.wait_ge(g_mm, mm)
                link(dve.tensor_copy(lg, bank[0][:, 0:NT * n].rearrange("p (t e) -> p t e", e=n)))
                link(dve.tensor_reduce(g_mx[:, :], lg, AX.X, ALU.max))
                dve.tensor_tensor(t1, lg, bcast(g_mx[:, :], 2, n), ALU.subtract).then_inc(g_exp, 1)
                dve.wait_ge(g_exp, exp_turn)
                link(dve.tensor_reduce(g_mx[:, :], t2, AX.X, ALU.add))
                link(dve.reciprocal(g_mx[:, :], g_mx[:, :]))
                link(dve.tensor_tensor(sc, t2, bcast(g_mx[:, :], 2, n), ALU.mult))

            def first_largest(n, score, best, onehot):
                t1 = g_t1[:, :, 0:n]
                io = bcast(iota[:, 0:n], 1, NT)
                link(dve.tensor_reduce(best[:, :], score, AX.X, ALU.max))
                link(dve.tensor_tensor(t1, score, bcast(best[:, :], 2, n), ALU.is_equal))
                link(dve.tensor_scalar(t1, t1, -64.0, 64.0, ALU.mult, ALU.add))
                link(dve.tensor_tensor(t1, t1, io, ALU.add))
                link(dve.tensor_reduce(g_mx[:, :], t1, AX.X, ALU.min))
                link(dve.tensor_tensor(onehot, io, bcast(g_mx[:, :], 2, n), ALU.is_equal))

            def top_two(n):
                sc, t2, oh1, oh2 = (x[:, :, 0:n] for x in (g_sc, g_t2, g_oh1, g_oh2))
                first_largest(n, sc, g_m1, oh1)
                link(dve.scalar_tensor_tensor(t2, oh1, -1e30, sc, ALU.mult, ALU.add))
                first_largest(n, t2, g_m2, oh2)

            def shared_expert(s):
                def add(k):
                    dve.wait_ge(sh_y, k + 1)
                    for t in range(QT):
                        tt = (k % B) * QT + t
                        ins = dve.scalar_tensor_tensor(X[:, tt, :], bank[4 + k % 2][:, t * P:(t + 1) * P], 1.0 / NSH, X[:, tt, :],
                                                       ALU.mult, ALU.add)
                    ins.then_inc(sh_acc, 1)

                for k in range(s * B, s * B + B):
                    for hf in range(2):
                        u = 2 * k + hf
                        dve.wait_ge(sh_silu, u + 1)
                        dve.tensor_tensor(hid[:, k % 2, hf, :], bank[2 * (u % 2) + 1][:, :], silu[:, u % 2, :],
                                          ALU.mult).then_inc(sh_hid, 1)
                    if k % B:
                        add(k - 1)
                add(s * B + B - 1)

            def routed_copy(e, k, first):
                dve.wait_ge(r_t, e + 1)
                if not (first and k < 2):
                    dve.wait_ge(r_h, e * 2 - 2)
                dve.tensor_copy(xsT[:, k % 2, :], bank[4 + k % 2][:, 0:CAP]).then_inc(r_tc, 1)

            def routed_hid(e, k, first):
                if not (first and k < 2):
                    dve.wait_ge(r_y, e - 1)
                for hf in range(2):
                    dve.wait_ge(r_silu, e * 2 + hf + 1)
                    dve.tensor_tensor(hs[:, k % 2, hf, 0:CAP], bank[2 * hf + 1][:, 0:CAP], silu[:, hf, 0:CAP], ALU.mult).then_inc(r_hid, 1)

            def routed_turn(j, first):
                for k in (0, 2):
                    e = j * 4 + k
                    routed_copy(e, k, first)
                    routed_copy(e + 1, k + 1, first)
                    routed_hid(e, k, first)
                    routed_hid(e + 1, k + 1, first)

            norm_layer(F0)
            dve.wait_ge(ld_f0, 160)
            softmax_scores(E0, 1, 2)
            link(dve.tensor_tensor(g_sc[:, :, :], g_sc[:, :, :], bcast(gb0[:, :], 1, NT), ALU.add))
            top_two(E0)
            link(dve.tensor_tensor(g_sc[:, :, :], g_oh1[:, :, :], g_oh2[:, :, :], ALU.add))
            link(dve.tensor_tensor(g_t1[:, :, :], g_lg[:, :, :], g_sc[:, :, :], ALU.mult))
            link(dve.tensor_scalar(g_t2[:, :, :], g_sc[:, :, :], -1.0, 1e30, ALU.add, ALU.mult))
            left = upto(60)
            dve.tensor_tensor(g_wm[:, :, :], g_t1[:, :, :], g_t2[:, :, :], ALU.add).then_inc(g_chain, left)
            dve.tensor_reduce(g_abs[:, :], g_lg[:, :, :], AX.XY, ALU.max, apply_absolute_value=True).then_inc(g_pool, 1)
            dve.wait_ge(g_chain, 60)
            for c, oh in enumerate((g_oh1, g_oh2)):
                link(dve.tensor_tensor(g_t1[:, :, :], g_lg[:, :, :], oh, ALU.mult))
                link(dve.tensor_reduce(g_w[:, c, :], g_t1[:, :, :], AX.X, ALU.add))
            dve.wait_ge(g_mm, 2)
            link(dve.tensor_copy(g_wmT[:, :], bank[1][:, 0:2 * P]))
            dve.wait_ge(g_pool, 2)
            link(dve.tensor_scalar(g_step[:, :], g_all[:, :], 1e-20, None, ALU.max))
            link(dve.tensor_scalar(g_lo[:, :], g_step[:, :], -1.0, None, ALU.mult))
            with dve.Fori(0, BISECT // BSTEPS) as i:
                for k in range(BSTEPS):
                    def blink(ins, n):
                        ins.then_inc(b_chain, 1)
                        dve.wait_ge(b_chain, i * (4 * BSTEPS) + k * 4 + n)
                    blink(dve.tensor_scalar(g_try[:, :], g_lo[:, :], g_step[:, 0:1], None, ALU.add), 1)
                    blink(dve.tensor_scalar(g_ge[:, :], g_wmT[:, :], g_try[:, 0:1], None, ALU.is_ge), 2)
                    dve.tensor_reduce(g_ge_cnt[:, :], g_ge[:, :], AX.X, ALU.add).then_inc(b_count, 1)
                    dve.wait_ge(b_total, i * BSTEPS + k + 1)
                    blink(dve.tensor_scalar(g_inc[:, :], bank[2][:, 0:1], CAP - 0.5, g_step[:, 0:1], ALU.is_ge, ALU.mult), 3)
                    dve.tensor_scalar(g_step[:, :], g_step[:, :], 0.5, None, ALU.mult)
                    blink(dve.tensor_tensor(g_lo[:, :], g_lo[:, :], g_inc[:, :], ALU.add), 4)
            link(dve.tensor_scalar(g_step[:, :], g_step[:, :], 2.0, None, ALU.mult))
            link(dve.tensor_scalar(g_try[:, :], g_lo[:, :], g_step[:, 0:1], None, ALU.add))
            link(dve.tensor_copy(g_edges[:, 0, :], g_lo[:, :].broadcast_to([P, P])))
            left = upto(80)
            dve.tensor_copy(g_edges[:, 1, :], g_try[:, :].broadcast_to([P, P])).then_inc(g_chain, left)
            dve.wait_ge(g_mm, 3)
            link(dve.tensor_copy(g_elo[:, :], bank[1][:, 0:E0]))
            link(dve.tensor_copy(g_ehi[:, :], bank[1][:, P:P + E0]))
            link(dve.tensor_tensor(g_t1[:, :, :], g_wm[:, :, :], bcast(g_elo[:, :], 1, NT), ALU.is_ge))
            link(dve.tensor_tensor(g_t2[:, :, :], g_wm[:, :, :], bcast(g_ehi[:, :], 1, NT), ALU.is_ge))
            link(dve.tensor_reduce(g_cnt[:, :], g_t2[:, :, :].rearrange("p t e -> p e t"), AX.X, ALU.add))
            left = upto(100)
            dve.tensor_tensor(g_t1[:, :, :], g_t1[:, :, :], g_t2[:, :, :], ALU.subtract).then_inc(g_chain, left)

            def places(into):
                tot = bank[3][:, 0:NT * E0].rearrange("p (t e) -> p t e", e=E0)
                link(dve.memset(into[:, 0, :], 0.0))
                for t in range(1, NT):
                    link(dve.tensor_tensor(into[:, t, :], into[:, t - 1, :], tot[:, t - 1, :], ALU.add))
                link(dve.tensor_tensor(into, into, bank[2][:, 0:NT * E0].rearrange("p (t e) -> p t e", e=E0), ALU.add))

            dve.wait_ge(g_mm, 4)
            link(dve.tensor_scalar(g_left[:, :], bank[1][:, 0:E0], -1.0, float(CAP), ALU.mult, ALU.add))
            places(g_sc)
            link(dve.tensor_tensor(g_sc[:, :, :], g_sc[:, :, :], bcast(g_left[:, :], 1, NT), ALU.is_lt))
            link(dve.tensor_tensor(g_sc[:, :, :], g_sc[:, :, :], g_t1[:, :, :], ALU.mult))
            left = upto(150)
            dve.tensor_tensor(g_sc[:, :, :], g_sc[:, :, :], g_t2[:, :, :], ALU.add).then_inc(g_chain, left)
            dve.wait_ge(g_mm, 5)
            places(g_rt)
            link(dve.scalar_tensor_tensor(g_rt[:, :, :], bcast(iota, 1, NT), float(PITCH), g_rt[:, :, :], ALU.mult, ALU.add))
            link(dve.tensor_scalar(g_t1[:, :, :], g_sc[:, :, :], -float(ROWS), float(ROWS), ALU.mult, ALU.add))
            link(dve.tensor_tensor(g_rt[:, :, :], g_rt[:, :, :], g_t1[:, :, :], ALU.add))
            for c, oh in enumerate((g_oh1, g_oh2)):
                link(dve.tensor_tensor(g_t1[:, :, :], g_rt[:, :, :], oh, ALU.mult))
                link(dve.tensor_reduce(g_m1[:, :], g_t1[:, :, :], AX.X, ALU.add))
                left = upto(200) if c else 1
                ins = dve.tensor_copy(g_row[:, c, :], g_m1[:, :])
                if c:
                    ins.then_inc(g_chain, left)
                else:
                    link(ins)
            shared_expert(0)
            routed_turn(0, True)
            with dve.Fori(1, E0 // 4) as j:
                routed_turn(j, False)
            shared_expert(1)
            dve.wait_ge(sh_acc, 2 * B)
            for b in range(B):
                dve.wait_ge(got[b], 16 * 2 * QT)
                for c in range(2):
                    if c:
                        dve.wait_ge(f0_x, b * 2 + 1)
                    for t in range(b * QT, b * QT + QT):
                        ins = dve.scalar_tensor_tensor(X[:, t, :], gathered[c][:, t, :], g_w[:, c, t:t + 1], X[:, t, :], ALU.mult, ALU.add)
                    ins.then_inc(f0_x, 1)
            dve.wait_ge(f0_x, 2 * B)

            norm_layer(A1)
            dve.wait_ge(ld_a1, 96)
            edge = SEQ - 1 - LEFT
            dve.tensor_copy(embpad[:, 0:edge], emb[:, 0:1].broadcast_to([HD, edge])).then_inc(a1_pre_dve, 1)
            dve.tensor_copy(embpad[:, edge:edge + NPOS], emb[:, :]).then_inc(a1_pre_dve, 1)
            dve.tensor_copy(embpad[:, edge + NPOS:], emb[:, NPOS - 1:NPOS].broadcast_to([HD, 2 * SEQ - 1 - edge - NPOS])).then_inc(a1_pre_dve, 1)
            dve.tensor_copy(ends[:, 0:WLAST], emb_ends[:, 0:1].broadcast_to([P, WLAST])).then_inc(a1_pre_dve, 1)
            dve.memset(ends[:, WLAST:SEQ], 0.0).then_inc(a1_pre_dve, 1)
            dve.tensor_copy(ends[:, SEQ:], emb_ends[:, 1:2].broadcast_to([P, WLAST])).then_inc(a1_pre_dve, 1)
            dve.tensor_scalar(a1bs[:, :], a1b[:, 0:1], SCALE1, None, ALU.mult).then_inc(a1_pre_dve, 1)
            for b in range(B):
                dve.wait_ge(a1_pre_mm, B + b + 1)
                dve.tensor_scalar(a1_k[:, b * SEQ:(b + 1) * SEQ], bank[4 + b][:, :], a1b[:, 1:2], None, ALU.add).then_inc(a1_pre_dve, 1)
            dve.wait_ge(ln_tp, (A1 + 1) * B)
            for b in range(B):
                dve.wait_ge(a1_pre_mm, 3 * B + b + 1)
                dve.tensor_copy(v1[:, b * QT:(b + 1) * QT, :], bank[4 + b][:, :].rearrange("p (t d) -> p t d", d=D)).then_inc(a1_pre_dve, 1)

            def a1_maximum(it, n):
                dve.wait_ge(a1_s, it * 16 + n + 1)
                dve.tensor_reduce(negmax[:, n % 8:n % 8 + 1], bank[n % 4][:, :], AX.X, ALU.max, negate=True).then_inc(a1_max, 1)

            def a1_copy(it, n):
                dve.wait_ge(a1_t, it * 16 + n + 1)
                hg, lg = n // 8, n % 8
                dve.tensor_copy(probTh[hg][:, :, :, lg * LG:(lg + 1) * LG].rearrange("p k h l -> p k l h"),
                                bank[4][:, :].rearrange("p (k l h) -> p k l h", k=QT, l=LG)).then_inc(a1_tcd, 1)

            def a1_out(it, hg):
                dve.wait_ge(a1_pv, it * 2 + hg + 1)
                dve.tensor_copy(osb[:, :, :], bank[6][:, 0:2 * P].rearrange("p (g l) -> p g l", g=2)).then_inc(a1_oc, 1)

            def a1_normalise(it, hg):
                dve.wait_ge(a1_ot, it * 2 + hg + 1)
                o = bank[7][:, 0:2 * P].rearrange("p (h d) -> p h d", d=32)
                dve.reciprocal(rd1[:, :].unsqueeze(2), o[:, :, HD:HD + 1]).then_inc(a1_rd, 1)
                dve.wait_ge(a1_rd, it * 2 + hg + 1)
                dve.tensor_tensor(feats1[:, hg * HG * HD:(hg + 1) * HG * HD].rearrange("p (h d) -> p h d", d=HD), o[:, :, 0:HD],
                                  bcast(rd1[:, :], 2, HD), ALU.mult).then_inc(a1_norm, 1)

            def a1_feats(it):
                dve.wait_ge(a1_ft, it + 1)
                dve.tensor_copy(feats1T[:, :], bank[7][:, 2 * P:3 * P]).then_inc(a1_ftc, 1)

            def a1_add(it):
                dve.wait_ge(a1_o, it + 1)
                xt = X[:, ds(it, 1), :].rearrange("p a d -> p (a d)")
                dve.tensor_tensor(xt, xt, bank[7][:, 3 * P:], ALU.add).then_inc(a1_x, 1)

            def a1_turn(it, first):
                for n in range(16):
                    a1_maximum(it, n)
                    if n >= 2 and n % 2 == 0:
                        a1_copy(it, n - 2)
                    elif n == 0 and not first:
                        a1_copy(it - 1, 14)
                    if not first:
                        if n == 3:
                            a1_out(it - 1, 1)
                        if n == 4:
                            a1_normalise(it - 1, 1)
                        if n == 6:
                            a1_feats(it - 1)
                        if n == 8:
                            a1_add(it - 1)
                    if n == 11:
                        a1_out(it, 0)
                    if n == 13:
                        a1_normalise(it, 0)

            a1_turn(0, True)
            with dve.Fori(1, NT) as it:
                a1_turn(it, False)
            it = NT - 1
            a1_copy(it, 14)
            a1_out(it, 1)
            a1_normalise(it, 1)
            a1_feats(it)
            a1_add(it)
            dve.wait_ge(a1_x, NT)

            norm_layer(X1)
            with dve.Fori(0, B) as b:
                s = bank[0][:, 0:QT * LK].rearrange("p (t k) -> p t k", k=LK)
                p3 = prob0[:, 0:QT * LK].rearrange("p (t k) -> p t k", k=LK)
                dve.wait_ge(x1_s, b + 1)
                dve.tensor_reduce(negmax[:, 0:QT], s, AX.X, ALU.max).then_inc(x1_max, 1)
                dve.wait_ge(x1_max, b + 1)
                dve.tensor_tensor(shifted0[:, 0:QT * LK].rearrange("p (t k) -> p t k", k=LK), s,
                                  bcast(negmax[:, 0:QT], 2, LK), ALU.subtract).then_inc(x1_sub, 1)
                dve.wait_ge(x1_exp, b + 1)
                dve.tensor_reduce(den[:, 0:QT], p3, AX.X, ALU.add).then_inc(x1_den, 1)
                dve.wait_ge(x1_den, b * 2 + 1)
                dve.reciprocal(den[:, 0:QT], den[:, 0:QT]).then_inc(x1_den, 1)
                dve.wait_ge(x1_den, b * 2 + 2)
                dve.wait_ge(x1_pv, b + 1)
                for t in range(QT):
                    xt = X[:, ds(b * QT + t, 1), :].rearrange("p a d -> p (a d)")
                    dve.scalar_tensor_tensor(xt, bank[5][:, t * D:(t + 1) * D], den[:, t:t + 1], xt, ALU.mult, ALU.add).then_inc(x1_x, 1)
            dve.wait_ge(x1_x, NT)

            norm_layer(F1)
            softmax_scores(E1, 6, 4)
            top_two(E1)
            dve.tensor_tensor(g_m2[:, :], g_m2[:, :], g_m1[:, :], ALU.subtract).then_inc(g_exp, 1)
            dve.wait_ge(g_exp, 6)
            link(dve.tensor_scalar(g_m1[:, :], g_m1[:, :], 1.0, None, ALU.add))
            link(dve.reciprocal(g_m1[:, :], g_m1[:, :]))
            link(dve.tensor_scalar(g_m2[:, :], g_m1[:, :], -1.0, 1.0, ALU.mult, ALU.add))
            link(dve.tensor_tensor(g_t1[:, :, 0:E1], g_oh1[:, :, 0:E1], bcast(g_m1[:, :], 2, E1), ALU.mult))
            link(dve.tensor_tensor(g_t2[:, :, 0:E1], g_oh2[:, :, 0:E1], bcast(g_m2[:, :], 2, E1), ALU.mult))
            left = upto(300)
            dve.tensor_tensor(G[:, :, 0:E1], g_t1[:, :, 0:E1], g_t2[:, :, 0:E1], ALU.add).then_inc(g_chain, left)
            dve.wait_ge(g_chain, 300)

            def add(i, k):
                dve.wait_ge(ff["y"], i * 8 + k + 1)
                for t in range(QT):
                    tt = (k % 4) * QT + t
                    ins = dve.scalar_tensor_tensor(
                        X[:, tt, :], bank[4 + k % 2][:, t * P:(t + 1) * P],
                        G[:, tt, ds(i * 2 + k // 4, 1)], X[:, tt, :], ALU.mult, ALU.add)
                ins.then_inc(ff["acc"], 1)

            with dve.Fori(0, E1 // 2) as i:
                for k in range(8):
                    for hf in range(2):
                        u = 2 * k + hf
                        dve.wait_ge(ff["silu"], i * 16 + u + 1)
                        dve.tensor_tensor(hid[:, k % 2, hf, :], bank[2 * (u % 2) + 1][:, :], silu[:, u % 2, :],
                                          ALU.mult).then_inc(ff["hid"], 1)
                    if k >= 1:
                        add(i, k - 1)
                add(i, 7)
            dve.wait_ge(ff["acc"], E1 * 4)


def kernel(**inputs):
    import concourse.bacc as _bacc
    from concourse.bass_utils import run_bass_kernel_spmd as _run

    i = {k: np.asarray(v) for k, v in inputs.items()}

    def swap(w):
        return w.reshape(w.shape[:-1] + (D // 2, 2))[..., ::-1].reshape(w.shape)

    def dh(w):
        return w.reshape(w.shape[:-1] + (H, HD)).swapaxes(-1, -2).reshape(w.shape)

    def heads(w):
        return w.transpose(1, 0, 2).reshape(D, H * DK)

    kv, bkv = i["L0_xattn_Wkv"], i["L0_xattn_bkv"]
    wk, wv, bk, bv = kv[:, :D], kv[:, D:], bkv[:D], bkv[D:]
    wq0, bq0 = i["L0_xattn_Wq"], i["L0_xattn_bq"]
    arrays = {
        "x": i["x"].reshape(TOK, D),
        "cst": shape_constants(),
        "wq": heads(i["L0_attn_wq"]), "wk": heads(i["L0_attn_wk"]), "wv": heads(i["L0_attn_wv"]), "wo": i["L0_attn_wo"],
        "ctxT": i["ctx_1024"].reshape(B * LK, D).T,
        "mask": i["mask_BxS2_bf1"].reshape(1, B * LK).view(np.uint8),
        "x0w": np.stack([wq0, swap(wq0), wk, swap(wk), wv, i["L0_xattn_Wo"]], 1),
        "x0b": np.stack([bq0, swap(bq0), bk, swap(bk)], 1),
        "x0rows": np.stack([bv, i["L0_xattn_bo"]], 0)[None],
        "x1w": np.stack([i["L1_xattn_Wq"], i["L1_xattn_Wk"], i["L1_xattn_Wv"]], 1),
        "x1b": np.stack([i["L1_xattn_bq"], i["L1_xattn_bk"]], 1),
        "x1rows": i["L1_xattn_bv"][None],
        "gw0": i["L0_ffn_gate_w"], "gb0": i["L0_ffn_gate_b"],
        "ew1": i["L0_ffn_ew1"], "ew3": i["L0_ffn_ew3"], "ew2": i["L0_ffn_ew2"],
        "sw1": i["L0_ffn_sw1"], "sw3": i["L0_ffn_sw3"], "sw2": i["L0_ffn_sw2"],
        "a1w": np.stack([i["L1_attn_Wq"].T, dh(i["L1_attn_Wq"].T), i["L1_attn_Wk"].T, i["L1_attn_Wv"].T, i["L1_attn_Wo"].T], 1),
        "a1b": np.stack([i["L1_attn_bq"], i["L1_attn_bk"]], 1),
        "a1rows": np.stack([dh(i["L1_attn_bq"]), i["L1_attn_bv"], i["L1_attn_bo"]], 0)[None],
        "emb": i["L1_attn_dist_emb"].T,
        "emb_ends": np.tile(i["L1_attn_dist_emb"][[0, -1]].T, (H, 1)),
        "gw1": i["L1_ffn_kernel_router_DE"],
        "f1g": i["L1_ffn_kernel_gating_EDF"], "f1u": i["L1_ffn_kernel_up_EDF"], "f1d": i["L1_ffn_kernel_down_EFD"],
    }
    nc = _bacc.Bacc("TRN2", target_bir_lowering=False, num_devices=1)
    feed, aps = {}, {}
    for name, v in arrays.items():
        v = np.ascontiguousarray(v)
        feed[f"in_{name}"] = v
        aps[name] = nc.dram_tensor(f"in_{name}", v.shape, mybir.dt.from_np(v.dtype), kind="ExternalInput").ap()
    out = nc.dram_tensor("out", (TOK, D), F32, kind="ExternalOutput").ap()
    decoder_kernel(nc, aps, out)
    r = _run(nc, [feed], core_ids=[0])
    return r.results[0]["out"].reshape(B, SEQ, D)
```

```python
from contextlib import ExitStack

import numpy as np

import concourse.bass as bass
from concourse import mybir
from concourse.bass import ds

F32 = mybir.dt.float32
F32R = mybir.dt.float32r
BF16 = mybir.dt.bfloat16
U8 = mybir.dt.uint8
U32 = mybir.dt.uint32
ALU = mybir.AluOpType
ACT = mybir.ActivationFunctionType
AX = mybir.AxisListType
RMAX = bass.bass_isa.ReduceOp.max

P = 128
B, SEQ, D = 4, 512, 128
TOK = B * SEQ
NT = TOK // P
QT = SEQ // P
LK = 77
H = 16
DK = 64
HP = H // 2
HD = D // H
E0, E1 = 16, 8
NSH = 2
FF = 256
CAP = -(-TOK * 2 // E0 * 5 // 4)
LEFT, RIGHT = 64, 8
NPOS = LEFT + RIGHT + 1
LG = 16
HG = 8
EPS = 1e-5
BISECT = 16
BSTEPS = 4
CUTS = 3
ET = -(-CAP // P)
PITCH = ET * P
ROWS = E0 * PITCH
OFF = SEQ - LG
WIN = P + LEFT + 2 * RIGHT
WLAST = SEQ - WIN

C_ID = 0
C_MH = C_ID + P
C_DL = C_MH + H
C_IO = C_DL + LG
C_TRI = C_IO + E0
C_CQ = C_TRI + P
C_SQ = C_CQ + SEQ
C_CK = C_SQ + SEQ
C_SK = C_CK + LK
C_BLK = C_SK + LK
C_HH = C_BLK + P
C_N = C_HH + HG


def shape_constants():
    c = np.zeros((P, C_N), np.float32)
    p = np.arange(P)
    c[:, C_ID:C_ID + P] = np.eye(P)
    c[p, C_MH + p // HD] = 1.0
    c[p, C_DL + p // HD] = 1.0
    c[:, C_IO:C_IO + E0] = np.arange(E0)
    c[:, C_TRI:C_TRI + P] = np.triu(np.ones((P, P)), 1)
    c[:, C_BLK:C_BLK + P] = (p[:, None] % E0) == (p[None, :] % E0)
    c[p, C_HH + p % (P // 2) // HD] = 1.0
    inv = (1.0 / 10000.0 ** (np.arange(0, HD, 2, dtype=np.float32) / HD)).astype(np.float32)
    sign = np.where(p % 2 == 0, -1.0, 1.0)[:, None]
    for n, at_c, at_s, scale in ((SEQ, C_CQ, C_SQ, 64 ** -0.5), (LK, C_CK, C_SK, 1.0)):
        pos = (np.float32(10.0) * (np.arange(n, dtype=np.float32) / np.float32(n))).astype(np.float32)
        ang = (pos[None, :] * inv[(p % HD) // 2][:, None]).astype(np.float32)
        c[:, at_c:at_c + n] = np.cos(ang) * scale
        c[:, at_s:at_s + n] = np.sin(ang) * sign * scale
    return c


def bcast(ap, axis, n):
    a = ap.unsqueeze(axis)
    shape = list(a.shape)
    shape[axis] = n
    return a.broadcast_to(shape)


def window(t):
    return (t * 3 // 2) * LEFT + (t // (QT - 1)) * (WLAST - (3 * (QT - 1) // 2) * LEFT)


assert all(window(t) <= max(0, P * t - LEFT + 1) and min(SEQ, P * t + P + RIGHT - 1) <= window(t) + WIN <= SEQ for t in range(QT))


def decoder_kernel(nc, a, out):
    ctx = ExitStack()
    with ctx:
        place = {}

        def sb(name, shape, dt=F32):
            place[name] = nc.sbuf_base
            return ctx.enter_context(nc.sbuf_tensor(name, shape, dt))

        def over(name, shape, buffer, column):
            return nc.alloc_sbuf_tensor_at(name, shape, F32R, offset=place[buffer] + 4 * column)

        def sem(name):
            return ctx.enter_context(nc.semaphore(name))

        bank = [ctx.enter_context(nc.psum_tensor(f"bank{i}", [P, 512], F32)) for i in range(8)]
        xs_rows = nc.dram_tensor("xs_rows", (ROWS, D), F32, kind="Internal").ap()
        ys_rows = nc.dram_tensor("ys_rows", (ROWS, D), F32, kind="Internal").ap()
        q_by_row = nc.dram_tensor("q_by_row", (TOK, D), F32, kind="Internal").ap()

        X = sb("X", [P, NT, D])
        hT = sb("hT", [P, TOK])
        cst = sb("cst", [P, C_N])
        ident = cst[:, C_ID:C_ID + P]
        headmask = cst[:, C_MH:C_MH + H]
        rowmask = cst[:, C_DL:C_DL + LG]
        iota = cst[:, C_IO:C_IO + E0]
        tri = cst[:, C_TRI:C_TRI + P]
        halfmask = cst[:, C_HH:C_HH + HG]
        same_expert = cst[:, C_BLK:C_BLK + P]
        ones = sb("ones", [P, P])
        ones_bf = sb("ones_bf", [1, P], BF16)

        ln_h = sb("ln_h", [P, NT, D])
        ln_stats = sb("ln_stats", [P, NT, 6])
        ln_mv = sb("ln_mv", [P, NT, 2])
        ln_var = sb("ln_var", [P, NT])
        ln_std = sb("ln_std", [P, NT])
        ln_rstd = sb("ln_rstd", [P, NT])
        ln_new = sb("ln_new", [P, NT])
        act_warm = sb("act_warm", [P, 16])

        wqkv0 = sb("wqkv0", [P, 4 * H * DK])
        wqkv = wqkv0[:, 0:3 * H * DK].rearrange("p (i n) -> p i n", i=3)
        wo0 = wqkv0[:, 3 * H * DK:].rearrange("p (c n) -> p c n", n=D)
        x0buf = sb("x0buf", [P, 2 * P * HG])
        x0w = x0buf[:, 0:6 * D].rearrange("p (i n) -> p i n", i=6)
        krope = x0buf[:, 6 * D:6 * D + B * LK].rearrange("p (b k) -> p b k", b=B)
        krope2 = x0buf[:, 6 * D + B * LK:6 * D + 2 * B * LK].rearrange("p (b k) -> p b k", b=B)
        qrope2 = x0buf[:, 6 * D + 2 * B * LK:6 * D + 2 * B * LK + SEQ]
        x0b = sb("x0b", [P, 4])
        x0rows = sb("x0rows", [1, 2, D])
        x1w = sb("x1w", [P, 3, D])
        x1b = sb("x1b", [P, 2])
        x1rows = sb("x1rows", [1, D])
        a1w = sb("a1w", [P, 5, D])
        a1b = sb("a1b", [P, 2])
        a1bs = sb("a1bs", [P, 1])
        a1rows = sb("a1rows", [1, 3, D])
        emb = sb("emb", [HD, NPOS])
        emb_ends = sb("emb_ends", [P, 2])
        gw0 = sb("gw0", [P, E0])
        gb0 = sb("gb0", [P, E0])
        gw1 = sb("gw1", [P, E1])
        w13 = sb("w13", [P, E0 + NSH, 2, FF])
        w2 = sb("w2", [P, E0 + NSH, 2, D])
        ctxT = sb("ctxT", [P, B * LK])
        mask8 = sb("mask8", [1, B * LK], U8)
        maskrow = sb("maskrow", [1, B * LK], BF16)

        wst = sb("wst", [P, 3, P])
        hst = sb("hst", [P, SEQ])
        qT = sb("qT", [P, SEQ])
        kT = sb("kT", [P, SEQ])
        vtok = sb("vtok", [P, QT, P])
        arena = sb("arena", [P, 4, QT, SEQ])
        prob = [arena[:, i, :, :] for i in range(2)]
        probT = [arena[:, 2 + i, :, :] for i in range(2)]
        negmax = sb("negmax", [P, 2 * QT])
        den = sb("den", [P, 2 * QT])
        rden = sb("rden", [P, 2 * QT])
        featsT = sb("featsT", [P, SEQ])
        a0_p = [arena[:, 0, i, :] for i in range(QT)]
        a0_pT = [arena[:, 1 + h, :, :] for h in range(2)]
        a0_vtok = [vtok[:, :, :], arena[:, 3, 2, :].rearrange("p (a b) -> p a b", a=QT)]

        big_q = sb("big_q", [P, TOK])
        big_k = sb("big_k", [P, B, H, LK])
        big_k_flat = big_k[:, :, :, :].rearrange("p b h k -> p (b h k)")
        gathered = [t.rearrange("p (t d) -> p t d", d=D) for t in (big_q[:, :], big_k_flat[:, 0:TOK])]
        a1_k = big_k_flat[:, 0:TOK]
        a1_q2 = big_k_flat[:, TOK:2 * TOK].rearrange("p (g h) -> p g h", h=H)
        vx0 = sb("vx0", [LK, B, H, HD + 1])
        k1T = sb("k1T", [P, B * LK])
        vx1 = sb("vx1", [LK, B, D])
        qst = sb("qst", [P, P])
        mx0 = sb("mx0", [P, H])
        rd0 = sb("rd0", [P, H])
        f0 = sb("f0", [P, D])
        f0T = sb("f0T", [P, D])
        a0_qk = [over(f"a0_qk{i}", [P, 4, SEQ], buffer, 0) for i, buffer in enumerate(("big_q", "ln_h"))]
        prob0 = prob[0][:, :, :].rearrange("p a b -> p (a b)")[:, 0:H * LK]
        shifted0 = prob[1][:, :, :].rearrange("p a b -> p (a b)")[:, 0:H * LK]
        prob0T = probT[0][:, :, :]

        w13st = arena[:, 3, 0:2, :].rearrange("p e (w f) -> p e w f", w=2)
        silu = arena[:, 3, 2:4, :]
        h_parts = [over(f"f1_h{i}", [P, TOK], buffer, 0) for i, buffer in enumerate(("big_q", "big_k"))]
        w_parts = over("f1_w", [P, 2, 2, 2 * FF], "arena", 0)
        hid = arena[:, 1, :, :].rearrange("p (u h) t -> p u h t", u=2)
        arena0 = arena[:, 0, :, :].rearrange("p a b -> p (a b)")
        g_tiles = arena[:, 2, :, :].rearrange("p a (b t e) -> p (a b) t e", b=2, e=E0)
        G = sb("G", [P, NT, E1])
        g_w = sb("g_w", [P, 2, NT])
        g_row = sb("g_row", [P, 2, NT], U32)
        g_wmT = big_k_flat[:, TOK:TOK + 2 * P]
        g_edges = big_k_flat[:, TOK + 2 * P:TOK + 4 * P].rearrange("p (i n) -> p i n", i=2)
        g_ge = arena0[:, 0:CUTS * 2 * P].rearrange("p (c n) -> p c n", c=CUTS)
        xs = arena0[:, 0:4 * PITCH].rearrange("p (i t d) -> p i t d", i=2, d=D)
        ys = wqkv0[:, 0:4 * PITCH].rearrange("p (i t d) -> p i t d", i=2, d=D)
        hs = wqkv0[:, 4 * PITCH:8 * PITCH].rearrange("p (e h n) -> p e h n", e=2, h=2)
        xsT = wqkv0[:, 8 * PITCH:8 * PITCH + 2 * CAP].rearrange("p (e n) -> p e n", e=2)
        g_lg = g_tiles[:, 0, :, :]
        g_sc = g_tiles[:, 1, :, :]
        g_t1 = g_tiles[:, 2, :, :]
        g_t2 = g_tiles[:, 3, :, :]
        g_oh1 = g_tiles[:, 4, :, :]
        g_oh2 = g_tiles[:, 5, :, :]
        g_wm = g_tiles[:, 6, :, :]
        g_rt = g_tiles[:, 7, :, :]
        g_m1 = sb("g_m1", [P, NT])
        g_m2 = sb("g_m2", [P, NT])
        g_mx = sb("g_mx", [P, NT])
        g_abs = sb("g_abs", [P, 1])
        g_all = sb("g_all", [P, 1])
        g_step = sb("g_step", [P, 1])
        g_lo = sb("g_lo", [P, 1])
        g_hi = sb("g_hi", [P, 1])
        g_try = sb("g_try", [P, 2, CUTS])
        g_full = sb("g_full", [P, 2, CUTS])
        g_ge_cnt = sb("g_ge_cnt", [P, CUTS])
        g_nfull = sb("g_nfull", [P, 1])
        g_fail = sb("g_fail", [P, CUTS])
        g_low_fail = sb("g_low_fail", [P, 1])
        g_elo = sb("g_elo", [P, E0])
        g_ehi = sb("g_ehi", [P, E0])
        g_cnt = sb("g_cnt", [P, E0])
        g_left = sb("g_left", [P, E0])

        LT = P // LG
        HR = P // 2
        spare = w13[:, E1:, :, :].rearrange("p e w f -> p (e w f)")
        embpad = spare[0:HD, 0:2 * SEQ - 1]
        relT = spare[:, 2 * SEQ:2 * SEQ + SEQ + OFF]
        vst = spare[:, 4 * SEQ:4 * SEQ + QT * H * 32].rearrange("p (k h d) -> p k h d", h=H, d=32)
        ends = spare[:, 4 * SEQ + QT * H * 32:4 * SEQ + QT * H * 32 + WLAST + SEQ]
        a1_kdup = [sb("a1_kdup", [P, SEQ]), featsT]
        spare2 = w2[:, E1:, :, :].rearrange("p e h d -> p (e h d)")
        a1_qdup = spare2[:, 4 * SEQ:4 * SEQ + 2 * P].rearrange("p (g n) -> p g n", g=2)
        a1_qhi = spare2[:, 4 * SEQ + 2 * P:4 * SEQ + 4 * P].rearrange("p (g n) -> p g n", g=2)
        blocks = wqkv0[:, 0:4 * P * HG].rearrange("p (n g l h) -> p n g l h", n=4, l=LG, h=HG)
        qhigh = over("a1_qhigh", [P, 2, LT, LG, HG], "wqkv0", 0)
        qblk = [qhigh[:, i, :, :, :] for i in range(2)]
        rblk = [blocks[:, 2 + i, :, :, :] for i in range(2)]
        qlow = over("a1_qlow", [P, 2, LT, LG, HG], "x0buf", 0)
        ksplit = over("a1_ksplit", [P, 2, 2, SEQ], "w2", E1 * 2 * D)
        v1 = ln_h
        osb = sb("osb", [P, 2, P])
        rd1 = sb("rd1", [P, HG])
        feats1 = sb("feats1", [P, D])
        feats1T = sb("feats1T", [P, D])
        qtok = prob[0][:, :, :].rearrange("p a (c d) -> p (a c) d", d=D)
        ptile = [hst[:, :], qT[:, :], kT[:, :], vtok[:, :, :].rearrange("p a b -> p (a b)")]
        probTh = [arena[:, 2 - 2 * i:4 - 2 * i, :, :].rearrange("p a b (c l) -> p (a b c) l", l=P)
                  .rearrange("p (k h) l -> p k h l", k=QT) for i in range(2)]

        ld_x, ld_cst, ld_a0, ld_x0, ld_f0, ld_a1, ld_x1, ld_f1 = (
            sem(n) for n in ("ld_x", "ld_cst", "ld_a0", "ld_x0", "ld_f0", "ld_a1", "ld_x1", "ld_f1"))
        stored = sem("stored")
        setup = sem("setup")
        ln_step, ln_stat, ln_mean_ok, ln_var_ok, ln_std_ok, ln_ready, ln_tp, ln_out = (
            sem(n) for n in ("ln_step", "ln_stat", "ln_mean_ok", "ln_var_ok", "ln_std_ok", "ln_ready", "ln_tp", "ln_out"))
        pre_mm, pre_act, pre_dve, pre_pool = (sem(n) for n in ("pre_mm", "pre_act", "pre_dve", "pre_pool"))
        a0_w_staged, a0_h_staged, a0_q, a0_k, a0_v, a0_s, a0_t, a0_pv, a0_o = (
            sem("a0_" + n) for n in ("w_staged", "h_staged", "q", "k", "v", "s", "t", "pv", "o"))
        a0_ql, a0_kl, a0_qc, a0_kc, a0_vc, a0_exp, a0_max, a0_rd, a0_tc, a0_norm, a0_ftc, a0_x = (
            sem("a0_" + n) for n in ("ql", "kl", "qc", "kc", "vc", "exp", "max", "rd", "tc", "norm", "ftc", "x"))
        x0_q, x0_qr, x0_staged, x0_s, x0_t, x0_pv, x0_ft, x0_o = (
            sem("x0_" + n) for n in ("q", "qr", "staged", "s", "t", "pv", "ft", "o"))
        x0_max, x0_sub, x0_exp, x0_tcd, x0_tca, x0_rd, x0_norm, x0_ftc, x0_x = (
            sem("x0_" + n) for n in ("max", "sub", "exp", "tcd", "tca", "rd", "norm", "ftc", "x"))
        g_mm, g_chain, g_exp, g_pool, b_chain, b_count, b_total = (
            sem(n) for n in ("g_mm", "g_chain", "g_exp", "g_pool", "b_chain", "b_count", "b_total"))
        zeroed, scattered, gath_zero = (sem(n) for n in ("zeroed", "scattered", "gath_zero"))
        got = [sem(f"got{b}") for b in range(B)]
        xs_in = [sem(f"xs_in{i}") for i in range(2)]
        ys_out = [sem(f"ys_out{i}") for i in range(2)]
        r_staged, r_t, r_tc, r_h, r_silu, r_hid, r_y, r_yc, r_pad = (
            sem("r_" + n) for n in ("staged", "t", "tc", "h", "silu", "hid", "y", "yc", "pad"))
        sh_h, sh_silu, sh_hid, sh_y, sh_acc, f0_x = (
            sem(n) for n in ("sh_h", "sh_silu", "sh_hid", "sh_y", "sh_acc", "f0_x"))
        ff = {n: sem(f"f1_{n}") for n in ("high", "staged", "h", "silu", "hid", "y", "acc")}
        f1_hin, f1_hlow = (sem(n) for n in ("f1_hin", "f1_hlow"))
        a1_pre_mm, a1_pre_act, a1_pre_dve, a1_qout, a1_qin, a1_rel = (
            sem("a1_" + n) for n in ("pre_mm", "pre_act", "pre_dve", "qout", "qin", "rel"))
        a1_dup, a1_high, a1_split, a1_qb, a1_vs, a1_s, a1_t, a1_pv, a1_ot, a1_ft, a1_o = (
            sem("a1_" + n) for n in ("dup", "high", "split", "qb", "vs", "s", "t", "pv", "ot", "ft", "o"))
        a1_max, a1_exp, a1_tcd, a1_tca, a1_oc, a1_rd, a1_norm, a1_ftc, a1_x = (
            sem("a1_" + n) for n in ("max", "exp", "tcd", "tca", "oc", "rd", "norm", "ftc", "x"))
        x1_q, x1_qc, x1_s, x1_max, x1_sub, x1_exp, x1_den, x1_t, x1_tc, x1_pv, x1_x = (
            sem("x1_" + n) for n in
            ("q", "qc", "s", "max", "sub", "exp", "den", "t", "tc", "pv", "x"))

        A0, X0, F0, A1, X1, F1 = range(6)
        SCALE1 = float(1.0 / np.sqrt(HD))
        SCALEX1 = float(D) ** -0.5
        DOUBLE_AT, HIGH_AT = (2, 3, 5, 7), (5, 8, 10)
        PAIRS = B * HP
        UN = 2 * QT

        block = ctx.enter_context(nc.Block())

        @block.sync
        def _(sp):
            sp.dma_start(X[:, :, :], a["x"].rearrange("(t p) d -> p t d", p=P)).then_inc(ld_x, 16)
            sp.dma_start(ctxT[:, :], a["ctxT"]).then_inc(ld_x0, 16)
            sp.dma_start(x0w[:, :, :], a["x0w"]).then_inc(ld_x0, 16)
            sp.dma_start(x1w[:, :, :], a["x1w"]).then_inc(ld_x0, 16)
            sp.dma_start(mask8[:, :], a["mask"]).then_inc(ld_x0, 16)
            sp.dma_start(x0b[:, :], a["x0b"]).then_inc(ld_x0, 16)
            sp.dma_start(x0rows[:, :, :], a["x0rows"]).then_inc(ld_x0, 16)
            sp.dma_start(x1b[:, :], a["x1b"]).then_inc(ld_x0, 16)
            sp.dma_start(x1rows[:, :], a["x1rows"]).then_inc(ld_x0, 16)
            sp.dma_start(cst[:, :], a["cst"]).then_inc(ld_cst, 16)
            for i, n in enumerate(("wq", "wk", "wv")):
                sp.dma_start(wqkv[:, i, :], a[n]).then_inc(ld_a0, 16)
            sp.dma_start(wo0[:, :, :], a["wo"].rearrange("(c p) n -> p c n", p=P)).then_inc(ld_a0, 16)

            def a0_stage(g):
                sp.dma_start(wst[:, :, :], wqkv[:, :, ds((g % HP) * P, P)]).then_inc(a0_w_staged, 16)
                sp.dma_start(hst[:, :], hT[:, ds((g // HP) * SEQ, SEQ)]).then_inc(a0_h_staged, 16)

            def zero_rows(i):
                sp.dma_start(xs_rows.rearrange("(i p r) d -> i p r d", p=P, r=NT)[i], bcast(f0[:, :], 1, NT)).then_inc(zeroed, 16)

            def load_gate():
                sp.dma_start(gw0[:, :], a["gw0"]).then_inc(ld_f0, 16)
                sp.dma_start(gb0[:, :], a["gb0"].partition_broadcast(P)).then_inc(ld_f0, 16)

            def load_up(w):
                sp.dma_start(w13[:, 0:E0, w, :], a[("ew1", "ew3")[w]].rearrange("e d f -> d e f")).then_inc(ld_f0, 16)

            def load_shared_up():
                for w, n in enumerate(("sw1", "sw3")):
                    sp.dma_start(w13[:, E0:, w, :], a[n].rearrange("e d f -> d e f")).then_inc(ld_f0, 16)

            def load_down(hf):
                sp.dma_start(w2[:, 0:E0, hf, :], a["ew2"][:, hf * P:(hf + 1) * P, :].rearrange("e p d -> p e d")).then_inc(ld_f0, 16)
                sp.dma_start(w2[:, E0:, hf, :], a["sw2"][:, hf * P:(hf + 1) * P, :].rearrange("e p d -> p e d")).then_inc(ld_f0, 16)

            def load_a1():
                sp.dma_start(a1w[:, :, :], a["a1w"]).then_inc(ld_a1, 16)
                sp.dma_start(a1b[:, :], a["a1b"]).then_inc(ld_a1, 16)
                sp.dma_start(a1rows[:, :, :], a["a1rows"]).then_inc(ld_a1, 16)
                sp.dma_start(emb[:, :], a["emb"]).then_inc(ld_a1, 16)
                sp.dma_start(emb_ends[:, :], a["emb_ends"]).then_inc(ld_a1, 16)
                sp.dma_start(gw1[:, :], a["gw1"]).then_inc(ld_a1, 16)

            sp.wait_ge(ld_a0, 64)
            sp.wait_ge(ln_out, 4)
            sp.wait_ge(setup, 4)
            a0_stage(0)
            between = [lambda: zero_rows(0), lambda: zero_rows(1), lambda: zero_rows(2), load_gate, lambda: load_up(0),
                       lambda: load_up(1), load_shared_up, lambda: load_down(0), lambda: load_down(1), load_a1]
            for g, load in enumerate(between, 1):
                sp.wait_ge(a0_v, g)
                a0_stage(g)
                load()
            with sp.Fori(len(between) + 1, PAIRS) as g:
                sp.wait_ge(a0_v, g)
                a0_stage(g)
            xs_pairs = xs_rows.rearrange("(j i t p) d -> j i p t d", i=2, t=2 * ET, p=P)
            ys_pairs = ys_rows.rearrange("(j i t p) d -> j i p t d", i=2, t=2 * ET, p=P)

            def load_xs(j, i):
                sp.dma_start(xs[:, i, :, :], xs_pairs[ds(j, 1), i].rearrange("j p t d -> p (j t) d")).then_inc(xs_in[i], 16)

            def store_ys(j, i):
                sp.wait_ge(r_yc, j * 4 + i * 2 + 2)
                sp.dma_start(ys_pairs[ds(j, 1), i].rearrange("j p t d -> p (j t) d"), ys[:, i, :, :]).then_inc(ys_out[i], 16)

            sp.wait_ge(scattered, 16 * 2 * NT)
            for i in range(2):
                load_xs(0, i)
            with sp.Fori(0, E0 // 4 - 1) as j:
                for i in range(2):
                    sp.wait_ge(r_t, j * 4 + i * 2 + 2)
                    load_xs(j + 1, i)
                    store_ys(j, i)
            for i in range(2):
                store_ys(E0 // 4 - 1, i)
            sp.wait_ge(a1_pre_dve, 3)
            for l in range(LG):
                sp.dma_start(relT[l * HD:(l + 1) * HD, :],
                             embpad[:, LG - 1 - l:LG - 1 - l + SEQ + OFF]).then_inc(a1_rel, 16)
            sp.wait_ge(r_y, E0)
            sp.dma_start(w13[:, 0:E1, 0, :], a["f1g"].rearrange("e d f -> d e f")).then_inc(ld_f1, 16)
            sp.dma_start(w13[:, 0:E1, 1, :], a["f1u"].rearrange("e d f -> d e f")).then_inc(ld_f1, 16)
            for hf in range(2):
                sp.dma_start(w2[:, 0:E1, hf, :], a["f1d"][:, hf * P:(hf + 1) * P, :].rearrange("e p d -> p e d")).then_inc(ld_f1, 16)
            sp.wait_ge(a1_pre_act, 4)
            sp.dma_start(q_by_row.rearrange("(t p) n -> p t n", p=P), qtok).then_inc(a1_qout, 16)
            sp.wait_ge(a1_qout, 16)
            sp.dma_start(a1_q2, q_by_row.rearrange("(g l) (d h) -> (l d) g h", l=LG, h=H)).then_inc(a1_qin, 16)
            sp.wait_ge(ff["acc"], E1 * B)
            sp.dma_start(out.rearrange("(t p) d -> p t d", p=P), X[:, :, :]).then_inc(stored, 16)
            sp.wait_ge(stored, 16)

        @block.gpsimd
        def _(pool):
            pool.memset(ones[:, :], 1.0).then_inc(setup, 1)
            pool.memset(ones_bf[:, :], 1.0).then_inc(setup, 1)
            pool.memset(vx0[:, :, :, HD:HD + 1], 1.0).then_inc(setup, 1)
            pool.memset(f0[:, :], 0.0).then_inc(setup, 1)
            pool.wait_ge(ld_cst, 16)
            pool.wait_ge(pre_dve, 4)
            for b in range(B):
                pool.tensor_tensor(big_k[:, b, :, :], bcast(krope[:, b, :], 1, H), bcast(headmask, 2, LK),
                                   ALU.mult).then_inc(pre_pool, 1)
            def a0_turn(g):
                for u in range(UN):
                    pool.wait_ge(a0_rd, g * UN + u + 1)
                    pool.tensor_tensor(a0_p[u % 4], a0_p[u % 4], rden[:, u:u + 1].broadcast_to([P, SEQ]), ALU.mult).then_inc(a0_norm, 1)

            with pool.Fori(0, PAIRS) as g:
                a0_turn(g)
            pool.wait_ge(x0_qr, 4)
            pool.tensor_copy(qst[:, :], big_q[:, 0:P]).then_inc(x0_staged, 1)
            with pool.Fori(1, NT) as t:
                pool.wait_ge(x0_s, t * 3)
                pool.tensor_copy(qst[:, :], big_q[:, ds(t * P, P)]).then_inc(x0_staged, 1)

            pool.wait_ge(g_pool, 1)
            pool.partition_all_reduce(g_all[:, :], g_abs[:, :], P, RMAX).then_inc(g_pool, 1)
            pool.wait_ge(x0_x, NT)
            for c in range(2):
                pool.memset(gathered[c], 0.0).then_inc(gath_zero, 1)
            pool.memset(hs[:, :, :, CAP:], 0.0).then_inc(r_pad, 1)
            pool.wait_ge(ld_f0, 160)
            for e in range(2):
                pool.tensor_copy(w13st[:, e, :, :], w13[:, e, :, :]).then_inc(r_staged, 1)
            pool.wait_ge(g_chain, 200)
            pool.wait_ge(zeroed, 16 * (ROWS // TOK))
            for t in range(NT):
                for c in range(2):
                    pool.indirect_dma_start(xs_rows, bass.IndirectOffsetOnAxis(ap=g_row[:, c, t:t + 1], axis=0), ln_h[:, t, :], None,
                                            bounds_check=ROWS - 1, oob_is_err=False).then_inc(scattered, 16)
            with pool.Fori(1, E0 // 2) as i:
                for e in range(2):
                    pool.wait_ge(r_h, i * 4 - 2 + e * 2)
                    pool.tensor_copy(w13st[:, e, :, :], w13[:, ds(i * 2 + e, 1), :, :].rearrange("p a b c -> p (a b) c")).then_inc(r_staged, 1)
            for i in range(2):
                pool.wait_ge(ys_out[i], 16 * E0 // 4)
            pool.wait_ge(gath_zero, 2)
            for t in range(NT):
                for c in range(2):
                    pool.indirect_dma_start(gathered[c][:, t, :], None, ys_rows, bass.IndirectOffsetOnAxis(ap=g_row[:, c, t:t + 1], axis=0),
                                            bounds_check=ROWS - 1, oob_is_err=False).then_inc(got[t // QT], 16)

            pool.wait_ge(sh_acc, 2 * B)
            pool.memset(vst, 0.0).then_inc(setup, 1)
            pool.wait_ge(setup, 5)
            pool.memset(vst[:, :, :, HD:HD + 1], 1.0).then_inc(setup, 1)
            pool.wait_ge(a1_qin, 16)

            def stage_a1(it, par, first):
                for hg in range(2):
                    if not first:
                        pool.wait_ge(a1_s, it * 16 - 8 + hg * 8)
                    pool.tensor_tensor(
                        rblk[hg][:, :, :, :],
                        bcast(a1_q2[:, ds(it * LT, LT), hg * HG:(hg + 1) * HG], 2, LG),
                        bcast(bcast(rowmask, 2, HG), 1, LT), ALU.mult).then_inc(a1_qb, 1)
                    if hg == 0:
                        pool.wait_ge(a1_qb, it * 6 + 1)
                        pool.wait_ge(a1_high, it * 3 + 3)
                        for g in range(2):
                            if g:
                                pool.wait_ge(a1_split, it * 3 + 1)
                            low = ksplit[HR:, par, g, :]
                            pool.tensor_tensor(low, a1_kdup[g][HR:, :], low.bitcast(F32), ALU.subtract).then_inc(a1_split, 1)
                        pool.wait_ge(a1_split, it * 3 + 2)
                        pool.tensor_tensor(a1_qdup[:, :, :], a1_qdup[:, :, :], a1_qhi[:, :, :], ALU.subtract).then_inc(a1_split, 1)
                        pool.wait_ge(a1_split, it * 3 + 3)
                    mask = bcast(bcast(halfmask, 1, LG), 1, LT)
                    for to, q in ((qblk[hg], a1_qhi), (qlow[:, hg, :, :, :], a1_qdup)):
                        pool.tensor_tensor(to, bcast(q[:, hg, :].rearrange("p (g l) -> p g l", l=LG), 3, HG), mask, ALU.mult).then_inc(a1_qb, 1)
                if first:
                    pool.wait_ge(a1_pre_dve, 15)
                else:
                    pool.wait_ge(a1_pv, it * 2)
                pool.tensor_copy(vst[:, :, :, 0:HD],
                                 v1[:, ds((it // QT) * QT, QT), :].rearrange("p a (h d) -> p a h d", d=HD)).then_inc(a1_vs, 1)

            stage_a1(0, 0, True)
            with pool.Fori(0, NT // 2 - 1) as i:
                stage_a1(i * 2 + 1, 1, False)
                stage_a1(i * 2 + 2, 0, False)
            stage_a1(NT - 1, 1, False)

            pool.wait_ge(ld_f1, 64)
            pool.wait_ge(x1_x, NT)

            def f1_stage(i, first):
                for e in range(2):
                    if not first:
                        pool.wait_ge(ff["h"], i * 16 - 8 + e * 8)
                    w = w13[:, e, :, :] if first else w13[:, ds(i * 2 + e, 1), :, :]
                    w = w.rearrange("p b c -> p (b c)") if first else w.rearrange("p a b c -> p (a b c)")
                    st = w13st[:, e, :, :].rearrange("p w f -> p (w f)")
                    pool.tensor_copy(st, w).then_inc(ff["high"], 1)
                    pool.wait_ge(ff["high"], i * 4 + 2 * e + 1)
                    pool.tensor_tensor(w_parts[:, e, 0, :], st, ones[:, 0:1].broadcast_to((P, 2 * FF)), ALU.mult).then_inc(ff["high"], 1)
                    pool.wait_ge(ff["high"], i * 4 + 2 * e + 2)
                    pool.tensor_tensor(w_parts[:, e, 1, :], st, w_parts[:, e, 0, :].bitcast(F32), ALU.subtract).then_inc(ff["staged"], 1)

            f1_stage(0, True)
            for b in range(B):
                pool.wait_ge(f1_hin, b + 1)
                pool.tensor_tensor(h_parts[1][:, b * SEQ:(b + 1) * SEQ], hT[:, b * SEQ:(b + 1) * SEQ],
                                   h_parts[0][:, b * SEQ:(b + 1) * SEQ].bitcast(F32), ALU.subtract).then_inc(f1_hlow, 1)
            with pool.Fori(1, E1 // 2) as i:
                f1_stage(i, False)

        @block.scalar
        def _(act):
            warmed = [0]

            def warm(func):
                act.activation(act_warm[:, warmed[0]:warmed[0] + 1], ones[:, 0:1], func)
                warmed[0] += 1

            def norm_layer(layer, then):
                warm(ACT.Sqrt)
                act.wait_ge(ln_var_ok, layer + 1)
                act.activation(ln_std[:, :], ln_var[:, :], ACT.Sqrt).then_inc(ln_std_ok, 1)
                warm(then)
                for b in range(B):
                    act.wait_ge(ln_tp, layer * B + b + 1)
                    act.activation(hT[:, b * SEQ:(b + 1) * SEQ], bank[4 + b][:, :], ACT.Copy).then_inc(ln_out, 1)

            act.wait_ge(ld_x0, 128)
            act.wait_ge(pre_mm, 3)
            act.activation(k1T[:, :], bank[2][:, 0:B * LK], ACT.Identity, bias=x1b[:, 1:2]).then_inc(pre_act, 1)
            act.wait_ge(setup, 4)
            act.wait_ge(pre_mm, 4)
            act.activation(vx0[:, :, :, 0:HD], bank[3][0:LK, :].rearrange("p (b h d) -> p b h d", b=B, d=HD),
                           ACT.Copy).then_inc(pre_act, 1)
            act.wait_ge(pre_mm, 5)
            act.activation(vx1[:, :, :], bank[4][0:LK, :].rearrange("p (b d) -> p b d", b=B), ACT.Copy).then_inc(pre_act, 1)
            norm_layer(A0, ACT.Exp)

            def a0_copy_q(g, par):
                act.wait_ge(a0_q, g + 1)
                act.activation(a0_qk[par][:, 0, :], bank[6][:, :], ACT.Copy, scale=float(DK) ** -0.5).then_inc(a0_qc, 1)

            def a0_copy_k(g, par):
                act.wait_ge(a0_k, g + 1)
                act.activation(a0_qk[par][:, 2, :], bank[6][:, :], ACT.Copy).then_inc(a0_kc, 1)

            def a0_copy_v(g, par):
                act.wait_ge(a0_v, g + 1)
                act.activation(a0_vtok[par], bank[6][:, :].rearrange("p (a b) -> p a b", a=QT), ACT.Copy).then_inc(a0_vc, 1)

            def a0_copy_feats(g):
                act.wait_ge(a0_pv, g + 1)
                act.activation(featsT[:, :], bank[7][:, :], ACT.Copy).then_inc(a0_ftc, 1)

            def a0_turn(g, par, first, last):
                for u in range(UN):
                    if not first and u == 4:
                        a0_copy_feats(g - 1)
                    act.wait_ge(a0_max, g * UN + u + 1)
                    if not (first and u < 4):
                        act.wait_ge(a0_t, g * UN + u - 3)
                    act.activation(a0_p[u % 4], bank[u % 4][:, :], ACT.Exp, bias=negmax[:, u:u + 1],
                                   accum_out=den[:, u:u + 1]).then_inc(a0_exp, 1)
                    if not last:
                        if u == 2:
                            a0_copy_q(g + 1, 1 - par)
                        if u == 4:
                            a0_copy_k(g + 1, 1 - par)
                        if u == 6:
                            a0_copy_v(g + 1, 1 - par)

            a0_copy_q(0, 0)
            a0_copy_k(0, 0)
            a0_copy_v(0, 0)
            a0_turn(0, 0, True, False)
            with act.Fori(0, PAIRS // 2 - 1) as i:
                a0_turn(i * 2 + 1, 1, False, False)
                a0_turn(i * 2 + 2, 0, False, False)
            a0_turn(PAIRS - 1, 1, False, True)
            a0_copy_feats(PAIRS - 1)

            norm_layer(X0, ACT.Exp)

            def x0_copies(t):
                for c in (1, 3):
                    act.wait_ge(x0_t, t * 4 + c + 1)
                    act.activation(prob0T[0:LK, c, :], bank[4 + c % 2][0:LK, :], ACT.Copy).then_inc(x0_tca, 1)

            def x0_exps(t, first):
                act.wait_ge(x0_sub, t * 3 + 3)
                if not first:
                    act.wait_ge(x0_t, t * 4)
                act.activation(prob0, shifted0, ACT.Exp).then_inc(x0_exp, 1)

            x0_exps(0, True)
            with act.Fori(1, NT) as t:
                x0_copies(t - 1)
                x0_exps(t, False)
            x0_copies(NT - 1)

            def shared_expert(s):
                for u in range(s * 8, s * 8 + 8):
                    act.wait_ge(sh_h, u + 1)
                    if u >= 2:
                        act.wait_ge(sh_hid, u - 1)
                    act.activation(silu[:, u % 2, :], bank[2 * (u % 2)][:, :], ACT.Silu).then_inc(sh_silu, 1)

            def routed_silu(e):
                for hf in range(2):
                    act.wait_ge(r_h, e * 2 + hf + 1)
                    act.activation(silu[:, hf, 0:CAP], bank[2 * hf][:, 0:CAP], ACT.Silu).then_inc(r_silu, 1)

            def routed_y(j, k):
                act.wait_ge(r_y, j * 4 + k + 1)
                act.activation(ys[:, k // 2, (k % 2) * ET:(k % 2 + 1) * ET, :],
                               bank[6 + k % 2][:, 0:PITCH].rearrange("p (t d) -> p t d", d=D), ACT.Copy).then_inc(r_yc, 1)

            def routed_turn(j, first):
                for k in range(4):
                    routed_silu(j * 4 + k)
                    if k:
                        routed_y(j, k - 1)
                    if k in (0, 2) and not first:
                        act.wait_ge(ys_out[k // 2], j * 16)
                routed_y(j, 3)

            norm_layer(F0, ACT.Exp)
            act.wait_ge(g_exp, 1)
            act.activation(g_t2[:, :, :], g_t1[:, :, :], ACT.Exp).then_inc(g_exp, 1)
            warm(ACT.Silu)
            shared_expert(0)
            routed_turn(0, True)
            with act.Fori(1, E0 // 4) as j:
                routed_turn(j, False)
            shared_expert(1)

            norm_layer(A1, ACT.Exp)
            for b in range(B):
                act.wait_ge(a1_pre_mm, b + 1)
                act.activation(qtok[:, b * QT:(b + 1) * QT, :], bank[b][:, :].rearrange("p (t d) -> p t d", d=D),
                               ACT.Copy, scale=SCALE1).then_inc(a1_pre_act, 1)
            act.wait_ge(a1_pre_dve, 7)
            for b in range(B):
                act.wait_ge(a1_pre_mm, 8 + b + 1)
                act.activation(big_q[:, b * SEQ:(b + 1) * SEQ], bank[b][:, :], ACT.Identity,
                               bias=a1bs[:, :], scale=SCALE1).then_inc(a1_pre_act, 1)

            def a1_high_part(it, k, first):
                act.wait_ge(a1_dup, it * 4 + min(k * 2 + 2, 4))
                if k < 2:
                    act.activation(ksplit[:, ds(it % 2, 1), k, :].rearrange("p i n -> p (i n)"), a1_kdup[k][:, :], ACT.Copy).then_inc(a1_high, 1)
                else:
                    if not first:
                        act.wait_ge(a1_qb, it * 6)
                    act.activation(a1_qhi[:, :, :].bitcast(F32R), a1_qdup[:, :, :], ACT.Copy).then_inc(a1_high, 1)

            def a1_copy(it, n):
                act.wait_ge(a1_t, it * 16 + n + 1)
                hg, lg = n // 8, n % 8
                act.activation(probTh[hg][:, :, :, lg * LG:(lg + 1) * LG].rearrange("p k h l -> p k l h"),
                               bank[5][:, :].rearrange("p (k l h) -> p k l h", k=QT, l=LG), ACT.Copy).then_inc(a1_tca, 1)

            def a1_turn(it, first, last=False):
                for n in range(16):
                    if n in HIGH_AT and not last:
                        a1_high_part(it + 1, HIGH_AT.index(n), False)
                    act.wait_ge(a1_max, it * 16 + n + 1)
                    act.activation(ptile[n % 4], bank[n % 4][:, :], ACT.Exp, bias=negmax[:, n % 8:n % 8 + 1]).then_inc(a1_exp, 1)
                    if n >= 3 and n % 2 == 1:
                        a1_copy(it, n - 2)
                    elif n == 1 and not first:
                        a1_copy(it - 1, 15)

            for k in range(3):
                a1_high_part(0, k, True)
            a1_turn(0, True)
            with act.Fori(1, NT - 1) as it:
                a1_turn(it, False)
            a1_turn(NT - 1, False, last=True)
            a1_copy(NT - 1, 15)

            norm_layer(X1, ACT.Exp)
            for b in range(B):
                act.wait_ge(x1_q, b + 1)
                act.activation(big_q[:, b * SEQ:(b + 1) * SEQ], bank[b][:, :], ACT.Identity, bias=x1b[:, 0:1]).then_inc(x1_qc, 1)
            def x1_exp_of(b):
                act.wait_ge(x1_sub, b + 1)
                act.activation(prob0[:, b * QT * LK:(b + 1) * QT * LK], shifted0[:, b * QT * LK:(b + 1) * QT * LK], ACT.Exp,
                               scale=SCALEX1).then_inc(x1_exp, 1)

            x1_exp_of(0)
            for b in range(B):
                if b < B - 1:
                    x1_exp_of(b + 1)
                act.wait_ge(x1_t, b + 1)
                act.activation(prob0T[0:LK, b, :], bank[4 + b % 2][0:LK, :], ACT.Copy).then_inc(x1_tc, 1)

            norm_layer(F1, ACT.Exp)
            for b in range(B):
                act.wait_ge(ln_out, F1 * B + b + 1)
                act.activation(h_parts[0][:, b * SEQ:(b + 1) * SEQ], hT[:, b * SEQ:(b + 1) * SEQ], ACT.Copy).then_inc(f1_hin, 1)
            act.wait_ge(g_exp, 3)
            act.activation(g_t2[:, :, 0:E1], g_t1[:, :, 0:E1], ACT.Exp).then_inc(g_exp, 1)
            act.wait_ge(g_exp, 5)
            act.activation(g_m1[:, :], g_m2[:, :], ACT.Exp).then_inc(g_exp, 1)
            warm(ACT.Silu)
            with act.Fori(0, E1 // 2) as i:
                for u in range(16):
                    act.wait_ge(ff["h"], i * 16 + u + 1)
                    if u >= 2:
                        act.wait_ge(ff["hid"], i * 16 + u - 1)
                    act.activation(silu[:, u % 2, :], bank[2 * (u % 2)][:, :], ACT.Silu).then_inc(ff["silu"], 1)

        @block.tensor
        def _(pe):
            def norm_layer(layer):
                for b in range(B):
                    pe.wait_ge(ln_ready, layer * B + b + 1)
                    for t in range(QT):
                        mm = pe.transpose(bank[4 + b][:, t * P:(t + 1) * P], ln_h[:, b * QT + t, :], ident)
                    mm.then_inc(ln_tp, 1)

            pe.wait_ge(ld_cst, 16)
            pe.wait_ge(setup, 4)
            pe.wait_ge(ld_x0, 128)
            for i, w in enumerate((x0w[:, 2, :], x0w[:, 3, :], x1w[:, 1, :])):
                pe.matmul(bank[i][:, 0:B * LK], w, ctxT[:, :], start=True, stop=True).then_inc(pre_mm, 1)
            for i, (w, row) in enumerate(((x0w[:, 4, :], x0rows[:, 0, :]), (x1w[:, 2, :], x1rows[:, :]))):
                for b in range(B):
                    o = bank[3 + i][0:LK, b * D:(b + 1) * D]
                    pe.matmul(o, ctxT[:, b * LK:(b + 1) * LK], w, start=True, stop=False)
                    mm = pe.matmul(o, ones[0:1, 0:LK], row, start=False, stop=True)
                mm.then_inc(pre_mm, 1)
            pe.wait_ge(pre_act, 3)
            norm_layer(A0)
            pe.wait_ge(pre_dve, 4)

            def a0_project_q(g):
                pe.wait_ge(a0_w_staged, g * 16 + 16)
                pe.wait_ge(a0_h_staged, g * 16 + 16)
                if not (isinstance(g, int) and g == 0):
                    pe.wait_ge(a0_vc, g)
                pe.matmul(bank[6][:, :], wst[:, 0, :], hst[:, :], start=True, stop=True).then_inc(a0_q, 1)

            def a0_project_k(g):
                pe.wait_ge(a0_ql, g + 1)
                pe.matmul(bank[6][:, :], wst[:, 1, :], hst[:, :], start=True, stop=True).then_inc(a0_k, 1)

            def a0_project_v(g):
                pe.wait_ge(a0_kl, g + 1)
                for kt in range(QT):
                    mm = pe.matmul(bank[6][:, kt * P:(kt + 1) * P], hst[:, kt * P:(kt + 1) * P], wst[:, 2, :],
                                   start=True, stop=True)
                mm.then_inc(a0_v, 1)

            def a0_scores(g, u, par, first):
                if u == 0:
                    pe.wait_ge(a0_ql, g + 1)
                    pe.wait_ge(a0_kl, g + 1)
                if not (first and u < 4):
                    pe.wait_ge(a0_exp, g * UN + u - 3)
                r = (u // QT) * DK
                j = u % QT
                for i, (q, k) in enumerate(((0, 2), (0, 3), (1, 2))):
                    mm = pe.matmul(bank[j][:, :], a0_qk[par][r:r + DK, q, j * P:(j + 1) * P], a0_qk[par][r:r + DK, k, :],
                                   start=(i == 0), stop=(i == 2))
                mm.then_inc(a0_s, 1)

            def a0_turn_t(g, u, first):
                pe.wait_ge(a0_norm, g * UN + u + 1)
                if not (first and u < 2):
                    pe.wait_ge(a0_tc, g * UN + u - 1)
                for kt in range(QT):
                    mm = pe.transpose(bank[4 + u % 2][:, kt * P:(kt + 1) * P], a0_p[u % 4][:, kt * P:(kt + 1) * P], ident)
                mm.then_inc(a0_t, 1)

            def a0_values(g, par, first):
                pe.wait_ge(a0_tc, g * UN + UN)
                pe.wait_ge(a0_vc, g + 1)
                if not first:
                    pe.wait_ge(a0_x, g)
                for kt in range(QT):
                    for h in range(2):
                        mm = pe.matmul(bank[7][h * DK:(h + 1) * DK, :], a0_vtok[par][:, kt, h * DK:(h + 1) * DK],
                                       a0_pT[h][:, kt, :], start=(kt == 0), stop=(kt == QT - 1))
                mm.then_inc(a0_pv, 1)

            def a0_output(g):
                pe.wait_ge(a0_ftc, g + 1)
                for q in range(QT):
                    mm = pe.matmul(bank[7][:, q * P:(q + 1) * P], featsT[:, q * P:(q + 1) * P],
                                   wo0[:, ds(g % HP, 1), :].rearrange("p a n -> p (a n)"), start=True, stop=True)
                mm.then_inc(a0_o, 1)

            def a0_turn(g, par, first, last, second=False):
                for u in range(UN):
                    a0_scores(g, u, par, first)
                    if not first and u < 3:
                        a0_turn_t(g - 1, u + 5, False)
                    if not first and u == 3:
                        a0_values(g - 1, 1 - par, second)
                    if u >= 3:
                        a0_turn_t(g, u - 3, first)
                    if not first and u == 5:
                        a0_output(g - 1)
                    if not last:
                        if u == 2:
                            a0_project_q(g + 1)
                        if u == 4:
                            a0_project_k(g + 1)
                        if u == 6:
                            a0_project_v(g + 1)

            a0_project_q(0)
            a0_project_k(0)
            a0_project_v(0)
            a0_turn(0, 0, True, False)
            a0_turn(1, 1, False, False, second=True)
            with pe.Fori(1, PAIRS // 2 - 1) as i:
                a0_turn(i * 2, 0, False, False)
                a0_turn(i * 2 + 1, 1, False, False)
            a0_turn(PAIRS - 2, 0, False, False)
            a0_turn(PAIRS - 1, 1, False, True)
            for u in range(5, UN):
                a0_turn_t(PAIRS - 1, u, False)
            a0_values(PAIRS - 1, 1, False)
            a0_output(PAIRS - 1)

            norm_layer(X0)
            for b in range(B):
                pe.wait_ge(ln_out, X0 * B + b + 1)
                if b >= 2:
                    pe.wait_ge(x0_qr, b - 1)
                for i in range(2):
                    mm = pe.matmul(bank[2 * (b % 2) + i][:, :], x0w[:, i, :], hT[:, b * SEQ:(b + 1) * SEQ], start=True, stop=True)
                mm.then_inc(x0_q, 1)
            pe.wait_ge(x0_qr, 4)
            pe.wait_ge(pre_pool, 4)
            HS = (0, 6, 12, 16)

            def x0_scores(t, i, first):
                if i == 0:
                    pe.wait_ge(x0_staged, t + 1)
                n = HS[i + 1] - HS[i]
                if not first:
                    pe.wait_ge(x0_sub, t * 3 - 2 + i)
                o = bank[i][:, 0:n * LK]
                pe.matmul(o, qst[:, :], big_k[:, ds(t // QT, 1), HS[i]:HS[i + 1], :].rearrange("p b h k -> p (b h k)"),
                          start=True, stop=False)
                pe.matmul(o.rearrange("p (h k) -> p h k", k=LK), ones_bf[:, :],
                          bcast(maskrow[:, ds((t // QT) * LK, LK)], 1, n), start=False, stop=True).then_inc(x0_s, 1)

            def x0_turn_t(t, c):
                if c == 0:
                    pe.wait_ge(x0_exp, t + 1)
                if c == 2:
                    pe.wait_ge(x0_tcd, t * 2 + 1)
                if c == 3:
                    pe.wait_ge(x0_tca, t * 2 + 1)
                for j in range(4):
                    mm = pe.transpose(bank[4 + c % 2][0:LK, j * P:(j + 1) * P],
                                      prob0[:, (c * 4 + j) * LK:(c * 4 + j + 1) * LK], ident)
                mm.then_inc(x0_t, 1)

            def x0_values(t):
                pe.wait_ge(x0_tcd, t * 2 + 2)
                pe.wait_ge(x0_tca, t * 2 + 2)
                if not (isinstance(t, int) and t == 0):
                    pe.wait_ge(x0_norm, t)
                for h in range(H):
                    mm = pe.matmul(bank[6][:, h * (HD + 1):(h + 1) * (HD + 1)], prob0T[0:LK, h // 4, (h % 4) * P:(h % 4 + 1) * P],
                                   vx0[:, ds(t // QT, 1), h, :].rearrange("p b d -> p (b d)"), start=True, stop=True)
                mm.then_inc(x0_pv, 1)

            def x0_feats(t):
                pe.wait_ge(x0_norm, t + 1)
                pe.transpose(bank[7][:, 0:P], f0[:, :], ident).then_inc(x0_ft, 1)

            def x0_output(t):
                pe.wait_ge(x0_ftc, t + 1)
                if not (isinstance(t, int) and t == 0):
                    pe.wait_ge(x0_x, t)
                pe.matmul(bank[3][:, 0:D], f0T[:, :], x0w[:, 5, :], start=True, stop=False)
                pe.matmul(bank[3][:, 0:D], ones[0:1, :], x0rows[:, 1, :], start=False, stop=True).then_inc(x0_o, 1)

            def x0_turn(t, back, last):
                x0_turn_t(t - 1, 0)
                x0_turn_t(t - 1, 1)
                if not last:
                    x0_scores(t, 0, False)
                if back:
                    x0_feats(t - 2)
                x0_turn_t(t - 1, 2)
                if not last:
                    x0_scores(t, 1, False)
                x0_turn_t(t - 1, 3)
                if back:
                    x0_output(t - 2)
                if not last:
                    x0_scores(t, 2, False)
                x0_values(t - 1)

            for i in range(3):
                x0_scores(0, i, True)
            x0_turn(1, False, False)
            with pe.Fori(2, NT) as t:
                x0_turn(t, True, False)
            x0_turn(NT, True, True)
            x0_feats(NT - 1)
            x0_output(NT - 1)

            def router(layer, w, n):
                for b in range(B):
                    pe.wait_ge(ln_out, layer * B + b + 1)
                for t in range(NT):
                    mm = pe.matmul(bank[0][:, t * n:(t + 1) * n], hT[:, t * P:(t + 1) * P], w, start=True, stop=True)
                mm.then_inc(g_mm, 1)

            def shared_expert(s):
                def products(k):
                    pe.wait_ge(sh_hid, 2 * k + 2)
                    if k >= 2:
                        pe.wait_ge(sh_acc, k - 1)
                    for t in range(QT):
                        for hf in range(2):
                            mm = pe.matmul(bank[4 + k % 2][:, t * P:(t + 1) * P], hid[:, k % 2, hf, t * P:(t + 1) * P],
                                           w2[:, E0 + s, hf, :], start=(hf == 0), stop=(hf == 1))
                    mm.then_inc(sh_y, 1)

                for k in range(s * B, s * B + B):
                    c = k % B
                    for hf in range(2):
                        u = 2 * k + hf
                        if u >= 2:
                            pe.wait_ge(sh_hid, u - 1)
                        for w in range(2):
                            mm = pe.matmul(bank[2 * (u % 2) + w][:, :], w13[:, E0 + s, w, hf * P:(hf + 1) * P],
                                           hT[:, c * SEQ:(c + 1) * SEQ], start=True, stop=True)
                        mm.then_inc(sh_h, 1)
                    if c:
                        products(k - 1)
                products(s * B + B - 1)

            def routed_t(e, k, first):
                pe.wait_ge(xs_in[k // 2], (e // 4) * 16 + 16)
                if not (first and k < 2):
                    pe.wait_ge(r_tc, e - 1)
                for t in range(ET):
                    mm = pe.transpose(bank[4 + k % 2][:, t * P:(t + 1) * P], xs[:, k // 2, (k % 2) * ET + t, :], ident)
                mm.then_inc(r_t, 1)

            def routed_up(e, k, first):
                pe.wait_ge(r_tc, e + 1)
                pe.wait_ge(r_staged, e + 1)
                for hf in range(2):
                    if not (first and k == 0):
                        pe.wait_ge(r_hid, e * 2 + hf - 1)
                    for w in range(2):
                        mm = pe.matmul(bank[2 * hf + w][:, 0:CAP], w13st[:, k % 2, w, hf * P:(hf + 1) * P], xsT[:, k % 2, :],
                                       start=True, stop=True)
                    mm.then_inc(r_h, 1)

            def routed_down(e, k, first):
                pe.wait_ge(r_hid, e * 2 + 2)
                if not (first and k < 2):
                    pe.wait_ge(r_yc, e - 1)
                for t in range(ET):
                    for hf in range(2):
                        mm = pe.matmul(bank[6 + k % 2][:, t * P:(t + 1) * P], hs[:, k % 2, hf, t * P:(t + 1) * P],
                                       w2[:, e, hf, :] if isinstance(e, int) else w2[:, ds(e, 1), hf, :].rearrange("p a n -> p (a n)"),
                                       start=(hf == 0), stop=(hf == 1))
                mm.then_inc(r_y, 1)

            def routed_turn(j, first):
                for k in (0, 2):
                    e = j * 4 + k
                    routed_t(e, k, first)
                    routed_t(e + 1, k + 1, first)
                    if not (first and k == 0):
                        routed_down(e - 1, (k + 3) % 4, first)
                    routed_up(e, k, first)
                    routed_up(e + 1, k + 1, first)
                    routed_down(e, k, first)

            norm_layer(F0)
            pe.wait_ge(ld_f0, 160)
            router(F0, gw0[:, :], E0)
            pe.wait_ge(g_chain, 60)
            for i in range(2):
                mm = pe.transpose(bank[1][:, i * P:(i + 1) * P], g_wm[:, i * NT // 2:(i + 1) * NT // 2, :].rearrange("p t e -> p (t e)"), ident)
            mm.then_inc(g_mm, 1)
            with pe.Fori(0, BISECT) as i:
                pe.wait_ge(b_count, i + 1)
                pe.matmul(bank[2][:, 0:CUTS], same_expert, g_ge_cnt[:, :], start=True, stop=True).then_inc(b_total, 1)
            pe.wait_ge(g_chain, 80)
            for i in range(2):
                mm = pe.transpose(bank[1][:, i * P:(i + 1) * P], g_edges[:, i, :], ident)
            mm.then_inc(g_mm, 1)
            pe.wait_ge(g_chain, 100)
            pe.matmul(bank[1][:, 0:E0], ones[:, :], g_cnt[:, :], start=True, stop=True)

            def places(mask):
                m = mask.rearrange("p t e -> p (t e)")
                pe.matmul(bank[2][:, 0:NT * E0], tri, m, start=True, stop=True)
                pe.matmul(bank[3][:, 0:NT * E0], ones[:, :], m, start=True, stop=True).then_inc(g_mm, 1)

            places(g_t1[:, :, :])
            pe.wait_ge(g_chain, 150)
            places(g_sc[:, :, :])
            pe.wait_ge(g_chain, 200)
            shared_expert(0)
            pe.wait_ge(sh_acc, B)
            pe.wait_ge(r_pad, 1)
            routed_turn(0, True)
            with pe.Fori(1, E0 // 4) as j:
                routed_turn(j, False)
            routed_down(E0 - 1, 3, False)
            pe.wait_ge(r_hid, 2 * E0)
            shared_expert(1)

            norm_layer(A1)
            pe.wait_ge(ld_a1, 96)
            def a1_token_major(w, row, b, to):
                for t in range(QT):
                    o = to[:, t * D:(t + 1) * D]
                    tt = b * QT + t
                    pe.matmul(o, hT[:, tt * P:(tt + 1) * P], a1w[:, w, :], start=True, stop=False)
                    mm = pe.matmul(o, ones[0:1, :], a1rows[:, row, :], start=False, stop=True)
                mm.then_inc(a1_pre_mm, 1)

            for b in range(B):
                pe.wait_ge(ln_out, A1 * B + b + 1)
                a1_token_major(1, 0, b, bank[b])
            for b in range(B):
                pe.matmul(bank[4 + b][:, :], a1w[:, 2, :], hT[:, b * SEQ:(b + 1) * SEQ], start=True, stop=True).then_inc(a1_pre_mm, 1)
            for b in range(B):
                pe.wait_ge(a1_pre_act, b + 1)
                pe.matmul(bank[b][:, :], a1w[:, 0, :], hT[:, b * SEQ:(b + 1) * SEQ], start=True, stop=True).then_inc(a1_pre_mm, 1)
            for b in range(B):
                pe.wait_ge(a1_pre_dve, 7 + b + 1)
                a1_token_major(3, 1, b, bank[4 + b])
            pe.wait_ge(a1_pre_act, 8)
            pe.wait_ge(a1_pre_dve, 15)
            pe.wait_ge(a1_rel, 16 * LG)

            def a1_scores(it, n, first):
                hg, lg = n // 8, n % 8
                if lg == 0:
                    pe.wait_ge(a1_split, it * 3 + 3)
                    pe.wait_ge(a1_qb, it * 6 + hg * 3 + 3)
                if not (first and n < 4):
                    pe.wait_ge(a1_exp, it * 16 + n - 3)
                pe.matmul(bank[n % 4][:, :], qblk[hg][:, lg, :, :].rearrange("p l h -> p (l h)"),
                          ksplit[:, ds(it % 2, 1), hg, :].rearrange("p i n -> p (i n)"), start=True, stop=False)
                pe.matmul(bank[n % 4][:, :], qlow[:, hg, lg, :, :].rearrange("p l h -> p (l h)"),
                          ksplit[:, ds(it % 2, 1), hg, :].rearrange("p i n -> p (i n)"), start=False, stop=False)
                first_key = window(it % QT)
                pe.matmul(bank[n % 4][:, ds(first_key, WIN)], rblk[hg][:, lg, :, :].rearrange("p l h -> p (l h)"),
                          relT[:, ds((it % QT) * -P + first_key + (OFF - lg * LG), WIN)], start=False, stop=True).then_inc(a1_s, 1)

            def a1_turn_t(it, n):
                pe.wait_ge(a1_exp, it * 16 + n + 1)
                if not (isinstance(it, int) and it == 0 and n < 2):
                    pe.wait_ge((a1_tcd, a1_tca)[n % 2], it * 8 + n // 2)
                for kt in range(QT):
                    mm = pe.transpose(bank[4 + n % 2][:, kt * P:(kt + 1) * P], ptile[n % 4][:, kt * P:(kt + 1) * P], ident)
                mm.then_inc(a1_t, 1)

            def a1_values(it, hg):
                for copied in (a1_tcd, a1_tca):
                    pe.wait_ge(copied, it * 8 + hg * 4 + 4)
                pe.wait_ge(a1_vs, it + 1)
                if not (isinstance(it, int) and it == 0 and hg == 0):
                    pe.wait_ge(a1_oc, it * 2 + hg)
                for grp in range(2):
                    for kt in range(QT):
                        for j in range(4):
                            mm = pe.matmul(bank[6][32 * j:32 * j + 32, grp * P:(grp + 1) * P],
                                           vst[:, kt, hg * HG + grp * 4 + j, :], probTh[hg][:, kt, grp * 4 + j, :],
                                           start=(kt == 0), stop=(kt == QT - 1))
                mm.then_inc(a1_pv, 1)

            def a1_back(it, hg):
                pe.wait_ge(a1_oc, it * 2 + hg + 1)
                if hg == 1:
                    pe.wait_ge(a1_norm, it * 2 + 1)
                elif not (isinstance(it, int) and it == 0):
                    pe.wait_ge(a1_x, it)
                for grp in range(2):
                    mm = pe.transpose(bank[7][:, grp * P:(grp + 1) * P], osb[:, grp, :], ident)
                mm.then_inc(a1_ot, 1)

            def a1_feats(it):
                pe.wait_ge(a1_norm, it * 2 + 2)
                pe.transpose(bank[7][:, 2 * P:3 * P], feats1[:, :], ident).then_inc(a1_ft, 1)

            def a1_project(it):
                pe.wait_ge(a1_ftc, it + 1)
                pe.matmul(bank[7][:, 3 * P:], feats1T[:, :], a1w[:, 4, :], start=True, stop=False)
                pe.matmul(bank[7][:, 3 * P:], ones[0:1, :], a1rows[:, 2, :], start=False, stop=True).then_inc(a1_o, 1)

            def a1_turn(it, first):
                for n in range(16):
                    a1_scores(it, n, first)
                    if n >= 2:
                        a1_turn_t(it, n - 2)
                    elif not first:
                        a1_turn_t(it - 1, 14 + n)
                    if not first:
                        if n == 3:
                            a1_values(it - 1, 1)
                        if n == 4:
                            a1_back(it - 1, 1)
                        if n == 6:
                            a1_feats(it - 1)
                        if n == 8:
                            a1_project(it - 1)
                    if n == 11:
                        a1_values(it, 0)
                    if n == 13:
                        a1_back(it, 0)

            a1_turn(0, True)
            with pe.Fori(1, NT) as it:
                a1_turn(it, False)
            it = NT - 1
            a1_turn_t(it, 14)
            a1_turn_t(it, 15)
            a1_values(it, 1)
            a1_back(it, 1)
            a1_feats(it)
            a1_project(it)

            norm_layer(X1)
            for b in range(B):
                pe.wait_ge(ln_out, X1 * B + b + 1)
                pe.matmul(bank[b][:, :], x1w[:, 0, :], hT[:, b * SEQ:(b + 1) * SEQ], start=True, stop=True).then_inc(x1_q, 1)
            for b in range(B):
                pe.wait_ge(x1_qc, b + 1)
                for t in range(QT):
                    mm = pe.matmul(bank[b][:, t * LK:(t + 1) * LK], big_q[:, (b * QT + t) * P:(b * QT + t + 1) * P],
                                   k1T[:, b * LK:(b + 1) * LK], start=True, stop=True)
                mm.then_inc(x1_s, 1)

            def x1_turn_t(b):
                pe.wait_ge(x1_exp, b + 1)
                if b >= 2:
                    pe.wait_ge(x1_tc, b - 1)
                for t in range(QT):
                    mm = pe.transpose(bank[4 + b % 2][0:LK, t * P:(t + 1) * P], prob0[:, (b * QT + t) * LK:(b * QT + t + 1) * LK], ident)
                mm.then_inc(x1_t, 1)

            x1_turn_t(0)
            for b in range(B):
                if b < B - 1:
                    x1_turn_t(b + 1)
                pe.wait_ge(x1_tc, b + 1)
                if b >= 2:
                    pe.wait_ge(x1_x, (b - 1) * QT)
                for t in range(QT):
                    mm = pe.matmul(bank[6 + b % 2][:, t * D:(t + 1) * D], prob0T[0:LK, b, t * P:(t + 1) * P], vx1[:, b, :], start=True, stop=True)
                mm.then_inc(x1_pv, 1)

            norm_layer(F1)
            router(F1, gw1[:, :], E1)
            pe.wait_ge(g_chain, 300)
            pe.wait_ge(f1_hlow, B)

            def products(i, k):
                c = k % 4
                pe.wait_ge(ff["hid"], i * 16 + 2 * k + 2)
                if k >= 2:
                    pe.wait_ge(ff["acc"], i * 8 + k - 1)
                for t in range(QT):
                    for hf in range(2):
                        mm = pe.matmul(bank[4 + k % 2][:, t * P:(t + 1) * P], hid[:, k % 2, hf, t * P:(t + 1) * P],
                                       w2[:, ds(i * 2 + k // 4, 1), hf, :].rearrange("p a n -> p (a n)"),
                                       start=(hf == 0), stop=(hf == 1))
                mm.then_inc(ff["y"], 1)

            with pe.Fori(0, E1 // 2) as i:
                for k in range(8):
                    e, c = k // 4, k % 4
                    if c == 0:
                        pe.wait_ge(ff["staged"], i * 2 + e + 1)
                    for hf in range(2):
                        u = 2 * k + hf
                        if u >= 2:
                            pe.wait_ge(ff["hid"], i * 16 + u - 1)
                        for w in range(2):
                            for n, (wp, hp) in enumerate(((0, 0), (0, 1), (1, 0))):
                                mm = pe.matmul(bank[2 * (u % 2) + w][:, :], w_parts[:, e, wp, w * FF + hf * P:w * FF + (hf + 1) * P],
                                               h_parts[hp][:, c * SEQ:(c + 1) * SEQ], start=(n == 0), stop=(n == 2))
                        mm.then_inc(ff["h"], 1)
                    if k >= 1:
                        products(i, k - 1)
                products(i, 7)

        @block.vector
        def _(dve):
            steps = [0]

            def ln(ins):
                steps[0] += 1
                ins.then_inc(ln_step, 1)
                dve.wait_ge(ln_step, steps[0])

            def norm_stats(t):
                xt = X[:, t, :] if isinstance(t, int) else X[:, ds(t, 1), :].rearrange("p a d -> p (a d)")
                st = ln_stats[:, t, :] if isinstance(t, int) else ln_stats[:, ds(t, 1), :].rearrange("p a d -> p (a d)")
                dve.bn_stats(st, xt).then_inc(ln_stat, 1)

            def norm_layer(layer, meanwhile=None):
                dve.wait_ge(ln_stat, (layer + 1) * NT)
                for t in range(NT):
                    dve.bn_aggr(ln_mv[:, t, :], ln_stats[:, t, :]).then_inc(ln_mean_ok, 1)
                dve.wait_ge(ln_mean_ok, (layer + 1) * NT)
                dve.tensor_scalar(ln_var[:, :], ln_mv[:, :, 1], EPS, None, ALU.add).then_inc(ln_var_ok, 1)
                if meanwhile:
                    meanwhile()
                dve.wait_ge(ln_std_ok, layer + 1)
                ln(dve.reciprocal(ln_rstd[:, :], ln_std[:, :]))
                ln(dve.tensor_tensor(ln_new[:, :], ln_rstd[:, :], ln_rstd[:, :], ALU.mult))
                ln(dve.tensor_tensor(ln_new[:, :], ln_new[:, :], ln_var[:, :], ALU.mult))
                ln(dve.tensor_scalar(ln_new[:, :], ln_new[:, :], -0.5, 1.5, ALU.mult, ALU.add))
                ln(dve.tensor_tensor(ln_rstd[:, :], ln_rstd[:, :], ln_new[:, :], ALU.mult))
                for t in range(NT):
                    ins = dve.tensor_scalar(ln_h[:, t, :], X[:, t, :], ln_mv[:, t, 0:1], ln_rstd[:, t:t + 1], ALU.subtract, ALU.mult)
                    if t % QT == QT - 1:
                        ins.then_inc(ln_ready, 1)

            def context_keys():
                dve.wait_ge(ld_x0, 128)
                dve.tensor_scalar(maskrow[:, :], mask8[:, :], -1.0, 1e38, ALU.add, ALU.mult).then_inc(pre_dve, 1)
                dve.wait_ge(ld_cst, 16)
                kc = bcast(cst[:, C_CK:C_CK + LK], 1, B)
                ks = bcast(cst[:, C_SK:C_SK + LK], 1, B)
                for i, (o, tab) in enumerate(((krope, kc), (krope2, ks))):
                    dve.wait_ge(pre_mm, i + 1)
                    dve.scalar_tensor_tensor(o[:, :, :], bank[i][:, 0:B * LK].rearrange("p (b k) -> p b k", b=B),
                                             x0b[:, 2 + i:3 + i], tab, ALU.add, ALU.mult).then_inc(pre_dve, 1)
                dve.wait_ge(pre_dve, 3)
                dve.tensor_tensor(krope[:, :, :], krope[:, :, :], krope2[:, :, :], ALU.add).then_inc(pre_dve, 1)

            dve.wait_ge(ld_x, 16)
            for t in range(NT):
                norm_stats(t)
            norm_layer(A0, context_keys)

            def a0_copy(g, u):
                dve.wait_ge(a0_t, g * UN + u + 1)
                dve.tensor_copy(a0_pT[u // QT][:, :, (u % QT) * P:(u % QT + 1) * P],
                                bank[4 + u % 2][:, :].rearrange("p (a b) -> p a b", a=QT)).then_inc(a0_tc, 1)

            def a0_maximum(g, u):
                dve.wait_ge(a0_s, g * UN + u + 1)
                dve.tensor_reduce(negmax[:, u:u + 1], bank[u % 4][:, :], AX.X, ALU.max, negate=True).then_inc(a0_max, 1)

            def a0_add(g):
                dve.wait_ge(a0_o, g + 1)
                xb = X[:, ds((g // HP) * QT, QT), :]
                dve.tensor_tensor(xb, xb, bank[7][:, :].rearrange("p (a b) -> p a b", b=P), ALU.add).then_inc(a0_x, 1)

            def a0_reciprocal(g, u):
                dve.wait_ge(a0_exp, g * UN + u + 1)
                dve.reciprocal(rden[:, u:u + 1], den[:, u:u + 1]).then_inc(a0_rd, 1)

            def a0_low_q(g, par):
                dve.wait_ge(a0_qc, g + 1)
                dve.scalar_tensor_tensor(a0_qk[par][:, 1, :], bank[6][:, :], float(DK) ** -0.5, a0_qk[par][:, 0, :].bitcast(F32),
                                         ALU.mult, ALU.subtract).then_inc(a0_ql, 1)

            def a0_low_k(g, par):
                dve.wait_ge(a0_kc, g + 1)
                dve.tensor_tensor(a0_qk[par][:, 3, :], bank[6][:, :], a0_qk[par][:, 2, :].bitcast(F32), ALU.subtract).then_inc(a0_kl, 1)

            def a0_turn(g, par, first, last):
                for u in range(UN):
                    a0_maximum(g, u)
                    if u == 3 and not last:
                        a0_low_q(g + 1, 1 - par)
                    if u == 5 and not last:
                        a0_low_k(g + 1, 1 - par)
                    if u:
                        a0_reciprocal(g, u - 1)
                    elif not first:
                        a0_reciprocal(g - 1, UN - 1)
                    if u >= 3:
                        a0_copy(g, u - 3)
                    elif not first:
                        a0_copy(g - 1, u + 5)
                    if u == 6 and not first:
                        a0_add(g - 1)

            a0_low_q(0, 0)
            a0_low_k(0, 0)
            a0_turn(0, 0, True, False)
            with dve.Fori(0, PAIRS // 2 - 1) as i:
                a0_turn(i * 2 + 1, 1, False, False)
                a0_turn(i * 2 + 2, 0, False, False)
            a0_turn(PAIRS - 1, 1, False, True)
            a0_reciprocal(PAIRS - 1, UN - 1)
            for u in range(5, UN):
                a0_copy(PAIRS - 1, u)
            a0_add(PAIRS - 1)
            dve.wait_ge(a0_x, PAIRS)

            for t in range(NT):
                norm_stats(t)
            norm_layer(X0)
            dve.wait_ge(zeroed, 16 * (ROWS // TOK))
            for b in range(B):
                dve.wait_ge(x0_q, b + 1)
                qb = big_q[:, b * SEQ:(b + 1) * SEQ]
                dve.scalar_tensor_tensor(qb, bank[2 * (b % 2)][:, :], x0b[:, 0:1], cst[:, C_CQ:C_CQ + SEQ], ALU.add, ALU.mult)
                if b:
                    dve.wait_ge(x0_qr, b)
                ln(dve.scalar_tensor_tensor(qrope2[:, :], bank[2 * (b % 2) + 1][:, :], x0b[:, 1:2], cst[:, C_SQ:C_SQ + SEQ], ALU.add, ALU.mult))
                dve.tensor_tensor(qb, qb, qrope2[:, :], ALU.add).then_inc(x0_qr, 1)
            HS = (0, 6, 12, 16)

            def x0_shift(t, i, first):
                n = HS[i + 1] - HS[i]
                s = bank[i][:, 0:n * LK].rearrange("p (h k) -> p h k", k=LK)
                dve.wait_ge(x0_s, t * 3 + i + 1)
                dve.tensor_reduce(mx0[:, HS[i]:HS[i + 1]], s, AX.X, ALU.max).then_inc(x0_max, 1)
                dve.wait_ge(x0_max, t * 3 + i + 1)
                if not first and i == 0:
                    dve.wait_ge(x0_exp, t)
                dve.tensor_tensor(shifted0[:, HS[i] * LK:HS[i + 1] * LK].rearrange("p (h k) -> p h k", k=LK), s,
                                  bcast(mx0[:, HS[i]:HS[i + 1]], 2, LK), ALU.subtract).then_inc(x0_sub, 1)

            def x0_copy(t, c):
                dve.wait_ge(x0_t, t * 4 + c + 1)
                dve.tensor_copy(prob0T[0:LK, c, :], bank[4][0:LK, :]).then_inc(x0_tcd, 1)

            def x0_normalise(t):
                dve.wait_ge(x0_pv, t + 1)
                o = bank[6][:, 0:H * (HD + 1)].rearrange("p (h d) -> p h d", h=H)
                dve.reciprocal(rd0[:, :].unsqueeze(2), o[:, :, HD:HD + 1]).then_inc(x0_rd, 1)
                dve.wait_ge(x0_rd, t + 1)
                dve.tensor_tensor(f0[:, :].rearrange("p (h d) -> p h d", h=H), o[:, :, 0:HD], bcast(rd0[:, :], 2, HD),
                                  ALU.mult).then_inc(x0_norm, 1)

            def x0_feats(t):
                dve.wait_ge(x0_ft, t + 1)
                dve.tensor_copy(f0T[:, :], bank[7][:, 0:P]).then_inc(x0_ftc, 1)

            def x0_add(t):
                dve.wait_ge(x0_o, t + 1)
                xt = X[:, ds(t, 1), :].rearrange("p a d -> p (a d)")
                dve.tensor_tensor(xt, xt, bank[3][:, 0:D], ALU.add).then_inc(x0_x, 1)

            def x0_turn(t, back, last):
                x0_copy(t - 1, 0)
                if not last:
                    x0_shift(t, 0, False)
                if back:
                    x0_feats(t - 2)
                x0_copy(t - 1, 2)
                if not last:
                    x0_shift(t, 1, False)
                if back:
                    x0_add(t - 2)
                if not last:
                    x0_shift(t, 2, False)
                if back:
                    dve.wait_ge(x0_x, t - 1)
                    norm_stats(t - 2)
                x0_normalise(t - 1)

            for i in range(3):
                x0_shift(0, i, True)
            x0_turn(1, False, False)
            with dve.Fori(2, NT) as t:
                x0_turn(t, True, False)
            x0_turn(NT, True, True)
            x0_feats(NT - 1)
            x0_add(NT - 1)
            dve.wait_ge(x0_x, NT)
            norm_stats(NT - 1)

            chain = [0]

            def link(ins):
                chain[0] += 1
                ins.then_inc(g_chain, 1)
                dve.wait_ge(g_chain, chain[0])

            def upto(n):
                ins_left = n - chain[0]
                chain[0] = n
                return ins_left

            def softmax_scores(n, mm, exp_turn):
                lg, t1, t2, sc = (x[:, :, 0:n] for x in (g_lg, g_t1, g_t2, g_sc))
                dve.wait_ge(g_mm, mm)
                link(dve.tensor_copy(lg, bank[0][:, 0:NT * n].rearrange("p (t e) -> p t e", e=n)))
                link(dve.tensor_reduce(g_mx[:, :], lg, AX.X, ALU.max))
                dve.tensor_tensor(t1, lg, bcast(g_mx[:, :], 2, n), ALU.subtract).then_inc(g_exp, 1)
                dve.wait_ge(g_exp, exp_turn)
                link(dve.tensor_reduce(g_mx[:, :], t2, AX.X, ALU.add))
                link(dve.reciprocal(g_mx[:, :], g_mx[:, :]))
                link(dve.tensor_tensor(sc, t2, bcast(g_mx[:, :], 2, n), ALU.mult))

            def first_largest(n, score, best, onehot):
                t1 = g_t1[:, :, 0:n]
                io = bcast(iota[:, 0:n], 1, NT)
                link(dve.tensor_reduce(best[:, :], score, AX.X, ALU.max))
                link(dve.tensor_tensor(t1, score, bcast(best[:, :], 2, n), ALU.is_equal))
                link(dve.tensor_scalar(t1, t1, -64.0, 64.0, ALU.mult, ALU.add))
                link(dve.tensor_tensor(t1, t1, io, ALU.add))
                link(dve.tensor_reduce(g_mx[:, :], t1, AX.X, ALU.min))
                link(dve.tensor_tensor(onehot, io, bcast(g_mx[:, :], 2, n), ALU.is_equal))

            def top_two(n):
                sc, t2, oh1, oh2 = (x[:, :, 0:n] for x in (g_sc, g_t2, g_oh1, g_oh2))
                first_largest(n, sc, g_m1, oh1)
                link(dve.scalar_tensor_tensor(t2, oh1, -1e30, sc, ALU.mult, ALU.add))
                first_largest(n, t2, g_m2, oh2)

            def shared_expert(s):
                def add(k):
                    dve.wait_ge(sh_y, k + 1)
                    for t in range(QT):
                        tt = (k % B) * QT + t
                        ins = dve.scalar_tensor_tensor(X[:, tt, :], bank[4 + k % 2][:, t * P:(t + 1) * P], 1.0 / NSH, X[:, tt, :],
                                                       ALU.mult, ALU.add)
                    ins.then_inc(sh_acc, 1)

                for k in range(s * B, s * B + B):
                    for hf in range(2):
                        u = 2 * k + hf
                        dve.wait_ge(sh_silu, u + 1)
                        dve.tensor_tensor(hid[:, k % 2, hf, :], bank[2 * (u % 2) + 1][:, :], silu[:, u % 2, :],
                                          ALU.mult).then_inc(sh_hid, 1)
                    if k % B:
                        add(k - 1)
                add(s * B + B - 1)

            def routed_copy(e, k, first):
                dve.wait_ge(r_t, e + 1)
                if not (first and k < 2):
                    dve.wait_ge(r_h, e * 2 - 2)
                dve.tensor_copy(xsT[:, k % 2, :], bank[4 + k % 2][:, 0:CAP]).then_inc(r_tc, 1)

            def routed_hid(e, k, first):
                if not (first and k < 2):
                    dve.wait_ge(r_y, e - 1)
                for hf in range(2):
                    dve.wait_ge(r_silu, e * 2 + hf + 1)
                    dve.tensor_tensor(hs[:, k % 2, hf, 0:CAP], bank[2 * hf + 1][:, 0:CAP], silu[:, hf, 0:CAP], ALU.mult).then_inc(r_hid, 1)

            def routed_turn(j, first):
                for k in (0, 2):
                    e = j * 4 + k
                    routed_copy(e, k, first)
                    routed_copy(e + 1, k + 1, first)
                    routed_hid(e, k, first)
                    routed_hid(e + 1, k + 1, first)

            norm_layer(F0)
            dve.wait_ge(ld_f0, 160)
            softmax_scores(E0, 1, 2)
            link(dve.tensor_tensor(g_sc[:, :, :], g_sc[:, :, :], bcast(gb0[:, :], 1, NT), ALU.add))
            top_two(E0)
            link(dve.tensor_tensor(g_sc[:, :, :], g_oh1[:, :, :], g_oh2[:, :, :], ALU.add))
            link(dve.tensor_tensor(g_t1[:, :, :], g_lg[:, :, :], g_sc[:, :, :], ALU.mult))
            link(dve.tensor_scalar(g_t2[:, :, :], g_sc[:, :, :], -1.0, 1e30, ALU.add, ALU.mult))
            left = upto(60)
            dve.tensor_tensor(g_wm[:, :, :], g_t1[:, :, :], g_t2[:, :, :], ALU.add).then_inc(g_chain, left)
            dve.tensor_reduce(g_abs[:, :], g_lg[:, :, :], AX.XY, ALU.max, apply_absolute_value=True).then_inc(g_pool, 1)
            dve.wait_ge(g_chain, 60)
            for c, oh in enumerate((g_oh1, g_oh2)):
                link(dve.tensor_tensor(g_t1[:, :, :], g_lg[:, :, :], oh, ALU.mult))
                link(dve.tensor_reduce(g_w[:, c, :], g_t1[:, :, :], AX.X, ALU.add))
            dve.wait_ge(g_mm, 2)
            link(dve.tensor_copy(g_wmT[:, :], bank[1][:, 0:2 * P]))
            dve.wait_ge(g_pool, 2)
            link(dve.tensor_scalar(g_hi[:, :], g_all[:, :], 1.0 + 2.0 ** -10, 1e-20, ALU.mult, ALU.max))
            link(dve.tensor_scalar(g_lo[:, :], g_hi[:, :], -1.0, None, ALU.mult))
            link(dve.tensor_scalar(g_step[:, :], g_hi[:, :], 0.5, None, ALU.mult))
            link(dve.memset(g_try[:, :, :], 0.0))
            link(dve.memset(g_full[:, :, :], 1.0))

            def lower_end(par, link):
                link(dve.scalar_tensor_tensor(g_fail[:, :], g_full[:, par, :], 1e30, g_try[:, par, :], ALU.mult, ALU.add))
                link(dve.tensor_reduce(g_low_fail[:, :], g_fail[:, :], AX.X, ALU.min))
                link(dve.tensor_tensor(g_hi[:, :], g_hi[:, :], g_low_fail[:, :], ALU.min))

            with dve.Fori(0, BISECT // BSTEPS) as i:
                done = [0]

                def blink(ins):
                    done[0] += 1
                    ins.then_inc(b_chain, 1)
                    dve.wait_ge(b_chain, i * (8 * BSTEPS) + done[0])

                for k in range(BSTEPS):
                    par = k % 2
                    blink(dve.scalar_tensor_tensor(g_try[:, par, :], iota[:, 1:1 + CUTS], g_step[:, 0:1], g_lo[:, :].broadcast_to([P, CUTS]),
                                                   ALU.mult, ALU.add))
                    for c in range(CUTS):
                        ins = dve.tensor_scalar(g_ge[:, c, :], g_wmT[:, :], g_try[:, par, c:c + 1], None, ALU.is_ge)
                    blink(ins)
                    dve.tensor_reduce(g_ge_cnt[:, :], g_ge[:, :, :], AX.X, ALU.add).then_inc(b_count, 1)
                    lower_end(1 - par, blink)
                    dve.wait_ge(b_total, i * BSTEPS + k + 1)
                    blink(dve.tensor_scalar(g_full[:, par, :], bank[2][:, 0:CUTS], CAP - 0.5, None, ALU.is_ge))
                    blink(dve.tensor_reduce(g_nfull[:, :], g_full[:, par, :], AX.X, ALU.add))
                    dve.scalar_tensor_tensor(g_lo[:, :], g_nfull[:, :], g_step[:, 0:1], g_lo[:, :], ALU.mult, ALU.add)
                    blink(dve.tensor_scalar(g_step[:, :], g_step[:, :], 1.0 / (CUTS + 1), None, ALU.mult))
            lower_end(1, link)
            link(dve.tensor_copy(g_edges[:, 0, :], g_lo[:, :].broadcast_to([P, P])))
            left = upto(80)
            dve.tensor_copy(g_edges[:, 1, :], g_hi[:, :].broadcast_to([P, P])).then_inc(g_chain, left)
            dve.wait_ge(g_mm, 3)
            link(dve.tensor_copy(g_elo[:, :], bank[1][:, 0:E0]))
            link(dve.tensor_copy(g_ehi[:, :], bank[1][:, P:P + E0]))
            link(dve.tensor_tensor(g_t1[:, :, :], g_wm[:, :, :], bcast(g_elo[:, :], 1, NT), ALU.is_ge))
            link(dve.tensor_tensor(g_t2[:, :, :], g_wm[:, :, :], bcast(g_ehi[:, :], 1, NT), ALU.is_ge))
            link(dve.tensor_reduce(g_cnt[:, :], g_t2[:, :, :].rearrange("p t e -> p e t"), AX.X, ALU.add))
            left = upto(100)
            dve.tensor_tensor(g_t1[:, :, :], g_t1[:, :, :], g_t2[:, :, :], ALU.subtract).then_inc(g_chain, left)

            def places(into):
                tot = bank[3][:, 0:NT * E0].rearrange("p (t e) -> p t e", e=E0)
                link(dve.memset(into[:, 0, :], 0.0))
                for t in range(1, NT):
                    link(dve.tensor_tensor(into[:, t, :], into[:, t - 1, :], tot[:, t - 1, :], ALU.add))
                link(dve.tensor_tensor(into, into, bank[2][:, 0:NT * E0].rearrange("p (t e) -> p t e", e=E0), ALU.add))

            dve.wait_ge(g_mm, 4)
            link(dve.tensor_scalar(g_left[:, :], bank[1][:, 0:E0], -1.0, float(CAP), ALU.mult, ALU.add))
            places(g_sc)
            link(dve.tensor_tensor(g_sc[:, :, :], g_sc[:, :, :], bcast(g_left[:, :], 1, NT), ALU.is_lt))
            link(dve.tensor_tensor(g_sc[:, :, :], g_sc[:, :, :], g_t1[:, :, :], ALU.mult))
            left = upto(150)
            dve.tensor_tensor(g_sc[:, :, :], g_sc[:, :, :], g_t2[:, :, :], ALU.add).then_inc(g_chain, left)
            dve.wait_ge(g_mm, 5)
            places(g_rt)
            link(dve.scalar_tensor_tensor(g_rt[:, :, :], bcast(iota, 1, NT), float(PITCH), g_rt[:, :, :], ALU.mult, ALU.add))
            link(dve.tensor_scalar(g_t1[:, :, :], g_sc[:, :, :], -float(ROWS), float(ROWS), ALU.mult, ALU.add))
            link(dve.tensor_tensor(g_rt[:, :, :], g_rt[:, :, :], g_t1[:, :, :], ALU.add))
            for c, oh in enumerate((g_oh1, g_oh2)):
                link(dve.tensor_tensor(g_t1[:, :, :], g_rt[:, :, :], oh, ALU.mult))
                link(dve.tensor_reduce(g_m1[:, :], g_t1[:, :, :], AX.X, ALU.add))
                left = upto(200) if c else 1
                ins = dve.tensor_copy(g_row[:, c, :], g_m1[:, :])
                if c:
                    ins.then_inc(g_chain, left)
                else:
                    link(ins)
            shared_expert(0)
            routed_turn(0, True)
            with dve.Fori(1, E0 // 4) as j:
                routed_turn(j, False)
            shared_expert(1)
            dve.wait_ge(sh_acc, 2 * B)
            dve.wait_ge(ld_a1, 96)
            edge = SEQ - 1 - LEFT
            dve.tensor_copy(embpad[:, 0:edge], emb[:, 0:1].broadcast_to([HD, edge])).then_inc(a1_pre_dve, 1)
            dve.tensor_copy(embpad[:, edge:edge + NPOS], emb[:, :]).then_inc(a1_pre_dve, 1)
            dve.tensor_copy(embpad[:, edge + NPOS:], emb[:, NPOS - 1:NPOS].broadcast_to([HD, 2 * SEQ - 1 - edge - NPOS])).then_inc(a1_pre_dve, 1)
            dve.tensor_copy(ends[:, 0:WLAST], emb_ends[:, 0:1].broadcast_to([P, WLAST])).then_inc(a1_pre_dve, 1)
            dve.memset(ends[:, WLAST:SEQ], 0.0).then_inc(a1_pre_dve, 1)
            dve.tensor_copy(ends[:, SEQ:], emb_ends[:, 1:2].broadcast_to([P, WLAST])).then_inc(a1_pre_dve, 1)
            dve.tensor_scalar(a1bs[:, :], a1b[:, 0:1], SCALE1, None, ALU.mult).then_inc(a1_pre_dve, 1)
            for b in range(B):
                dve.wait_ge(got[b], 16 * 2 * QT)
                for c in range(2):
                    if c:
                        dve.wait_ge(f0_x, b * 2 + 1)
                    for t in range(b * QT, b * QT + QT):
                        ins = dve.scalar_tensor_tensor(X[:, t, :], gathered[c][:, t, :], g_w[:, c, t:t + 1], X[:, t, :], ALU.mult, ALU.add)
                    ins.then_inc(f0_x, 1)
                dve.wait_ge(f0_x, b * 2 + 2)
                for t in range(b * QT, b * QT + QT):
                    norm_stats(t)

            norm_layer(A1)
            for b in range(B):
                dve.wait_ge(a1_pre_mm, B + b + 1)
                dve.tensor_scalar(a1_k[:, b * SEQ:(b + 1) * SEQ], bank[4 + b][:, :], a1b[:, 1:2], None, ALU.add).then_inc(a1_pre_dve, 1)
            def a1_double(it, k, first):
                g = k // 2
                if not first and k == 0:
                    dve.wait_ge(a1_split, it * 3)
                    dve.wait_ge(a1_qb, it * 6)
                src = slice(g * HR, g * HR + HR)
                to = (slice(0, HR), slice(HR, P))[k % 2]
                dve.tensor_tensor(a1_kdup[g][to, :], a1_k[src, ds((it // QT) * SEQ, SEQ)],
                                  ends[src, ds(window(it % QT) * -1 + WLAST, SEQ)], ALU.add)
                dve.tensor_copy(a1_qdup[to, g, :], big_q[src, ds(it * P, P)]).then_inc(a1_dup, 1)

            dve.wait_ge(a1_pre_act, B + 1)
            dve.wait_ge(a1_pre_dve, 11)
            for k in range(4):
                a1_double(0, k, True)
            dve.wait_ge(ln_tp, (A1 + 1) * B)
            for b in range(B):
                dve.wait_ge(a1_pre_mm, 3 * B + b + 1)
                dve.tensor_copy(v1[:, b * QT:(b + 1) * QT, :], bank[4 + b][:, :].rearrange("p (t d) -> p t d", d=D)).then_inc(a1_pre_dve, 1)

            def a1_maximum(it, n):
                dve.wait_ge(a1_s, it * 16 + n + 1)
                dve.tensor_reduce(negmax[:, n % 8:n % 8 + 1], bank[n % 4][:, :], AX.X, ALU.max, negate=True).then_inc(a1_max, 1)

            def a1_copy(it, n):
                dve.wait_ge(a1_t, it * 16 + n + 1)
                hg, lg = n // 8, n % 8
                dve.tensor_copy(probTh[hg][:, :, :, lg * LG:(lg + 1) * LG].rearrange("p k h l -> p k l h"),
                                bank[4][:, :].rearrange("p (k l h) -> p k l h", k=QT, l=LG)).then_inc(a1_tcd, 1)

            def a1_out(it, hg):
                dve.wait_ge(a1_pv, it * 2 + hg + 1)
                dve.tensor_copy(osb[:, :, :], bank[6][:, 0:2 * P].rearrange("p (g l) -> p g l", g=2)).then_inc(a1_oc, 1)

            def a1_normalise(it, hg):
                dve.wait_ge(a1_ot, it * 2 + hg + 1)
                o = bank[7][:, 0:2 * P].rearrange("p (h d) -> p h d", d=32)
                dve.reciprocal(rd1[:, :].unsqueeze(2), o[:, :, HD:HD + 1]).then_inc(a1_rd, 1)
                dve.wait_ge(a1_rd, it * 2 + hg + 1)
                dve.tensor_tensor(feats1[:, hg * HG * HD:(hg + 1) * HG * HD].rearrange("p (h d) -> p h d", d=HD), o[:, :, 0:HD],
                                  bcast(rd1[:, :], 2, HD), ALU.mult).then_inc(a1_norm, 1)

            def a1_feats(it):
                dve.wait_ge(a1_ft, it + 1)
                dve.tensor_copy(feats1T[:, :], bank[7][:, 2 * P:3 * P]).then_inc(a1_ftc, 1)

            def a1_add(it):
                dve.wait_ge(a1_o, it + 1)
                xt = X[:, ds(it, 1), :].rearrange("p a d -> p (a d)")
                dve.tensor_tensor(xt, xt, bank[7][:, 3 * P:], ALU.add).then_inc(a1_x, 1)

            def a1_turn(it, first, last=False):
                for n in range(16):
                    a1_maximum(it, n)
                    if n in DOUBLE_AT and not last:
                        a1_double(it + 1, DOUBLE_AT.index(n), False)
                    if n >= 2 and n % 2 == 0:
                        a1_copy(it, n - 2)
                    elif n == 0 and not first:
                        a1_copy(it - 1, 14)
                    if not first:
                        if n == 3:
                            a1_out(it - 1, 1)
                        if n == 4:
                            a1_normalise(it - 1, 1)
                        if n == 6:
                            a1_feats(it - 1)
                        if n == 8:
                            a1_add(it - 1)
                        if n == 9:
                            dve.wait_ge(a1_x, it)
                            norm_stats(it - 1)
                    if n == 11:
                        a1_out(it, 0)
                    if n == 13:
                        a1_normalise(it, 0)

            dve.wait_ge(a1_pre_act, 2 * B)
            a1_turn(0, True)
            with dve.Fori(1, NT - 1) as it:
                a1_turn(it, False)
            it = NT - 1
            a1_turn(it, False, last=True)
            a1_copy(it, 14)
            a1_out(it, 1)
            a1_normalise(it, 1)
            a1_feats(it)
            a1_add(it)
            dve.wait_ge(a1_x, NT)
            norm_stats(it)

            norm_layer(X1)
            for b in range(B):
                s = bank[b][:, 0:QT * LK].rearrange("p (t k) -> p t k", k=LK)
                dve.wait_ge(x1_s, b + 1)
                dve.tensor_reduce(mx0[:, b * QT:(b + 1) * QT], s, AX.X, ALU.max).then_inc(x1_max, 1)
                dve.wait_ge(x1_max, b + 1)
                dve.tensor_tensor(shifted0[:, b * QT * LK:(b + 1) * QT * LK].rearrange("p (t k) -> p t k", k=LK), s,
                                  bcast(mx0[:, b * QT:(b + 1) * QT], 2, LK), ALU.subtract).then_inc(x1_sub, 1)
            for b in range(B):
                dve.wait_ge(x1_exp, b + 1)
                dve.tensor_reduce(rd0[:, b * QT:(b + 1) * QT],
                                  prob0[:, b * QT * LK:(b + 1) * QT * LK].rearrange("p (t k) -> p t k", k=LK), AX.X, ALU.add).then_inc(x1_den, 1)
                dve.wait_ge(x1_den, b * 2 + 1)
                dve.reciprocal(rd0[:, b * QT:(b + 1) * QT], rd0[:, b * QT:(b + 1) * QT]).then_inc(x1_den, 1)
                dve.wait_ge(x1_den, b * 2 + 2)
                dve.wait_ge(x1_pv, b + 1)
                for t in range(QT):
                    tt = b * QT + t
                    dve.scalar_tensor_tensor(X[:, tt, :], bank[6 + b % 2][:, t * D:(t + 1) * D], rd0[:, tt:tt + 1], X[:, tt, :],
                                             ALU.mult, ALU.add).then_inc(x1_x, 1)
            dve.wait_ge(x1_x, NT)
            for t in range(NT):
                norm_stats(t)

            norm_layer(F1)
            softmax_scores(E1, 6, 4)
            top_two(E1)
            dve.tensor_tensor(g_m2[:, :], g_m2[:, :], g_m1[:, :], ALU.subtract).then_inc(g_exp, 1)
            dve.wait_ge(g_exp, 6)
            link(dve.tensor_scalar(g_m1[:, :], g_m1[:, :], 1.0, None, ALU.add))
            link(dve.reciprocal(g_m1[:, :], g_m1[:, :]))
            link(dve.tensor_scalar(g_m2[:, :], g_m1[:, :], -1.0, 1.0, ALU.mult, ALU.add))
            link(dve.tensor_tensor(g_t1[:, :, 0:E1], g_oh1[:, :, 0:E1], bcast(g_m1[:, :], 2, E1), ALU.mult))
            link(dve.tensor_tensor(g_t2[:, :, 0:E1], g_oh2[:, :, 0:E1], bcast(g_m2[:, :], 2, E1), ALU.mult))
            left = upto(300)
            dve.tensor_tensor(G[:, :, 0:E1], g_t1[:, :, 0:E1], g_t2[:, :, 0:E1], ALU.add).then_inc(g_chain, left)
            dve.wait_ge(g_chain, 300)

            def add(i, k):
                dve.wait_ge(ff["y"], i * 8 + k + 1)
                for t in range(QT):
                    tt = (k % 4) * QT + t
                    ins = dve.scalar_tensor_tensor(
                        X[:, tt, :], bank[4 + k % 2][:, t * P:(t + 1) * P],
                        G[:, tt, ds(i * 2 + k // 4, 1)], X[:, tt, :], ALU.mult, ALU.add)
                ins.then_inc(ff["acc"], 1)

            with dve.Fori(0, E1 // 2) as i:
                for k in range(8):
                    for hf in range(2):
                        u = 2 * k + hf
                        dve.wait_ge(ff["silu"], i * 16 + u + 1)
                        dve.tensor_tensor(hid[:, k % 2, hf, :], bank[2 * (u % 2) + 1][:, :], silu[:, u % 2, :],
                                          ALU.mult).then_inc(ff["hid"], 1)
                    if k >= 1:
                        add(i, k - 1)
                add(i, 7)
            dve.wait_ge(ff["acc"], E1 * 4)


def kernel(**inputs):
    import concourse.bacc as _bacc
    from concourse.bass_utils import run_bass_kernel_spmd as _run

    i = {k: np.asarray(v) for k, v in inputs.items()}

    def swap(w):
        return w.reshape(w.shape[:-1] + (D // 2, 2))[..., ::-1].reshape(w.shape)

    def dh(w):
        return w.reshape(w.shape[:-1] + (H, HD)).swapaxes(-1, -2).reshape(w.shape)

    def heads(w):
        return w.transpose(1, 0, 2).reshape(D, H * DK)

    kv, bkv = i["L0_xattn_Wkv"], i["L0_xattn_bkv"]
    wk, wv, bk, bv = kv[:, :D], kv[:, D:], bkv[:D], bkv[D:]
    wq0, bq0 = i["L0_xattn_Wq"], i["L0_xattn_bq"]
    arrays = {
        "x": i["x"].reshape(TOK, D),
        "cst": shape_constants(),
        "wq": heads(i["L0_attn_wq"]), "wk": heads(i["L0_attn_wk"]), "wv": heads(i["L0_attn_wv"]), "wo": i["L0_attn_wo"],
        "ctxT": i["ctx_1024"].reshape(B * LK, D).T,
        "mask": i["mask_BxS2_bf1"].reshape(1, B * LK).view(np.uint8),
        "x0w": np.stack([wq0, swap(wq0), wk, swap(wk), wv, i["L0_xattn_Wo"]], 1),
        "x0b": np.stack([bq0, swap(bq0), bk, swap(bk)], 1),
        "x0rows": np.stack([bv, i["L0_xattn_bo"]], 0)[None],
        "x1w": np.stack([i["L1_xattn_Wq"], i["L1_xattn_Wk"], i["L1_xattn_Wv"]], 1),
        "x1b": np.stack([i["L1_xattn_bq"], i["L1_xattn_bk"]], 1),
        "x1rows": i["L1_xattn_bv"][None],
        "gw0": i["L0_ffn_gate_w"], "gb0": i["L0_ffn_gate_b"],
        "ew1": i["L0_ffn_ew1"], "ew3": i["L0_ffn_ew3"], "ew2": i["L0_ffn_ew2"],
        "sw1": i["L0_ffn_sw1"], "sw3": i["L0_ffn_sw3"], "sw2": i["L0_ffn_sw2"],
        "a1w": np.stack([i["L1_attn_Wq"].T, dh(i["L1_attn_Wq"].T), i["L1_attn_Wk"].T, i["L1_attn_Wv"].T, i["L1_attn_Wo"].T], 1),
        "a1b": np.stack([i["L1_attn_bq"], i["L1_attn_bk"]], 1),
        "a1rows": np.stack([dh(i["L1_attn_bq"]), i["L1_attn_bv"], i["L1_attn_bo"]], 0)[None],
        "emb": i["L1_attn_dist_emb"].T,
        "emb_ends": np.tile(i["L1_attn_dist_emb"][[0, -1]].T, (H, 1)),
        "gw1": i["L1_ffn_kernel_router_DE"],
        "f1g": i["L1_ffn_kernel_gating_EDF"], "f1u": i["L1_ffn_kernel_up_EDF"], "f1d": i["L1_ffn_kernel_down_EFD"],
    }
    nc = _bacc.Bacc("TRN2", target_bir_lowering=False, num_devices=1)
    feed, aps = {}, {}
    for name, v in arrays.items():
        v = np.ascontiguousarray(v)
        feed[f"in_{name}"] = v
        aps[name] = nc.dram_tensor(f"in_{name}", v.shape, mybir.dt.from_np(v.dtype), kind="ExternalInput").ap()
    out = nc.dram_tensor("out", (TOK, D), F32, kind="ExternalOutput").ap()
    decoder_kernel(nc, aps, out)
    r = _run(nc, [feed], core_ids=[0])
    return r.results[0]["out"].reshape(B, SEQ, D)
```
